# Optimizing a Trainium2 kernel written in Bass

```python
import numpy as np
import jax
import jax.numpy as jnp

def _softmax(x, axis=-1):
    return jax.nn.softmax(x, axis=axis)

def _gelu(x):
    return jax.nn.gelu(x, approximate=True)

def _silu(x):
    return jax.nn.silu(x)

def _sigmoid(x):
    return jax.nn.sigmoid(x)

def _layernorm(x, axis=-1, eps=1e-05):
    m = jnp.mean(x, axis=axis, keepdims=True)
    v = jnp.var(x, axis=axis, keepdims=True)
    return (x - m) / jnp.sqrt(v + eps)

def _scatter_add(tgt, idx, src, axis=0):
    return tgt.at[idx].add(src)

def _segment_sum(src, seg, n):
    return jax.ops.segment_sum(src, seg, n)
kernel_name = 'mk_xattn_ffn_d2_seqx_r4_55fe3f'

def setup_inputs(seed: int=0):
    np.random.seed(seed)
    _w = jnp.asarray

    def _rec_inputs():
        import jax
        import jax.numpy as jnp
        _rk = jax.random.key(seed)
        x = -0.0002928 + 1 * jax.random.normal(jax.random.fold_in(_rk, 1), (4, 1024, 256), jnp.float32)
        _lenS = 1024 - jax.random.randint(jax.random.fold_in(_rk, 7), (4,), 0, max(1, 1024 // 4) + 1, jnp.int32)
        _lenS2 = 64 - jax.random.randint(jax.random.fold_in(_rk, 8), (4,), 0, max(1, 64 // 4) + 1, jnp.int32)
        _ctx_1024P = jax.random.normal(jax.random.fold_in(_rk, 11), (4, 16, 256), jnp.float32)
        _ctx_1024c = jax.random.dirichlet(jax.random.fold_in(_rk, 511), 0.3 * jnp.ones((16,), jnp.float32), (4, 64))
        _ctx_1024t = jnp.einsum('bsk,bkd->bsd', _ctx_1024c, _ctx_1024P)
        _ctx_1024t = _ctx_1024t * jax.lax.rsqrt(jnp.mean(jnp.square(_ctx_1024t)) + 1e-12) * 0.953939
        ctx_1024 = -1.39393e-06 + 0.999914 * (_ctx_1024t + 0.3 * jax.random.normal(jax.random.fold_in(_rk, 611), (4, 64, 256), jnp.float32))
        _validS = jnp.arange(1024)[None, :] < _lenS[:, None]
        _validS2 = jnp.arange(64)[None, :] < _lenS2[:, None]
        _causal = jnp.tril(jnp.ones((1024, 1024), dtype=bool))
        mask_Bx1xSxS2_ik0 = jnp.where(jnp.broadcast_to(_validS2[:, None, None, :], (4, 1, 1024, 64)), 0, 1).astype(jnp.int32)
        return (x, ctx_1024, mask_Bx1xSxS2_ik0)
    x, ctx_1024, mask_Bx1xSxS2_ik0 = _rec_inputs()

    def _L0_xattn_setup():
        import jax, jax.numpy as jnp
        import numpy as np
        import math
        B, S, D, H = (2, 512, 256, 16)
        DK = D // H
        key = jax.random.key(seed)
        ks = jax.random.split(key, 12)
        s = 1.0 / math.sqrt(D)
        inp = {'q': jax.random.normal(ks[0], (B, S, D), jnp.float32), 'k': jax.random.normal(ks[1], (B, S, D), jnp.float32), 'v': jax.random.normal(ks[2], (B, S, D), jnp.float32), 'mask': jnp.broadcast_to(jnp.tril(jnp.ones((S, S), jnp.int32))[None, None], (B, 1, S, S)), 'Wq': jax.random.normal(ks[3], (D, D), jnp.float32) * s, 'bq': jnp.zeros((D,), jnp.float32), 'Wk': jax.random.normal(ks[4], (D, D), jnp.float32) * s, 'bk': jnp.zeros((D,), jnp.float32), 'Wv': jax.random.normal(ks[5], (D, D), jnp.float32) * s, 'bv': jnp.zeros((D,), jnp.float32), 'Wo': jax.random.normal(ks[6], (D, D), jnp.float32) * s, 'bo': jnp.zeros((D,), jnp.float32)}
        return inp
    _L0_xattn_all = _L0_xattn_setup()
    _L0_xattn_in = {k: v for k, v in _L0_xattn_all.items() if k in ('Wq', 'bq', 'Wk', 'bk', 'Wv', 'bv', 'Wo', 'bo')}
    del _L0_xattn_all

    def _L0_ffn_setup():
        import jax, jax.numpy as jnp
        import numpy as np
        B, S, D, H, F, E = (2, 256, 256, 16, 512, 8)
        HD = D // H

        def _ln(x, g, b, eps=1e-05):
            m = x.mean(-1, keepdims=True)
            v = ((x - m) ** 2).mean(-1, keepdims=True)
            return (x - m) / jnp.sqrt(v + eps) * g + b
        key = jax.random.key(seed)
        ks = jax.random.split(key, 12)
        rn = lambda k, shp, s=0.02: jax.random.normal(k, shp, jnp.float32) * s
        return {'src': jax.random.normal(ks[0], (B, S, D), jnp.float32), 'q_w': rn(ks[1], (D, D)), 'k_w': rn(ks[2], (D, D)), 'v_w': rn(ks[3], (D, D)), 'out_w': rn(ks[4], (D, D)), 'gate_w': rn(ks[5], (D, D)), 'gate_b': rn(ks[6], (D,)), 'scale_w': rn(ks[7], (H, HD)), 'n1_g': jnp.ones((D,), jnp.float32), 'n1_b': jnp.zeros((D,), jnp.float32), 'n2_g': jnp.ones((D,), jnp.float32), 'n2_b': jnp.zeros((D,), jnp.float32), 'moe_gate_w': rn(ks[8], (D, E)), 'moe_gate_b': jnp.zeros((E,), jnp.float32), 'w1': rn(ks[9], (E, D, F)), 'b1': jnp.zeros((E, F), jnp.float32), 'ln_g': jnp.ones((E, F), jnp.float32), 'ln_b': jnp.zeros((E, F), jnp.float32), 'w2': rn(ks[10], (E, F, D)), 'b2': jnp.zeros((E, D), jnp.float32), 'res_scale': jnp.ones((E,), jnp.float32)}
    _L0_ffn_all = _L0_ffn_setup()
    _L0_ffn_in = {k: v for k, v in _L0_ffn_all.items() if k in ('q_w', 'k_w', 'v_w', 'out_w', 'gate_w', 'gate_b', 'scale_w', 'n1_g', 'n1_b', 'n2_g', 'n2_b', 'moe_gate_w', 'moe_gate_b', 'w1', 'b1', 'ln_g', 'ln_b', 'w2', 'b2', 'res_scale')}
    del _L0_ffn_all

    def _L1_xattn_setup():
        import jax, jax.numpy as jnp
        import numpy as np
        EMBED_DIM = 256
        NUM_HEADS = 16
        DEPTH = EMBED_DIM // NUM_HEADS

        def _split_heads(x):
            B, S, _ = x.shape
            return x.reshape(B, S, NUM_HEADS, DEPTH).transpose(0, 2, 1, 3)
        key = jax.random.key(seed)
        ks = jax.random.split(key, 11)
        B, S, D = (2, 512, EMBED_DIM)
        scale = 1.0 / np.sqrt(D)
        inp = {'q': jax.random.normal(ks[0], (B, S, D), jnp.float32), 'k': jax.random.normal(ks[1], (B, S, D), jnp.float32), 'v': jax.random.normal(ks[2], (B, S, D), jnp.float32), 'Wq': jax.random.normal(ks[3], (D, D), jnp.float32) * scale, 'bq': jnp.zeros((D,), jnp.float32), 'Wk': jax.random.normal(ks[4], (D, D), jnp.float32) * scale, 'bk': jnp.zeros((D,), jnp.float32), 'Wv': jax.random.normal(ks[5], (D, D), jnp.float32) * scale, 'bv': jnp.zeros((D,), jnp.float32), 'Wo': jax.random.normal(ks[6], (D, D), jnp.float32) * scale, 'bo': jnp.zeros((D,), jnp.float32)}
        return inp
    _L1_xattn_all = _L1_xattn_setup()
    _L1_xattn_in = {k: v for k, v in _L1_xattn_all.items() if k in ('Wq', 'bq', 'Wk', 'bk', 'Wv', 'bv', 'Wo', 'bo')}
    del _L1_xattn_all

    def _L1_ffn_setup():
        import jax, jax.numpy as jnp
        import numpy as np
        B, T, C, H, E = (4, 512, 256, 512, 8)
        CAPACITY_FACTOR = 1.0
        key = jax.random.key(seed)
        ks = jax.random.split(key, 5)
        scale = 0.02
        return {'x': jax.random.normal(ks[0], (B, T, C), dtype=jnp.float32), 'Wg': jax.random.normal(ks[1], (E, C), dtype=jnp.float32) * scale, 'W1': jax.random.normal(ks[2], (E, H, C), dtype=jnp.float32) * scale, 'W2': jax.random.normal(ks[3], (E, C, H), dtype=jnp.float32) * scale, 'W3': jax.random.normal(ks[4], (E, H, C), dtype=jnp.float32) * scale}
    _L1_ffn_all = _L1_ffn_setup()
    _L1_ffn_in = {k: v for k, v in _L1_ffn_all.items() if k in ('Wg', 'W1', 'W2', 'W3')}
    del _L1_ffn_all
    return {'x': x, 'ctx_1024': ctx_1024, 'mask_Bx1xSxS2_ik0': mask_Bx1xSxS2_ik0, 'L0_xattn_Wq': _L0_xattn_in['Wq'], 'L0_xattn_bq': _L0_xattn_in['bq'], 'L0_xattn_Wk': _L0_xattn_in['Wk'], 'L0_xattn_bk': _L0_xattn_in['bk'], 'L0_xattn_Wv': _L0_xattn_in['Wv'], 'L0_xattn_bv': _L0_xattn_in['bv'], 'L0_xattn_Wo': _L0_xattn_in['Wo'], 'L0_xattn_bo': _L0_xattn_in['bo'], 'L0_ffn_q_w': _L0_ffn_in['q_w'], 'L0_ffn_k_w': _L0_ffn_in['k_w'], 'L0_ffn_v_w': _L0_ffn_in['v_w'], 'L0_ffn_out_w': _L0_ffn_in['out_w'], 'L0_ffn_gate_w': _L0_ffn_in['gate_w'], 'L0_ffn_gate_b': _L0_ffn_in['gate_b'], 'L0_ffn_scale_w': _L0_ffn_in['scale_w'], 'L0_ffn_n1_g': _L0_ffn_in['n1_g'], 'L0_ffn_n1_b': _L0_ffn_in['n1_b'], 'L0_ffn_n2_g': _L0_ffn_in['n2_g'], 'L0_ffn_n2_b': _L0_ffn_in['n2_b'], 'L0_ffn_moe_gate_w': _L0_ffn_in['moe_gate_w'], 'L0_ffn_moe_gate_b': _L0_ffn_in['moe_gate_b'], 'L0_ffn_w1': _L0_ffn_in['w1'], 'L0_ffn_b1': _L0_ffn_in['b1'], 'L0_ffn_ln_g': _L0_ffn_in['ln_g'], 'L0_ffn_ln_b': _L0_ffn_in['ln_b'], 'L0_ffn_w2': _L0_ffn_in['w2'], 'L0_ffn_b2': _L0_ffn_in['b2'], 'L0_ffn_res_scale': _L0_ffn_in['res_scale'], 'L1_xattn_Wq': _L1_xattn_in['Wq'], 'L1_xattn_bq': _L1_xattn_in['bq'], 'L1_xattn_Wk': _L1_xattn_in['Wk'], 'L1_xattn_bk': _L1_xattn_in['bk'], 'L1_xattn_Wv': _L1_xattn_in['Wv'], 'L1_xattn_bv': _L1_xattn_in['bv'], 'L1_xattn_Wo': _L1_xattn_in['Wo'], 'L1_xattn_bo': _L1_xattn_in['bo'], 'L1_ffn_Wg': _L1_ffn_in['Wg'], 'L1_ffn_W1': _L1_ffn_in['W1'], 'L1_ffn_W2': _L1_ffn_in['W2'], 'L1_ffn_W3': _L1_ffn_in['W3']}

def reference(x, ctx_1024, mask_Bx1xSxS2_ik0, L0_xattn_Wq, L0_xattn_bq, L0_xattn_Wk, L0_xattn_bk, L0_xattn_Wv, L0_xattn_bv, L0_xattn_Wo, L0_xattn_bo, L0_ffn_q_w, L0_ffn_k_w, L0_ffn_v_w, L0_ffn_out_w, L0_ffn_gate_w, L0_ffn_gate_b, L0_ffn_scale_w, L0_ffn_n1_g, L0_ffn_n1_b, L0_ffn_n2_g, L0_ffn_n2_b, L0_ffn_moe_gate_w, L0_ffn_moe_gate_b, L0_ffn_w1, L0_ffn_b1, L0_ffn_ln_g, L0_ffn_ln_b, L0_ffn_w2, L0_ffn_b2, L0_ffn_res_scale, L1_xattn_Wq, L1_xattn_bq, L1_xattn_Wk, L1_xattn_bk, L1_xattn_Wv, L1_xattn_bv, L1_xattn_Wo, L1_xattn_bo, L1_ffn_Wg, L1_ffn_W1, L1_ffn_W2, L1_ffn_W3):
    import jax
    import jax.numpy as jnp

    def _L0_xattn_ref(q, k, v, mask, Wq, bq, Wk, bk, Wv, bv, Wo, bo):
        import jax, jax.numpy as jnp
        import numpy as np
        import math
        B, S, D, H = (2, 512, 256, 16)
        DK = D // H
        b = q.shape[0]

        def heads(x, W, bias):
            y = x @ W.T + bias
            return y.reshape(b, -1, H, DK).transpose(0, 2, 1, 3)
        qh = heads(q, Wq, bq)
        kh = heads(k, Wk, bk)
        vh = heads(v, Wv, bv)
        scores = jnp.einsum('bhqd,bhkd->bhqk', qh, kh) / math.sqrt(DK)
        scores = jnp.where(mask == 0, jnp.float32(-1000000000.0), scores)
        weights = jax.nn.softmax(scores, axis=-1)
        out = jnp.einsum('bhqk,bhkd->bhqd', weights, vh)
        out = out.transpose(0, 2, 1, 3).reshape(b, -1, H * DK)
        return out @ Wo.T + bo

    def _L0_ffn_ref(src, q_w, k_w, v_w, out_w, gate_w, gate_b, scale_w, n1_g, n1_b, n2_g, n2_b, moe_gate_w, moe_gate_b, w1, b1, ln_g, ln_b, w2, b2, res_scale):
        import jax, jax.numpy as jnp
        import numpy as np
        B, S, D, H, F, E = (2, 256, 256, 16, 512, 8)
        HD = D // H

        def _ln(x, g, b, eps=1e-05):
            m = x.mean(-1, keepdims=True)
            v = ((x - m) ** 2).mean(-1, keepdims=True)
            return (x - m) / jnp.sqrt(v + eps) * g + b
        b, s, d = src.shape
        h = scale_w.shape[0]
        hd = d // h
        q = (src @ q_w).reshape(b, s, h, hd).transpose(0, 2, 1, 3)
        k = (src @ k_w).reshape(b, s, h, hd).transpose(0, 2, 1, 3)
        v = (src @ v_w).reshape(b, s, h, hd).transpose(0, 2, 1, 3)
        scores = jnp.einsum('bhqd,bhkd->bhqk', q, k) / np.float32(np.sqrt(hd))
        scale = jax.nn.sigmoid(jnp.einsum('bhsd,hd->bhs', q, scale_w)) * 2.0
        scores = scores * scale[..., None]
        aw = jax.nn.softmax(scores, axis=-1)
        out = jnp.einsum('bhqk,bhkd->bhqd', aw, v).transpose(0, 2, 1, 3).reshape(b, s, d)
        gate = jax.nn.sigmoid(out @ gate_w + gate_b)
        attn = out * gate @ out_w
        x = _ln(src + attn, n1_g, n1_b)
        xr = x.reshape(-1, d)
        n = xr.shape[0]
        logits = xr @ moe_gate_w + moe_gate_b
        top_v, top_i = jax.lax.top_k(logits, 2)
        wts = jax.nn.softmax(top_v, axis=-1)
        chosen = jnp.max(top_i, axis=-1)

        def expert(W1, B1, G, Bt, W2, B2, rsc):
            hh = xr @ W1 + B1
            hh = jax.nn.gelu(_ln(hh, G, Bt), approximate=False)
            return (hh @ W2 + B2) * rsc + xr
        outs = jax.vmap(expert)(w1, b1, ln_g, ln_b, w2, b2, res_scale)
        sel = jnp.take_along_axis(outs.transpose(1, 0, 2), chosen[:, None, None], axis=1)[:, 0]
        moe = sel * jnp.sum(wts, axis=-1, keepdims=True)
        return _ln(x + moe.reshape(b, s, d), n2_g, n2_b)

    def _L1_xattn_ref(q, k, v, Wq, bq, Wk, bk, Wv, bv, Wo, bo):
        import jax, jax.numpy as jnp
        import numpy as np
        EMBED_DIM = 256
        NUM_HEADS = 16
        DEPTH = EMBED_DIM // NUM_HEADS

        def _split_heads(x):
            B, S, _ = x.shape
            return x.reshape(B, S, NUM_HEADS, DEPTH).transpose(0, 2, 1, 3)
        query = _split_heads(q @ Wq + bq)
        key_ = _split_heads(k @ Wk + bk)
        value = _split_heads(v @ Wv + bv)
        logits = jnp.einsum('bhqd,bhkd->bhqk', query, key_) / jnp.sqrt(jnp.asarray(DEPTH, query.dtype))
        attn = jax.nn.softmax(logits, axis=-1)
        out = jnp.einsum('bhqk,bhkd->bhqd', attn, value)
        B, H, S, d = out.shape
        concat = out.transpose(0, 2, 1, 3).reshape(B, S, H * d)
        return concat @ Wo + bo

    def _L1_ffn_ref(x, Wg, W1, W2, W3):
        import jax, jax.numpy as jnp
        import numpy as np
        B, T, C, H, E = (4, 512, 256, 512, 8)
        CAPACITY_FACTOR = 1.0
        b, t, c = x.shape
        e = Wg.shape[0]
        n = b * t
        capacity = max(1, int(CAPACITY_FACTOR * n / e))
        x_flat = x.reshape(n, c)
        scores = (x_flat @ Wg.T).T
        top_vals, token_idx = jax.lax.top_k(scores, capacity)
        token_w = jax.nn.softmax(top_vals, axis=-1)
        xg = x_flat[token_idx]
        h = jax.nn.silu(jnp.einsum('eic,ehc->eih', xg, W1)) * jnp.einsum('eic,ehc->eih', xg, W3)
        y = jnp.einsum('eih,ech->eic', h, W2) * token_w[..., None]
        out = jnp.zeros_like(x_flat).at[token_idx.reshape(-1)].add(y.reshape(-1, c))
        return out.reshape(b, t, c)
    x = x + _L0_xattn_ref(_layernorm(x, axis=-1), ctx_1024, ctx_1024, mask_Bx1xSxS2_ik0, L0_xattn_Wq, L0_xattn_bq, L0_xattn_Wk, L0_xattn_bk, L0_xattn_Wv, L0_xattn_bv, L0_xattn_Wo, L0_xattn_bo)
    x = x + _L0_ffn_ref(_layernorm(x, axis=-1), L0_ffn_q_w, L0_ffn_k_w, L0_ffn_v_w, L0_ffn_out_w, L0_ffn_gate_w, L0_ffn_gate_b, L0_ffn_scale_w, L0_ffn_n1_g, L0_ffn_n1_b, L0_ffn_n2_g, L0_ffn_n2_b, L0_ffn_moe_gate_w, L0_ffn_moe_gate_b, L0_ffn_w1, L0_ffn_b1, L0_ffn_ln_g, L0_ffn_ln_b, L0_ffn_w2, L0_ffn_b2, L0_ffn_res_scale)
    x = x + _L1_xattn_ref(_layernorm(x, axis=-1), ctx_1024, ctx_1024, L1_xattn_Wq, L1_xattn_bq, L1_xattn_Wk, L1_xattn_bk, L1_xattn_Wv, L1_xattn_bv, L1_xattn_Wo, L1_xattn_bo)
    x = x + _L1_ffn_ref(_layernorm(x, axis=-1), L1_ffn_Wg, L1_ffn_W1, L1_ffn_W2, L1_ffn_W3)
    return x

_drawn_inputs = setup_inputs


def setup_inputs(seed=0):
    import zlib

    import numpy as np

    out = dict(_drawn_inputs(seed))
    spreads = {'L0_xattn_bq': (0.0, 0.1),
     'L0_xattn_bk': (0.0, 0.8),
     'L0_xattn_bv': (0.0, 0.1),
     'L0_xattn_bo': (0.0, 0.1),
     'L0_ffn_n1_g': (1.0, 0.2),
     'L0_ffn_n1_b': (0.0, 0.1),
     'L0_ffn_n2_g': (1.0, 0.2),
     'L0_ffn_n2_b': (0.0, 0.1),
     'L0_ffn_moe_gate_b': (0.0, 0.1),
     'L0_ffn_b1': (0.0, 0.368),
     'L0_ffn_ln_g': (1.0, 0.6),
     'L0_ffn_ln_b': (0.0, 0.8),
     'L0_ffn_b2': (0.0, 0.326),
     'L0_ffn_res_scale': (1.0, 0.6),
     'L1_xattn_bq': (0.0, 0.8),
     'L1_xattn_bk': (0.0, 0.8),
     'L1_xattn_bv': (0.0, 0.1),
     'L1_xattn_bo': (0.0, 0.1)}
    factors = {'L0_ffn_q_w': 8.0,
     'L0_ffn_k_w': 8.0,
     'L0_ffn_v_w': 3.145,
     'L0_ffn_out_w': 2.943,
     'L0_ffn_gate_w': 8.0,
     'L0_ffn_gate_b': 8.0,
     'L0_ffn_scale_w': 8.0,
     'L1_ffn_Wg': 8.0,
     'L1_ffn_W1': 8.0,
     'L1_ffn_W2': 8.0,
     'L1_ffn_W3': 8.0}
    for name, (base, spread) in spreads.items():
        noise = np.random.default_rng([zlib.crc32(name.encode()), seed]).standard_normal(out[name].shape)
        drawn = base * np.exp(spread * noise) if base else spread * noise
        out[name] = jnp.asarray(drawn.astype(out[name].dtype))
    for name, factor in factors.items():
        out[name] = (out[name] * factor).astype(out[name].dtype)
    return out
```

```python
import concourse.bass as bass
from concourse import mybir
from contextlib import ExitStack

fp32 = mybir.dt.float32
bf16 = mybir.dt.bfloat16
i32 = mybir.dt.int32
u32 = mybir.dt.uint32
ALU = mybir.AluOpType
ACT = mybir.ActivationFunctionType
X = mybir.AxisListType.X
ds = bass.ds

P = 128
B, S, D = 4, 1024, 256
SC = 64
H = 16
DK = D // H
HALVES = D // P
TOKENS = B * S
TILES = TOKENS // P
CT = 4
CW = CT * P
CHUNKS = TOKENS // CW
HH = H // HALVES
EPS = 1e-5
NEG = -4.0e9
SCALE = 1.0 / DK ** 0.5


class Kit:

    def __init__(self, nc, ctx, prefix):
        self.nc, self.ctx, self.prefix = nc, ctx, prefix
        self.numbers = []
        ctx.callback(self.clear_semaphores)

    def clear_semaphores(self):
        if not self.numbers:
            return
        with self.nc.Block() as block:
            @block.gpsimd
            def _(pool):
                first = 0
                for i, number in enumerate(self.numbers):
                    if i + 1 == len(self.numbers) or self.numbers[i + 1] != number + 1:
                        pool.sem_clear(range(self.numbers[first], number + 1))
                        first = i + 1

    def sb(self, name, shape, dt=fp32):
        return self.ctx.enter_context(self.nc.sbuf_tensor(self.prefix + name, shape, dt))

    def ps(self, name, shape):
        return self.ctx.enter_context(self.nc.psum_tensor(self.prefix + name, shape, fp32))

    def sem(self, name):
        semaphore = self.ctx.enter_context(self.nc.semaphore(self.prefix + name))
        self.numbers.append(semaphore.num)
        return semaphore


def bc(ap, axis, shape):
    return ap.unsqueeze(axis).broadcast_to(shape)


def later(k, first):
    return not isinstance(k, int) or k >= first


def passed(eng, semaphore, value, turnstile):
    eng.wait_ge(semaphore, value)
    eng.sem_inc(turnstile, 1)


def cross_attention(nc, x_sb, ident, eps_pow, w, name, masked):
    with ExitStack() as ctx:
        kit = Kit(nc, ctx, name + "_")
        sb, ps, sem = kit.sb, kit.ps, kit.sem
        turnstile = sem("turnstile")
        wts = sb("wts", [P, 4, HALVES, D])
        ctxT = sb("ctxT", [P, HALVES, B, 2, SC])
        bqk = sb("bqk", [P, 2, HALVES])
        bv = sb("bv", [P, D])
        bo = sb("bo", [P, D])
        headmask = sb("headmask", [P, HH])
        pairmask = sb("pairmask", [P, D])
        kT = sb("kT", [P, HALVES, B, SC])
        kblk = sb("kblk", [P, B, HALVES, HH, SC])
        vblk = sb("vblk", [P, B, D])
        vst = sb("vst", [P, D])
        if masked:
            mask_i = sb("mask_i", [P, TILES, SC], i32)
            keep = sb("keep", [P, TILES, SC])
            fill = sb("fill", [P, TILES, SC])
        stats = sb("stats", [P, CT, 6])
        mv = sb("mv", [P, CT, 2])
        var = sb("var", [P, CT])
        rstd = sb("rstd", [P, CT])
        xn = sb("xn", [P, CT, D])
        xnT = sb("xnT", [P, HALVES, CW])
        qT = sb("qT", [P, HALVES, CW])
        prob = sb("prob", [P, CT, H, SC])
        mx = sb("mx", [P, CT, H])
        den = sb("den", [P, CT, H])
        rden = sb("rden", [P, CT, H])
        pT = sb("pT", [P, H // 2, CW])
        oT = sb("oT", [P, HALVES, CW])
        front = ps("front", [P, HALVES, CW])
        score = [ps(f"score{i}", [P, H, SC]) for i in range(2)]
        ptps = ps("ptps", [P, H // 2, P])

        loaded = sem("loaded")
        masks_made, pair_made = sem("masks_made"), sem("pair_made")
        k_psum, k_made = sem("k_psum"), sem("k_made")
        v_psum, v_made = sem("v_psum"), sem("v_made")
        kblk_made, mask_step = sem("kblk_made"), sem("mask_step")

        with nc.Block() as block:
            @block.sync
            def _(sp):
                sp.dma_start(wts[:], w["wts"].rearrange("f (k p) n -> p f k n", p=P)).then_inc(loaded, 16)
                for twice in range(2):
                    for k in range(HALVES):
                        sp.dma_start(ctxT[:, k, :, twice, :], w["ctxT"][k * P:(k + 1) * P]).then_inc(loaded, 16)
                sp.dma_start(bqk[:], w["bqk"].rearrange("p f k -> p f k")).then_inc(loaded, 16)
                sp.dma_start(bv[:], w["bv"].partition_broadcast(P)).then_inc(loaded, 16)
                sp.dma_start(bo[:], w["bo"].partition_broadcast(P)).then_inc(loaded, 16)
                if masked:
                    sp.dma_start(mask_i[:], w["mask"].rearrange("(t p) k -> p t k", p=P)).then_inc(loaded, 16)

            LOADS = 16 * (9 if masked else 8)

            @block.gpsimd
            def _(pool):
                nc.gpsimd.memset(headmask[:], 1.0).then_inc(masks_made, 1)
                pool.wait_ge(masks_made, 1)
                nc.gpsimd.affine_select(out=headmask[:], in_=headmask[:], compare_op=ALU.is_ge, fill=0.0, base=0,
                                        pattern=[[-DK, HH]], channel_multiplier=1).then_inc(masks_made, 1)
                pool.wait_ge(masks_made, 2)
                nc.gpsimd.affine_select(out=headmask[:], in_=headmask[:], compare_op=ALU.is_ge, fill=0.0,
                                        base=DK - 1, pattern=[[DK, HH]], channel_multiplier=-1).then_inc(masks_made, 1)

            @block.tensor
            def _(pe):
                pe.wait_ge(loaded, LOADS)
                for half in range(HALVES):
                    for k in range(HALVES):
                        last = nc.tensor.matmul(front[:, half, 0:B * SC], wts[:, 1, k, half * P:(half + 1) * P],
                                                ctxT[:, k, :, 0, :], start=(k == 0), stop=(k == HALVES - 1))
                    last.then_inc(k_psum, 1)
                for b in range(B):
                    for k in range(HALVES):
                        last = nc.tensor.matmul(score[b // 2][:].rearrange("p h k -> p (h k)")[:, 512 * (b % 2):512 * (b % 2) + D],
                                                ctxT[:, k, b, :, :], wts[:, 2, k, :],
                                                start=(k == 0), stop=(k == HALVES - 1))
                    last.then_inc(v_psum, 1)

            @block.scalar
            def _(act):
                for half in range(HALVES):
                    act.wait_ge(k_psum, half + 1)
                    nc.scalar.activation(kT[:, half], front[:, half, 0:B * SC], ACT.Identity,
                                         bias=bqk[:, 1, half:half + 1]).then_inc(k_made, 1)

            @block.vector
            def _(dve):
                dve.wait_ge(loaded, LOADS)
                if masked:
                    nc.vector.tensor_scalar(keep[:], mask_i[:], 0.0, None, ALU.not_equal).then_inc(mask_step, 1)
                    dve.wait_ge(mask_step, 1)
                    nc.vector.tensor_scalar(fill[:], keep[:], 1.0, -NEG, ALU.subtract, ALU.mult).then_inc(mask_step, 1)
                pm = pairmask[:].rearrange("p (j a d) -> p j a d", a=2, d=DK)
                for rows in range(2):
                    for a in range(2):
                        nc.vector.memset(pm[SC * rows:SC * rows + SC, :, a, :],
                                         1.0 if a == rows else 0.0).then_inc(pair_made, 1)
                dve.wait_ge(pair_made, 4)
                dve.wait_ge(masks_made, 3)
                for b in range(B):
                    dve.wait_ge(v_psum, b + 1)
                    nc.vector.tensor_tensor(vblk[:, b], score[b // 2][:].rearrange("p h k -> p (h k)")[:, 512 * (b % 2):512 * (b % 2) + D],
                                            bv[:], ALU.add).then_inc(v_made, 1)
                    dve.wait_ge(v_made, 2 * b + 1)
                    nc.vector.tensor_tensor(vblk[:, b], vblk[:, b], pairmask[:], ALU.mult).then_inc(v_made, 1)
                for half in range(HALVES):
                    dve.wait_ge(k_made, half + 1)
                    for b in range(B):
                        nc.vector.tensor_tensor(kblk[:, b, half], bc(kT[:, half, b, :], 1, [P, HH, SC]),
                                                bc(headmask[:], 2, [P, HH, SC]), ALU.mult).then_inc(kblk_made, 1)

        stats_done, ln_stats, var_done, rstd_ready = sem("stats_done"), sem("ln_stats"), sem("var_done"), sem("rstd_ready")
        xn_ready, xnT_psum, xnT_ready = sem("xn_ready"), sem("xnT_psum"), sem("xnT_ready")
        q_psum, qT_ready, bo_added = sem("q_psum"), sem("qT_ready"), sem("bo_added")
        scores_ready, scores_used, masked_mult, masked_ready = (sem("scores_ready"), sem("scores_used"), sem("masked_mult"),
                                                   sem("masked_ready"))
        max_done, centered, exp_ready, sum_done = sem("max_done"), sem("centered"), sem("exp_ready"), sem("sum_done")
        rden_ready, probs_ready, probsT_psum, pT_ready = (sem("rden_ready"), sem("probs_ready"), sem("probsT_psum"),
                                                          sem("pT_ready"))
        vst_ready, o_psum, oT_ready, y_psum, y_added = (sem("vst_ready"), sem("o_psum"), sem("oT_ready"),
                                                        sem("y_psum"), sem("y_added"))
        used = scores_used

        with nc.Block() as block:
            @block.vector
            def _(dve):
                def ln_moments(c):
                    for t in range(CT):
                        nc.vector.bn_stats(stats[:, t], x_sb[:, ds(CT * c + t, 1), :]).then_inc(stats_done, 1)
                    dve.wait_ge(var_done, c)
                    passed(dve, stats_done, CT * (c + 1), turnstile)
                    for t in range(CT):
                        nc.vector.bn_aggr(mv[:, t], stats[:, t]).then_inc(ln_stats, 1)

                def ln_apply(c):
                    dve.wait_ge(rstd_ready, c + 1)
                    dve.wait_ge(ln_stats, CT * (c + 1))
                    dve.wait_ge(xnT_psum, c)
                    for t in range(CT):
                        nc.vector.tensor_scalar(xn[:, t], x_sb[:, ds(CT * c + t, 1), :], mv[:, t, 0:1], rstd[:, t:t + 1],
                                                ALU.subtract, ALU.mult).then_inc(xn_ready, 1)

                def apply_mask(c, t):
                    if not masked:
                        return
                    dve.wait_ge(scores_ready, CT * c + t + 1)
                    dve.wait_ge(probsT_psum, CT * c + t + 1)
                    nc.vector.tensor_tensor(prob[:, t], score[t % 2][:], keep[:, ds(CT * c + t, 1), :].broadcast_to([P, H, SC]),
                                            ALU.mult).then_inc(scores_used, 1)

                def center(c, t):
                    if masked:
                        dve.wait_ge(masked_ready, CT * c + t + 1)
                        src = prob[:, t]
                    else:
                        dve.wait_ge(scores_ready, CT * c + t + 1)
                        dve.wait_ge(probsT_psum, CT * c + t + 1)
                        src = score[t % 2][:]
                    if t == 0:
                        dve.wait_ge(centered if masked else scores_used, CT * c + (0 if masked else 2))
                    nc.vector.tensor_reduce(mx[:, t], src, axis=X, op=ALU.max).then_inc(max_done, 1)
                    dve.wait_ge(max_done, CT * c + t + 1)
                    nc.vector.tensor_tensor(prob[:, t], src, bc(mx[:, t], 2, [P, H, SC]),
                                            ALU.subtract).then_inc(centered if masked else scores_used, 1)

                def normalizer(c, t):
                    dve.wait_ge(exp_ready, CT * c + t + 1)
                    nc.vector.tensor_reduce(den[:, t], prob[:, t], axis=X, op=ALU.add).then_inc(sum_done, 1)
                    dve.wait_ge(sum_done, CT * c + t + 1)
                    if t == 0:
                        dve.wait_ge(probs_ready, CT * c)
                    nc.vector.reciprocal(rden[:, t], den[:, t]).then_inc(rden_ready, 1)

                def add_residual(c):
                    dve.wait_ge(bo_added, c + 1)
                    for bank in range(2):
                        dve.wait_ge(y_psum, 2 * c + bank + 1)
                        xs = x_sb[:, ds(CT * c + 2 * bank, 2), :]
                        nc.vector.tensor_tensor(xs, front[:, bank].rearrange("p (t d) -> p t d", t=2), xs,
                                                ALU.add).then_inc(y_added, 1)

                def chunk(c, last):
                    apply_mask(c, 0)
                    apply_mask(c, 1)
                    center(c, 0)
                    apply_mask(c, 2)
                    center(c, 1)
                    normalizer(c, 0)
                    if not last:
                        ln_moments(c + 1)
                    apply_mask(c, 3)
                    center(c, 2)
                    normalizer(c, 1)
                    if not last:
                        ln_apply(c + 1)
                    center(c, 3)
                    normalizer(c, 2)
                    normalizer(c, 3)
                    add_residual(c)

                nc.vector.memset(var[:], 0.0).then_inc(probsT_psum, CT)
                nc.vector.memset(den[:], 0.0).then_inc(used, 2)
                dve.wait_ge(probsT_psum, CT)
                dve.wait_ge(used, 2)
                ln_moments(0)
                ln_apply(0)
                with dve.Fori(0, CHUNKS - 1) as c:
                    chunk(c, False)
                chunk(CHUNKS - 1, True)

            @block.gpsimd
            def _(pool):
                def make_rstd(c):
                    pool.wait_ge(ln_stats, CT * (c + 1))
                    nc.gpsimd.tensor_tensor(var[:], mv[:, :, 1], eps_pow[:, 0], ALU.add).then_inc(var_done, 1)
                    pool.wait_ge(var_done, c + 1)
                    pool.wait_ge(xn_ready, CT * c)
                    nc.gpsimd.tensor_tensor(rstd[:], var[:], eps_pow[:, 1], ALU.pow).then_inc(rstd_ready, 1)

                def add_bo(c):
                    pool.wait_ge(xn_ready, CT * (c + 1))
                    xs = x_sb[:, ds(CT * c, CT), :]
                    nc.gpsimd.tensor_tensor(xs, xs, bc(bo[:], 1, [P, CT, D]), ALU.add).then_inc(bo_added, 1)

                def add_fill(c, t):
                    if not masked:
                        return
                    pool.wait_ge(scores_used, CT * c + t + 3)
                    nc.gpsimd.tensor_tensor(prob[:, t], prob[:, t], fill[:, ds(CT * c + t, 1), :].broadcast_to([P, H, SC]),
                                            ALU.add).then_inc(masked_ready, 1)

                def normalize(c, t):
                    pool.wait_ge(rden_ready, CT * c + t + 1)
                    nc.gpsimd.tensor_tensor(prob[:, t], prob[:, t], bc(rden[:, t], 2, [P, H, SC]),
                                            ALU.mult).then_inc(probs_ready, 1)

                def chunk(c, last):
                    pool.wait_ge(o_psum, 2 * c)
                    nc.gpsimd.tensor_copy(vst[:], vblk[:, ds(c // 2, 1), :]).then_inc(vst_ready, 1)
                    add_fill(c, 0)
                    add_fill(c, 1)
                    add_fill(c, 2)
                    normalize(c, 0)
                    if not last:
                        make_rstd(c + 1)
                    add_fill(c, 3)
                    normalize(c, 1)
                    if not last:
                        add_bo(c + 1)
                    normalize(c, 2)
                    normalize(c, 3)

                pool.wait_ge(probsT_psum, CT)
                make_rstd(0)
                add_bo(0)
                with pool.Fori(0, CHUNKS - 1) as c:
                    chunk(c, False)
                chunk(CHUNKS - 1, True)

            @block.scalar
            def _(act):
                def evacuate_xnT(c):
                    act.wait_ge(xnT_psum, c + 1)
                    act.wait_ge(q_psum, 2 * c)
                    nc.scalar.activation(xnT[:], front[:], ACT.Copy).then_inc(xnT_ready, 1)

                def evacuate_qT(c):
                    act.wait_ge(scores_ready, CT * c)
                    for half in range(HALVES):
                        act.wait_ge(q_psum, 2 * c + half + 1)
                        nc.scalar.activation(qT[:, half], front[:, half], ACT.Identity,
                                             bias=bqk[:, 0, half:half + 1]).then_inc(qT_ready, 1)

                def exponential(c, t):
                    if masked:
                        act.wait_ge(centered, CT * c + t + 1)
                    else:
                        act.wait_ge(scores_used, CT * c + t + 3)
                    nc.scalar.activation(prob[:, t], prob[:, t], ACT.Exp, scale=SCALE).then_inc(exp_ready, 1)

                def evacuate_pT(c, t):
                    act.wait_ge(probsT_psum, CT * c + t + 1 + CT)
                    if t == 0:
                        act.wait_ge(o_psum, 2 * c)
                    nc.scalar.activation(pT[:, :, t * P:(t + 1) * P], ptps[:], ACT.Copy).then_inc(pT_ready, 1)

                def evacuate_oT(c):
                    act.wait_ge(y_psum, 2 * c)
                    for half in range(HALVES):
                        act.wait_ge(o_psum, 2 * c + half + 1)
                        nc.scalar.activation(oT[:, half], front[:, half], ACT.Copy).then_inc(oT_ready, 1)

                def chunk(c, last):
                    exponential(c, 0)
                    exponential(c, 1)
                    exponential(c, 2)
                    evacuate_pT(c, 0)
                    if not last:
                        evacuate_xnT(c + 1)
                    evacuate_pT(c, 1)
                    if not last:
                        evacuate_qT(c + 1)
                    exponential(c, 3)
                    evacuate_pT(c, 2)
                    evacuate_pT(c, 3)
                    evacuate_oT(c)

                evacuate_xnT(0)
                evacuate_qT(0)
                with act.Fori(0, CHUNKS - 1) as c:
                    chunk(c, False)
                chunk(CHUNKS - 1, True)

            @block.tensor
            def _(pe):
                def transpose_xn(c):
                    pe.wait_ge(xn_ready, CT * (c + 1))
                    for t in range(CT):
                        for half in range(HALVES):
                            last = nc.tensor.transpose(front[:, half, t * P:(t + 1) * P],
                                                       xn[:, t, half * P:(half + 1) * P], ident[:])
                    last.then_inc(xnT_psum, 1)

                def project_q(c):
                    pe.wait_ge(xnT_ready, c + 1)
                    for half in range(HALVES):
                        for k in range(HALVES):
                            last = nc.tensor.matmul(front[:, half], wts[:, 0, k, half * P:(half + 1) * P], xnT[:, k],
                                                    start=(k == 0), stop=(k == HALVES - 1))
                        last.then_inc(q_psum, 1)

                def scores(c, t):
                    if t == 0:
                        pe.wait_ge(qT_ready, 2 * (c + 1))
                    pe.wait_ge(scores_used, CT * c + t + 1)
                    for half in range(HALVES):
                        last = nc.tensor.matmul(score[t % 2][:, half * HH:(half + 1) * HH, :],
                                                qT[:, half, t * P:(t + 1) * P],
                                                kblk[:, ds(c // 2, 1), half].rearrange("p o h k -> p (o h k)"),
                                                start=True, stop=True)
                    last.then_inc(scores_ready, 1)

                def transpose_probs(c, t):
                    pe.wait_ge(probs_ready, CT * c + t + 1)
                    pe.wait_ge(pT_ready, CT * c + t)
                    for pair in range(H // 2):
                        last = nc.tensor.transpose(ptps[:, pair], prob[:, t, 2 * pair:2 * pair + 2, :], ident[:])
                    last.then_inc(probsT_psum, 1)

                def weigh_values(c):
                    pe.wait_ge(vst_ready, c + 1)
                    pe.wait_ge(pT_ready, CT * (c + 1))
                    for half in range(HALVES):
                        for j in range(4):
                            last = nc.tensor.matmul(front[32 * j:32 * j + 32, half],
                                                    vst[:, half * P + 32 * j:half * P + 32 * j + 32],
                                                    pT[:, half * 4 + j], start=True, stop=True)
                        last.then_inc(o_psum, 1)

                def project_out(c):
                    for bank in range(2):
                        pe.wait_ge(oT_ready, 2 * (c + 1))
                        for t in (2 * bank, 2 * bank + 1):
                            for k in range(HALVES):
                                last = nc.tensor.matmul(front[:, bank, (t % 2) * D:(t % 2 + 1) * D],
                                                        oT[:, k, t * P:(t + 1) * P], wts[:, 3, k],
                                                        start=(k == 0), stop=(k == HALVES - 1))
                        last.then_inc(y_psum, 1)

                def chunk(c, last):
                    for t in range(CT):
                        scores(c, t)
                    transpose_probs(c, 0)
                    pe.wait_ge(y_added, 2 * c)
                    if not last:
                        transpose_xn(c + 1)
                    transpose_probs(c, 1)
                    if not last:
                        project_q(c + 1)
                    transpose_probs(c, 2)
                    transpose_probs(c, 3)
                    if not last:
                        pe.wait_ge(qT_ready, 2 * (c + 2))
                    weigh_values(c)
                    project_out(c)

                transpose_xn(0)
                project_q(0)
                with pe.Fori(0, CHUNKS - 1) as c:
                    chunk(c, False)
                chunk(CHUNKS - 1, True)

PAIRS = ((0, 0), (1, 0), (2, 0), (0, 1), (1, 1), (0, 2))
KROWS = len(PAIRS) * DK
MROWS = 2
GH = 4
GROUPS = B * H // GH
KT = S // P
VW = DK + 1
UNITS = GROUPS * 2


def self_projections(nc, x_sb, src_sb, ident, eps_pow, w, q_parts, k_parts, v_dram):
    with ExitStack() as ctx:
        kit = Kit(nc, ctx, "sp_")
        sb, ps, sem = kit.sb, kit.ps, kit.sem
        turnstile = sem("turnstile")
        wts = sb("wts", [P, 3, HALVES, D])
        swcol = sb("swcol", [P, HALVES])
        swblk = sb("swblk", [P, HALVES, P])
        stats, mv = sb("stats", [P, CT, 6]), sb("mv", [P, CT, 2])
        var, rstd = sb("var", [P, CT]), sb("rstd", [P, CT])
        xn = sb("xn", [P, CT, D])
        srcT = sb("srcT", [P, HALVES, CW])
        qT, th = sb("qT", [P, HALVES, CW]), sb("th", [P, HALVES, CW])
        qrest, krest = sb("qrest", [P, HALVES, CW]), sb("krest", [P, HALVES, CW])
        qpart = [sb(f"qpart{i}", [P, 3, HALVES, CW], bf16) for i in range(2)]
        kpart = [sb(f"kpart{i}", [P, 3, HALVES, CW], bf16) for i in range(2)]
        vt = [sb(f"vt{i}", [P, CT, H, VW]) for i in range(2)]
        vps, qps, kps, zps = (ps(n, [P, HALVES, CW]) for n in ("vps", "qps", "kps", "zps"))

        loaded, blk_made = sem("loaded"), sem("blk_made")
        stats_done, ln_stats, var_done, rstd_ready = sem("stats_done"), sem("ln_stats"), sem("var_done"), sem("rstd_ready")
        xn_ready, xnT_psum, srcT_ready = sem("xn_ready"), sem("xnT_psum"), sem("srcT_ready")
        v_psum, v_ready, q_psum, k_psum, z_psum = (sem("v_psum"), sem("v_ready"), sem("q_psum"), sem("k_psum"),
                                                   sem("z_psum"))
        qT_ready, th_ready, q_scaled = sem("qT_ready"), sem("th_ready"), sem("q_scaled")
        k1, krest_made, k2, k3 = sem("k1"), sem("krest_made"), sem("k2"), sem("k3")
        q1, qrest_made, q2, q3 = sem("q1"), sem("qrest_made"), sem("q2"), sem("q3")
        src_kept = sem("src_kept")
        q_stored, k_stored, v_stored = ([sem(f"{n}_stored{i}") for i in range(2)] for n in "qkv")

        with nc.Block() as block:
            @block.sync
            def _(sp):
                sp.dma_start(wts[:], w["ffn_qkv"].rearrange("f (k p) n -> p f k n", p=P)).then_inc(loaded, 16)
                sp.dma_start(swcol[:], w["scale_w"]).then_inc(loaded, 16)

                def store(i, par):
                    c = 2 * i + par
                    cols = slice(par * CW, (par + 1) * CW)
                    sp.wait_ge(v_ready, 2 * (c + 1))
                    for t in range(CT):
                        sp.dma_start(v_dram[ds(4 * i, 4), :, CT * par + t, :].rearrange("g p x -> p g x"),
                                     vt[par][:, t].rearrange("p (g h) v -> p g (h v)", g=4)).then_inc(v_stored[par], 16)
                    for parts, dram, ready, stored, which in ((kpart, k_parts, k3, k_stored, 1),
                                                              (qpart, q_parts, q3, q_stored, 0)):
                        sp.wait_ge(ready, c + 1)
                        for row, pair in enumerate(PAIRS):
                            for half in range(HALVES):
                                dst = dram[ds(4 * i + 2 * half, 2), :, row * DK:(row + 1) * DK, cols]
                                sp.dma_start(dst.rearrange("g h d t -> (g h) d t"),
                                             parts[par][:, pair[which], half, :]).then_inc(stored[par], 16)

                with sp.Fori(0, B) as i:
                    for par in range(2):
                        store(i, par)
                for par in range(2):
                    sp.wait_ge(v_stored[par], 16 * B * CT)
                    for stored in (q_stored, k_stored):
                        sp.wait_ge(stored[par], 16 * B * 12)

            @block.vector
            def _(dve):
                dve.wait_ge(loaded, 32)
                for half in range(HALVES):
                    nc.vector.tensor_tensor(swblk[:, half].rearrange("p (h d) -> p h d", d=DK),
                                            bc(w["headmask"][:], 2, [P, HH, DK]),
                                            bc(swcol[:, half:half + 1].broadcast_to([P, HH]), 2, [P, HH, DK]),
                                            ALU.mult).then_inc(blk_made, 1)
                for i in range(2):
                    nc.vector.memset(vt[i][:, :, :, DK:], 1.0).then_inc(blk_made, 1)

                def layernorm(c):
                    for t in range(CT):
                        nc.vector.bn_stats(stats[:, t], x_sb[:, ds(CT * c + t, 1), :]).then_inc(stats_done, 1)
                    dve.wait_ge(var_done, c)
                    passed(dve, stats_done, CT * (c + 1), turnstile)
                    for t in range(CT):
                        nc.vector.bn_aggr(mv[:, t], stats[:, t]).then_inc(ln_stats, 1)

                def ln_apply(c):
                    dve.wait_ge(rstd_ready, c + 1)
                    dve.wait_ge(ln_stats, CT * (c + 1))
                    dve.wait_ge(xnT_psum, c)
                    dve.wait_ge(src_kept, c)
                    for t in range(CT):
                        nc.vector.tensor_scalar(xn[:, t], x_sb[:, ds(CT * c + t, 1), :], mv[:, t, 0:1], rstd[:, t:t + 1],
                                                ALU.subtract, ALU.mult).then_inc(xn_ready, 1)

                def chunk(i, par, last):
                    c = 2 * i + par
                    if not last:
                        layernorm(c + 1)
                    dve.wait_ge(k1, c + 1)
                    dve.wait_ge(k3, c)
                    nc.vector.tensor_tensor(krest[:], kps[:], kpart[par][:, 0], ALU.subtract).then_inc(krest_made, 1)
                    if not last:
                        ln_apply(c + 1)
                    dve.wait_ge(th_ready, c + 1)
                    dve.wait_ge(qT_ready, c + 1)
                    nc.vector.scalar_tensor_tensor(out=qT[:], in0=th[:], scalar=1.0, in1=qT[:], op0=ALU.add,
                                                   op1=ALU.mult).then_inc(q_scaled, 1)
                    dve.wait_ge(q1, c + 1)
                    dve.wait_ge(q3, c)
                    nc.vector.tensor_tensor(qrest[:], qT[:], qpart[par][:, 0], ALU.subtract).then_inc(qrest_made, 1)

                layernorm(0)
                ln_apply(0)
                with dve.Fori(0, B - 1) as i:
                    chunk(i, 0, False)
                    chunk(i, 1, False)
                chunk(B - 1, 0, False)
                chunk(B - 1, 1, True)

            @block.gpsimd
            def _(pool):
                def make_rstd(c):
                    pool.wait_ge(ln_stats, CT * (c + 1))
                    nc.gpsimd.tensor_tensor(var[:], mv[:, :, 1], eps_pow[:, 0], ALU.add).then_inc(var_done, 1)
                    pool.wait_ge(var_done, c + 1)
                    pool.wait_ge(xn_ready, CT * c)
                    nc.gpsimd.tensor_tensor(rstd[:], var[:], eps_pow[:, 1], ALU.pow).then_inc(rstd_ready, 1)

                def keep_src(c):
                    pool.wait_ge(xn_ready, CT * (c + 1))
                    nc.gpsimd.tensor_copy(src_sb[:, ds(CT * c, CT), :], xn[:]).then_inc(src_kept, 1)

                def chunk(i, par, last):
                    c = 2 * i + par
                    if not last:
                        make_rstd(c + 1)
                    pool.wait_ge(k2, c + 1)
                    nc.gpsimd.tensor_tensor(kpart[par][:, 2], krest[:], kpart[par][:, 1], ALU.subtract).then_inc(k3, 1)
                    if not last:
                        keep_src(c + 1)
                    pool.wait_ge(q2, c + 1)
                    nc.gpsimd.tensor_tensor(qpart[par][:, 2], qrest[:], qpart[par][:, 1], ALU.subtract).then_inc(q3, 1)

                make_rstd(0)
                keep_src(0)
                with pool.Fori(0, B - 1) as i:
                    chunk(i, 0, False)
                    chunk(i, 1, False)
                chunk(B - 1, 0, False)
                chunk(B - 1, 1, True)

            @block.scalar
            def _(act):
                def evacuate_srcT(c):
                    act.wait_ge(xnT_psum, c + 1)
                    act.wait_ge(k_psum, c)
                    nc.scalar.activation(srcT[:], vps[:], ACT.Copy).then_inc(srcT_ready, 1)

                def chunk(i, par, last):
                    c = 2 * i + par
                    act.wait_ge(blk_made, 4)
                    act.wait_ge(v_stored[par], 16 * CT * i)
                    for bank in range(2):
                        act.wait_ge(v_psum, 2 * c + bank + 1)
                        nc.scalar.activation(vt[par][:, 2 * bank:2 * bank + 2, :, 0:DK],
                                             vps[:, bank].rearrange("p (t h d) -> p t h d", t=2, h=H),
                                             ACT.Copy).then_inc(v_ready, 1)
                    act.wait_ge(q_psum, c + 1)
                    act.wait_ge(qrest_made, c)
                    nc.scalar.activation(qT[:], qps[:], ACT.Copy).then_inc(qT_ready, 1)
                    act.wait_ge(k_psum, c + 1)
                    act.wait_ge(k_stored[par], 16 * 12 * i)
                    nc.scalar.activation(kpart[par][:, 0], kps[:], ACT.Copy).then_inc(k1, 1)
                    if not last:
                        evacuate_srcT(c + 1)
                    act.wait_ge(krest_made, c + 1)
                    nc.scalar.activation(kpart[par][:, 1], krest[:], ACT.Copy).then_inc(k2, 1)
                    act.wait_ge(z_psum, c + 1)
                    act.wait_ge(q_scaled, c)
                    nc.scalar.activation(th[:], zps[:], ACT.Tanh, scale=0.5).then_inc(th_ready, 1)
                    act.wait_ge(q_scaled, c + 1)
                    act.wait_ge(q_stored[par], 16 * 12 * i)
                    nc.scalar.activation(qpart[par][:, 0], qT[:], ACT.Copy).then_inc(q1, 1)
                    act.wait_ge(qrest_made, c + 1)
                    nc.scalar.activation(qpart[par][:, 1], qrest[:], ACT.Copy).then_inc(q2, 1)

                evacuate_srcT(0)
                with act.Fori(0, B - 1) as i:
                    chunk(i, 0, False)
                    chunk(i, 1, False)
                chunk(B - 1, 0, False)
                chunk(B - 1, 1, True)

            @block.tensor
            def _(pe):
                def transpose_xn(c):
                    pe.wait_ge(xn_ready, CT * (c + 1))
                    pe.wait_ge(v_ready, 2 * c)
                    for t in range(CT):
                        for half in range(HALVES):
                            last = nc.tensor.transpose(vps[:, half, t * P:(t + 1) * P],
                                                       xn[:, t, half * P:(half + 1) * P], ident[:])
                    last.then_inc(xnT_psum, 1)

                def chunk(i, par, last_chunk):
                    c = 2 * i + par
                    pe.wait_ge(srcT_ready, c + 1)
                    for bank in range(2):
                        for t in (2 * bank, 2 * bank + 1):
                            for k in range(HALVES):
                                last = nc.tensor.matmul(vps[:, bank, (t % 2) * D:(t % 2 + 1) * D],
                                                        srcT[:, k, t * P:(t + 1) * P], wts[:, 2, k],
                                                        start=(k == 0), stop=(k == HALVES - 1))
                        last.then_inc(v_psum, 1)
                    pe.wait_ge(qT_ready, c)
                    for half in range(HALVES):
                        for k in range(HALVES):
                            last = nc.tensor.matmul(qps[:, half], wts[:, 0, k, half * P:(half + 1) * P], srcT[:, k],
                                                    start=(k == 0), stop=(k == HALVES - 1))
                    last.then_inc(q_psum, 1)
                    pe.wait_ge(krest_made, c)
                    for half in range(HALVES):
                        for k in range(HALVES):
                            last = nc.tensor.matmul(kps[:, half], wts[:, 1, k, half * P:(half + 1) * P], srcT[:, k],
                                                    start=(k == 0), stop=(k == HALVES - 1))
                    last.then_inc(k_psum, 1)
                    if not last_chunk:
                        transpose_xn(c + 1)
                    pe.wait_ge(qT_ready, c + 1)
                    pe.wait_ge(th_ready, c)
                    for half in range(HALVES):
                        last = nc.tensor.matmul(zps[:, half], swblk[:, half], qT[:, half], start=True, stop=True)
                    last.then_inc(z_psum, 1)

                pe.wait_ge(loaded, 32)
                pe.wait_ge(blk_made, 4)
                transpose_xn(0)
                with pe.Fori(0, B - 1) as i:
                    chunk(i, 0, False)
                    chunk(i, 1, False)
                chunk(B - 1, 0, False)
                chunk(B - 1, 1, True)


def self_attention(nc, attn, ident, q_parts, k_parts, v_dram, m_dram):
    SETS = 3
    with ExitStack() as ctx:
        kit = Kit(nc, ctx, "sa_")
        sb, ps, sem = kit.sb, kit.ps, kit.sem
        turnstile = sem("turnstile")
        qs = [sb(f"q{i}", [KROWS + MROWS, GH, S], bf16) for i in range(SETS)]
        ks = [sb(f"k{i}", [KROWS + MROWS, GH, S], bf16) for i in range(SETS)]
        vs = [sb(f"v{i}", [P, KT, GH, VW]) for i in range(SETS)]
        ex = [[sb(f"e{i}{p}", [P, 2, CW]) for p in range(2)] for i in range(2)]
        mpart = [sb(f"mpart{i}", [P, GH, CT, 2]) for i in range(2)]
        mfull = sb("mfull", [P, GH, CT])
        negm = sb("negm", [GH * CT, MROWS, P], bf16)
        o_sb = sb("o", [P, CW])
        rden = sb("rden", [P, CT, GH])
        bps = [ps(f"b{p}", [P, 2, CW]) for p in range(2)]
        aps = [ps(f"a{i}", [P, CW]) for i in range(2)]
        ops = ps("ops", [P, CW])
        misc = ps("misc", [P, CT, P])

        q_loaded, k_loaded, v_loaded = ([sem(f"{n}_loaded{i}") for i in range(SETS)] for n in "qkv")
        ones_made, b_scores, exp_done, pv_done = sem("ones_made"), sem("b_scores"), sem("exp_done"), sem("pv_done")
        a_scores, max_done, m_full, m_psum = sem("a_scores"), sem("max_done"), sem("m_full"), sem("m_psum")
        negm_hi, negm_ready, m_stored, m_loaded = sem("negm_hi"), sem("negm_ready"), sem("m_stored"), sem("m_loaded")
        o_evacuated, o_psum, rden_made, o_done = sem("o_evacuated"), sem("o_psum"), sem("rden_made"), sem("o_done")
        AM = GH * CT * 2

        def groups(eng, body):
            with eng.Fori(0, GROUPS // SETS - 1) as i:
                for j in range(SETS):
                    body(i * SETS + j, i, j)
            for g in range(GROUPS - SETS - 1, GROUPS):
                body(g, g // SETS, g % SETS)

        with nc.Block() as block:
            @block.sync
            def _(sp):
                def load(g, turn, s):
                    sp.dma_start(qs[s][0:KROWS], q_parts[ds(g, 1)].rearrange("g h r t -> r (g h) t")).then_inc(q_loaded[s], 16)
                    sp.dma_start(ks[s][0:KROWS], k_parts[ds(g, 1)].rearrange("g h r t -> r (g h) t")).then_inc(k_loaded[s], 16)
                    sp.dma_start(vs[s][:].rearrange("p k h v -> p k (h v)"),
                                 v_dram[ds(g, 1)].rearrange("g p k x -> p (g k) x")).then_inc(v_loaded[s], 16)

                def pass_max(a, s, qc):
                    sp.wait_ge(negm_ready, a + 1)
                    sp.dma_start(m_dram[ds(a, 1)].rearrange("a r c q -> (a c) r q"), negm[:]).then_inc(m_stored, 16)
                    sp.wait_ge(m_stored, 16 * (a + 1))
                    sp.dma_start(qs[s][KROWS:, :, qc * CW:(qc + 1) * CW],
                                 m_dram[ds(a, 1)].rearrange("a r (h t) q -> r (a h) (t q)", h=GH)).then_inc(m_loaded, 16)

                def body(g, turn, j):
                    for qc in range(2):
                        n = 2 * g + qc
                        if qc == 0 and not (isinstance(g, int) and g + 2 >= GROUPS):
                            sp.wait_ge(pv_done, 16 * n + 4)
                            load(g + 2, turn, (j + 2) % SETS)
                        a = n + 1
                        if not (isinstance(a, int) and a >= UNITS):
                            pass_max(a, (j + (a_is_next(qc))) % SETS, (qc + 1) % 2)

                def a_is_next(qc):
                    return 1 if qc == 1 else 0

                load(0, 0, 0)
                load(1, 0, 1)
                pass_max(0, 0, 0)
                groups(sp, body)

            @block.gpsimd
            def _(pool):
                for s in range(SETS):
                    nc.gpsimd.memset(ks[s][KROWS:], 1.0).then_inc(ones_made, 1)

            @block.vector
            def _(dve):
                def maxima(a, k, par):
                    head, rest = k // (CT * 2), k % (CT * 2)
                    dve.wait_ge(a_scores, AM * a + k + 1)
                    nc.vector.tensor_reduce(mpart[par][:, head, rest // 2, rest % 2:rest % 2 + 1], aps[k % 2][:], axis=X,
                                            op=ALU.max).then_inc(max_done, 1)

                def combine(a, par):
                    dve.wait_ge(max_done, AM * (a + 1))
                    dve.wait_ge(m_psum, a)
                    nc.vector.tensor_tensor(mfull[:], mpart[par][:, :, :, 0], mpart[par][:, :, :, 1],
                                            ALU.max).then_inc(m_full, 1)

                def split_max(a):
                    src = misc[:].rearrange("p a b -> p (a b)")[0:GH * CT, 0:P]
                    dve.wait_ge(m_psum, a + 1)
                    dve.wait_ge(m_stored, 16 * a)
                    nc.vector.tensor_scalar(negm[:, 0], src, -1.0, None, ALU.mult).then_inc(negm_hi, 1)
                    dve.wait_ge(negm_hi, a + 1)
                    nc.vector.scalar_tensor_tensor(out=negm[:, 1], in0=src, scalar=-1.0, in1=negm[:, 0], op0=ALU.mult,
                                                   op1=ALU.subtract).then_inc(negm_ready, 1)

                def normalize(n):
                    view = misc[:].rearrange("p t (h x) -> p t h x", h=GH)
                    dve.wait_ge(o_psum, n + 1)
                    nc.vector.reciprocal(rden[:], view[:, :, :, DK]).then_inc(rden_made, 1)
                    dve.wait_ge(rden_made, n + 1)
                    nc.vector.tensor_tensor(attn[:, ds(n, 1)].rearrange("p o (t h d) -> p (o t) h d", t=CT, h=GH),
                                            view[:, :, :, 0:DK], bc(rden[:], 3, [P, CT, GH, DK]),
                                            ALU.mult).then_inc(o_done, 1)

                def body(g, turn, j):
                    for qc in range(2):
                        n = 2 * g + qc
                        known = isinstance(g, int)
                        for kt in range(KT):
                            if not (known and g + 1 >= GROUPS):
                                for k in range(4 * kt, 4 * kt + 4):
                                    maxima(n + 2, k, qc)
                            if kt == 1 and not (known and n + 1 >= UNITS):
                                split_max(n + 1)
                            if kt == 4:
                                normalize(n)
                        if not (known and n + 2 >= UNITS):
                            combine(n + 2, qc)

                nc.vector.memset(o_sb[:], 1.0).then_inc(ones_made, 1)
                nc.vector.memset(ops[:], 0.0).then_inc(ones_made, 1)
                nc.vector.memset(rden[:], 0.0).then_inc(exp_done, 2)
                nc.vector.memset(mfull[:], 0.0).then_inc(pv_done, 4)
                dve.wait_ge(exp_done, 2)
                dve.wait_ge(pv_done, 4)
                for a in range(2):
                    for k in range(AM):
                        maxima(a, k, a)
                    combine(a, a)
                    if a == 0:
                        split_max(0)
                groups(dve, body)
                normalize(UNITS)

            @block.scalar
            def _(act):
                def body(g, turn, j):
                    for qc in range(2):
                        n = 2 * g + qc
                        for kt in range(KT):
                            for p in range(2):
                                act.wait_ge(b_scores, 16 * n + 2 * kt + p + 1)
                                act.wait_ge(pv_done, 16 * n + 2 * kt + p + 1)
                                nc.scalar.activation(ex[kt % 2][p][:], bps[p][:], ACT.Exp, scale=SCALE).then_inc(exp_done, 1)
                        act.wait_ge(pv_done, 16 * (n + 1) + 4)
                        act.wait_ge(o_psum, n + 1)
                        nc.scalar.activation(o_sb[:], ops[:], ACT.Copy).then_inc(o_evacuated, 1)

                act.wait_ge(ones_made, SETS + 2)
                groups(act, body)

            @block.tensor
            def _(pe):
                def first_scores(a, k, s, turn, qc):
                    head, rest = k // (CT * 2), k % (CT * 2)
                    if k == 0:
                        pe.wait_ge(q_loaded[s], 16 * (turn + 1))
                        pe.wait_ge(k_loaded[s], 16 * (turn + 1))
                    if not (isinstance(a, int) and a == 0 and k < 2):
                        pe.wait_ge(max_done, AM * a + k - 1)
                    q0 = (qc * CT + rest // 2) * P
                    nc.tensor.matmul(aps[k % 2][:], qs[s][0:KROWS, head, q0:q0 + P],
                                     ks[s][0:KROWS, head, (rest % 2) * CW:(rest % 2 + 1) * CW],
                                     start=True, stop=True).then_inc(a_scores, 1)

                def transpose_max(a):
                    pe.wait_ge(m_full, a + 1)
                    if not (isinstance(a, int) and a == 0):
                        pe.wait_ge(o_done, a - 1)
                    nc.tensor.transpose(misc[:].rearrange("p a b -> p (a b)")[0:GH * CT, 0:P],
                                        mfull[:].rearrange("p h t -> p (h t)"), ident[:]).then_inc(m_psum, 1)

                def transpose_out(n):
                    pe.wait_ge(o_evacuated, n)
                    if not (isinstance(n, int) and n >= UNITS - 1):
                        pe.wait_ge(negm_ready, n + 2)
                    else:
                        pe.wait_ge(o_done, n)
                    for t in range(CT):
                        last = nc.tensor.transpose(misc[:, t], o_sb[:, t * P:(t + 1) * P], ident[:])
                    last.then_inc(o_psum, 1)

                def scores(n, kt, p, s, qc):
                    if kt == 0 and p == 0:
                        pe.wait_ge(m_loaded, 16 * (n + 1))
                    pe.wait_ge(exp_done, 16 * n + 2 * kt + p + 1)
                    for head in (2 * p, 2 * p + 1):
                        last = nc.tensor.matmul(bps[p][:, head % 2], ks[s][:, head, kt * P:(kt + 1) * P],
                                                qs[s][:, head, qc * CW:(qc + 1) * CW], start=True, stop=True)
                    last.then_inc(b_scores, 1)

                def weigh_values(n, kt, p, s, turn):
                    if kt == 0 and p == 0:
                        pe.wait_ge(o_evacuated, n)
                        pe.wait_ge(v_loaded[s], 16 * (turn + 1))
                    pe.wait_ge(exp_done, 16 * n + 2 * kt + p + 3)
                    for head in (2 * p, 2 * p + 1):
                        last = nc.tensor.matmul(ops[32 * head:32 * head + VW], vs[s][:, kt, head], ex[kt % 2][p][:, head % 2],
                                                start=(kt == 0), stop=(kt == KT - 1))
                    last.then_inc(pv_done, 1)

                def body(g, turn, j):
                    known = isinstance(g, int)
                    s1 = (j + 1) % SETS
                    turn1 = turn + (j + 1) // SETS
                    for qc in range(2):
                        n = 2 * g + qc

                        def ahead(k):
                            if not (known and g + 1 >= GROUPS):
                                first_scores(n + 2, k, s1, turn1, qc)

                        for kt in range(KT):
                            scores(n, kt, 0, j, qc)
                            ahead(4 * kt)
                            if kt:
                                weigh_values(n, kt - 1, 0, j, turn)
                            ahead(4 * kt + 1)
                            scores(n, kt, 1, j, qc)
                            ahead(4 * kt + 2)
                            if kt:
                                weigh_values(n, kt - 1, 1, j, turn)
                            ahead(4 * kt + 3)
                            if kt == 1 and not (known and n + 1 >= UNITS):
                                transpose_max(n + 1)
                            if kt == 3:
                                transpose_out(n)
                        for p in range(2):
                            weigh_values(n, KT - 1, p, j, turn)

                pe.wait_ge(ones_made, SETS + 2)
                for a in range(2):
                    for k in range(AM):
                        first_scores(a, k, 0, 0, a)
                    if a == 0:
                        transpose_max(0)
                groups(pe, body)
                transpose_out(UNITS)

E8 = 8
MT = TILES + E8
F1 = 512
FK = F1 // P


def attention_out(nc, src_sb, attn, ident, eps_pow, w, logits, top, topi, gathered_in):
    with ExitStack() as ctx:
        kit = Kit(nc, ctx, "ao_")
        sb, ps, sem = kit.sb, kit.ps, kit.sem
        turnstile = sem("turnstile")
        wg, wo = sb("wg", [P, HALVES, D]), sb("wo", [P, HALVES, D])
        wr, br = sb("wr", [P, HALVES, E8]), sb("br", [P, E8])
        gb, n1g, n1b = sb("gb", [P, HALVES]), sb("n1g", [P, D]), sb("n1b", [P, D])
        gbh = sb("gbh", [P, HALVES])
        zero = sb("zero", [P, D])
        ao = sb("ao", [P, CT, D])
        outT, th, ogT = sb("outT", [P, HALVES, CW]), sb("th", [P, HALVES, CW]), sb("ogT", [P, HALVES, CW])
        y = sb("y", [P, CT, D])
        stats, mv = sb("stats", [P, CT, 6]), sb("mv", [P, CT, 2])
        var, rstd = sb("var", [P, CT]), sb("rstd", [P, CT])
        xr = sb("xr", [P, CT, D])
        xrT = sb("xrT", [P, HALVES, CW])
        tps, gps, yps, xps = (ps(n, [P, HALVES, CW]) for n in ("tps", "gps", "yps", "xps"))

        loaded, cleared, zero_made, gbh_made = sem("loaded"), sem("cleared"), sem("zero_made"), sem("gbh_made")
        ao_ready, outT_psum, outT_ready = sem("ao_ready"), sem("outT_psum"), sem("outT_ready")
        gate_psum, th_ready, og_ready, y_psum, y_ready = (sem("gate_psum"), sem("th_ready"), sem("og_ready"),
                                                          sem("y_psum"), sem("y_ready"))
        stats_done, ln_stats, var_done, rstd_ready = sem("stats_done"), sem("ln_stats"), sem("var_done"), sem("rstd_ready")
        yn_ready, yg_ready, xr_ready, src_ready = sem("yn_ready"), sem("yg_ready"), sem("xr_ready"), sem("src_ready")
        xrT_psum, xrT_ready, lg_psum, lg_ready, top_done = (
            sem("xrT_psum"), sem("xrT_ready"), sem("lg_psum"), sem("lg_ready"), sem("top_done"))

        def chunks(eng, first, body):
            first(0)
            with eng.Fori(0, CHUNKS - 1) as c:
                body(c, False)
            body(CHUNKS - 1, True)

        with nc.Block() as block:
            @block.sync
            def _(sp):
                for dst, name in ((wg, "gate_w"), (wo, "out_w"), (wr, "moe_gate_w")):
                    sp.dma_start(dst[:], w[name].rearrange("(k p) n -> p k n", p=P)).then_inc(loaded, 16)
                for dst, name in ((br, "moe_gate_b"), (n1g, "n1_g"), (n1b, "n1_b")):
                    sp.dma_start(dst[:], w[name].partition_broadcast(P)).then_inc(loaded, 16)
                sp.dma_start(gb[:], w["gate_b"]).then_inc(loaded, 16)
                sp.wait_ge(zero_made, 1)
                sp.dma_start(gathered_in.rearrange("(k p) d -> p k d", p=P),
                             bc(zero[:], 1, [P, MT, D])).then_inc(cleared, 16)
                sp.wait_ge(cleared, 16)

            @block.gpsimd
            def _(pool):
                def copy_attention(c):
                    pool.wait_ge(outT_psum, c)
                    units = attn[:, ds(c + 6 * (c // 2) + 1, 7), :][:, 0:7:2, :]
                    nc.gpsimd.tensor_copy(ao[:].rearrange("p t (g x) -> p g t x", g=4),
                                          units.rearrange("p g (t x) -> p g t x", t=CT)).then_inc(ao_ready, 1)

                def body(c, last):
                    if not last:
                        copy_attention(c + 1)
                    pool.wait_ge(ln_stats, CT * (c + 1))
                    nc.gpsimd.tensor_tensor(var[:], mv[:, :, 1], eps_pow[:, 0], ALU.add).then_inc(var_done, 1)
                    pool.wait_ge(var_done, c + 1)
                    pool.wait_ge(yn_ready, CT * c)
                    nc.gpsimd.tensor_tensor(rstd[:], var[:], eps_pow[:, 1], ALU.pow).then_inc(rstd_ready, 1)
                    pool.wait_ge(yn_ready, CT * (c + 1))
                    nc.gpsimd.tensor_tensor(y[:], y[:], bc(n1g[:], 1, [P, CT, D]), ALU.mult).then_inc(yg_ready, 1)
                    pool.wait_ge(yg_ready, c + 1)
                    pool.wait_ge(xrT_psum, c)
                    pool.wait_ge(src_ready, c)
                    nc.gpsimd.tensor_tensor(xr[:], y[:], bc(n1b[:], 1, [P, CT, D]), ALU.add).then_inc(xr_ready, 1)

                pool.wait_ge(loaded, 16 * 7)
                chunks(pool, copy_attention, body)

            @block.scalar
            def _(act):
                def gate(c):
                    act.wait_ge(outT_psum, c + 1)
                    act.wait_ge(og_ready, c)
                    nc.scalar.activation(outT[:], tps[:], ACT.Copy).then_inc(outT_ready, 1)
                    act.wait_ge(gate_psum, c + 1)
                    for half in range(HALVES):
                        nc.scalar.activation(th[:, half], gps[:, half], ACT.Tanh, bias=gbh[:, half:half + 1],
                                             scale=0.5).then_inc(th_ready, 1)

                def body(c, last):
                    if not last:
                        gate(c + 1)
                    act.wait_ge(xr_ready, c + 1)
                    nc.scalar.activation(src_sb[:, ds(CT * c, CT), :], xr[:], ACT.Copy).then_inc(src_ready, 1)
                    act.wait_ge(xrT_psum, c + 1)
                    act.wait_ge(lg_psum, c)
                    nc.scalar.activation(xrT[:], xps[:], ACT.Copy).then_inc(xrT_ready, 1)

                act.wait_ge(gbh_made, 1)
                chunks(act, gate, body)

            @block.vector
            def _(dve):
                nc.vector.memset(zero[:], 0.0).then_inc(zero_made, 1)
                dve.wait_ge(loaded, 16 * 7)
                nc.vector.tensor_scalar(gbh[:], gb[:], 0.5, None, ALU.mult).then_inc(gbh_made, 1)

                def apply_gate(c):
                    dve.wait_ge(th_ready, 2 * (c + 1))
                    dve.wait_ge(outT_ready, c + 1)
                    dve.wait_ge(y_psum, 2 * c)
                    nc.vector.scalar_tensor_tensor(out=ogT[:], in0=th[:], scalar=1.0, in1=outT[:], op0=ALU.add,
                                                   op1=ALU.mult).then_inc(og_ready, 1)

                def body(c, last):
                    for bank in range(2):
                        dve.wait_ge(y_psum, 2 * c + bank + 1)
                        if bank == 0:
                            dve.wait_ge(xr_ready, c)
                        nc.vector.scalar_tensor_tensor(
                            out=y[:, 2 * bank:2 * bank + 2], in0=yps[:, bank].rearrange("p (t d) -> p t d", t=2), scalar=0.5,
                            in1=src_sb[:, ds(CT * c + 2 * bank, 2), :], op0=ALU.mult, op1=ALU.add).then_inc(y_ready, 1)
                    for t in range(CT):
                        if t % 2 == 0:
                            dve.wait_ge(y_ready, 2 * c + t // 2 + 1)
                        nc.vector.bn_stats(stats[:, t], y[:, t]).then_inc(stats_done, 1)
                    passed(dve, stats_done, CT * (c + 1), turnstile)
                    for t in range(CT):
                        nc.vector.bn_aggr(mv[:, t], stats[:, t]).then_inc(ln_stats, 1)
                    if not last:
                        apply_gate(c + 1)
                    dve.wait_ge(rstd_ready, c + 1)
                    dve.wait_ge(ln_stats, CT * (c + 1))
                    for t in range(CT):
                        nc.vector.tensor_scalar(y[:, t], y[:, t], mv[:, t, 0:1], rstd[:, t:t + 1], ALU.subtract,
                                                ALU.mult).then_inc(yn_ready, 1)
                    dve.wait_ge(lg_psum, c + 1)
                    nc.vector.tensor_tensor(logits[:, ds(CT * c, CT), :],
                                            tps[:, 0, 0:CT * E8].rearrange("p (t e) -> p t e", t=CT),
                                            bc(br[:], 1, [P, CT, E8]), ALU.add).then_inc(lg_ready, 1)

                chunks(dve, apply_gate, body)
                dve.wait_ge(lg_ready, CHUNKS)
                for t in range(TILES):
                    nc.vector.max(out=top[:, t], in_=logits[:, t]).then_inc(top_done, 1)
                for t in range(TILES):
                    dve.wait_ge(top_done, t + 1)
                    nc.vector.max_index(out=topi[:, t], in_max=top[:, t], in_values=logits[:, t])

            @block.tensor
            def _(pe):
                def gate(c):
                    pe.wait_ge(ao_ready, c + 1)
                    for t in range(CT):
                        for half in range(HALVES):
                            last = nc.tensor.transpose(tps[:, half, t * P:(t + 1) * P], ao[:, t, half * P:(half + 1) * P],
                                                       ident[:])
                    last.then_inc(outT_psum, 1)
                    pe.wait_ge(outT_ready, c + 1)
                    pe.wait_ge(th_ready, 2 * c)
                    for half in range(HALVES):
                        for k in range(HALVES):
                            last = nc.tensor.matmul(gps[:, half], wg[:, k, half * P:(half + 1) * P], outT[:, k],
                                                    start=(k == 0), stop=(k == HALVES - 1))
                    last.then_inc(gate_psum, 1)

                def project(c):
                    pe.wait_ge(og_ready, c + 1)
                    pe.wait_ge(y_ready, 2 * c)
                    for bank in range(2):
                        for t in (2 * bank, 2 * bank + 1):
                            for k in range(HALVES):
                                last = nc.tensor.matmul(yps[:, bank, (t % 2) * D:(t % 2 + 1) * D],
                                                        ogT[:, k, t * P:(t + 1) * P], wo[:, k],
                                                        start=(k == 0), stop=(k == HALVES - 1))
                        last.then_inc(y_psum, 1)

                def route(c):
                    pe.wait_ge(xr_ready, c + 1)
                    pe.wait_ge(xrT_ready, c)
                    for t in range(CT):
                        for half in range(HALVES):
                            last = nc.tensor.transpose(xps[:, half, t * P:(t + 1) * P], xr[:, t, half * P:(half + 1) * P],
                                                       ident[:])
                    last.then_inc(xrT_psum, 1)
                    pe.wait_ge(xrT_ready, c + 1)
                    for t in range(CT):
                        for k in range(HALVES):
                            last = nc.tensor.matmul(tps[:, 0, t * E8:(t + 1) * E8], xrT[:, k, t * P:(t + 1) * P], wr[:, k],
                                                    start=(k == 0), stop=(k == HALVES - 1))
                    last.then_inc(lg_psum, 1)

                def first(c):
                    gate(c)
                    project(c)

                def body(c, last):
                    if not last:
                        pe.wait_ge(lg_ready, c)
                        gate(c + 1)
                    route(c)
                    if not last:
                        project(c + 1)

                pe.wait_ge(loaded, 16 * 7)
                chunks(pe, first, body)


def make_prefix(nc, kit, tri, ones):
    return dict(pre=kit.ps("prefix", [P, TILES * E8]), tot=kit.ps("totals", [P, TILES * E8]),
                tot_sb=kit.sb("tot_sb", [P, TILES, E8]), incl=kit.sb("incl", [P, TILES, E8]),
                one=kit.sb("one", [P, TILES]), tri=tri, ones=ones)


def prefix_products(nc, pe, pf, marks, done):
    nc.tensor.matmul(pf["pre"][:], pf["tri"][:], marks[:].rearrange("p t e -> p (t e)"), start=True, stop=True)
    nc.tensor.matmul(pf["tot"][:], pf["ones"][:], marks[:].rearrange("p t e -> p (t e)"), start=True,
                     stop=True).then_inc(done, 1)


def route_tokens(nc, w, src_sb, logits, top, topi, tri, ones, wsum, slot_i, tile_expert, gathered_in):
    with ExitStack() as ctx:
        kit = Kit(nc, ctx, "rt_")
        sb, sem = kit.sb, kit.sem
        turnstile = sem("turnstile")
        pf = make_prefix(nc, kit, tri, ones)
        chosen = sb("chosen", [P, TILES])
        iota8 = sb("iota8", [P, E8])
        mark, markb = sb("mark", [P, TILES, E8]), sb("markb", [P, TILES, E8], bf16)
        rank = sb("rank", [P, TILES, E8])
        count_i, tiles, end, start = sb("count_i", [P, E8], i32), sb("tiles", [P, E8]), sb("end", [P, E8]), sb("start", [P, E8])
        delta, total = sb("delta", [P, TILES]), sb("total", [P, TILES])
        slot = sb("slot", [P, TILES])
        iotam = sb("iotam", [1, MT])
        past = sb("past", [1, MT, E8])
        texp = sb("texp", [1, MT])
        iota_made, step, marks_ready, products = sem("iota_made"), sem("step"), sem("marks_ready"), sem("products")
        delta_ready, exp_ready, slots_ready, scattered = sem("delta_ready"), sem("exp_ready"), sem("slots_ready"), sem("scattered")

        with nc.Block() as block:
            @block.gpsimd
            def _(pool):
                nc.gpsimd.iota(iota8[:], [[1, E8]], base=0, channel_multiplier=0,
                               allow_small_or_imprecise_dtypes=True).then_inc(iota_made, 1)
                pool.wait_ge(iota_made, 1)
                nc.gpsimd.iota(iotam[:], [[1, MT]], base=0, channel_multiplier=0,
                               allow_small_or_imprecise_dtypes=True).then_inc(iota_made, 1)
                pool.wait_ge(slots_ready, 1)
                for t in range(TILES):
                    pool.indirect_dma_start(out=gathered_in, out_offset=bass.IndirectOffsetOnAxis(ap=slot_i[:, t:t + 1], axis=0),
                                            in_=src_sb[:, t, :], in_offset=None).then_inc(scattered, 16)
                pool.wait_ge(scattered, 16 * TILES)

            @block.scalar
            def _(act):
                act.wait_ge(delta_ready, 1)
                nc.scalar.activation(delta[:], delta[:], ACT.Exp).then_inc(exp_ready, 1)

            @block.tensor
            def _(pe):
                pe.wait_ge(marks_ready, 1)
                prefix_products(nc, pe, pf, markb, products)

            @block.vector
            def _(dve):
                at = [0]

                def link(instruction):
                    at[0] += 1
                    instruction.then_inc(step, 1)
                    dve.wait_ge(step, at[0])

                nc.vector.tensor_tensor(delta[:], top[:, :, 1], top[:, :, 0], ALU.subtract).then_inc(delta_ready, 1)
                link(nc.vector.tensor_tensor(chosen[:], topi[:, :, 0], topi[:, :, 1], ALU.max))
                dve.wait_ge(iota_made, 2)
                link(nc.vector.tensor_tensor(mark[:], bc(chosen[:], 2, [P, TILES, E8]), bc(iota8[:], 1, [P, TILES, E8]),
                                             ALU.is_equal))
                nc.vector.tensor_copy(markb[:], mark[:]).then_inc(marks_ready, 1)
                link(nc.vector.memset(pf["one"][:], 1.0))
                dve.wait_ge(products, 1)
                link(nc.vector.tensor_copy(pf["tot_sb"][:], pf["tot"][:].rearrange("p (t e) -> p t e", e=E8)))
                for e in range(E8):
                    last = nc.vector.tensor_tensor_scan(pf["incl"][:, :, e], pf["one"][:], pf["tot_sb"][:, :, e], 0.0,
                                                        ALU.mult, ALU.add)
                    link(last)
                link(nc.vector.tensor_tensor(rank[:], pf["pre"][:].rearrange("p (t e) -> p t e", e=E8), pf["incl"][:], ALU.add))
                link(nc.vector.tensor_tensor(rank[:], rank[:], pf["tot_sb"][:], ALU.subtract))
                link(nc.vector.tensor_scalar(count_i[:], pf["incl"][:, TILES - 1], float(P - 1), None, ALU.add))
                link(nc.vector.tensor_scalar(count_i[:], count_i[:], 7, None, ALU.arith_shift_right))
                link(nc.vector.tensor_copy(tiles[:], count_i[:]))
                link(nc.vector.tensor_tensor_scan(end[:], pf["one"][:, 0:E8], tiles[:], 0.0, ALU.mult, ALU.add))
                link(nc.vector.tensor_tensor(start[:], end[:], tiles[:], ALU.subtract))
                link(nc.vector.tensor_scalar(start[:], start[:], float(P), None, ALU.mult))
                link(nc.vector.tensor_tensor(rank[:], rank[:], bc(start[:], 1, [P, TILES, E8]), ALU.add))
                link(nc.vector.tensor_tensor(rank[:], rank[:], mark[:], ALU.mult))
                link(nc.vector.tensor_reduce(slot[:], rank[:], axis=X, op=ALU.add))
                nc.vector.tensor_copy(slot_i[:], slot[:]).then_inc(slots_ready, 1)
                link(nc.vector.tensor_tensor(past[:], bc(iotam[:], 2, [1, MT, E8]), bc(end[0:1, :], 1, [1, MT, E8]), ALU.is_ge))
                link(nc.vector.tensor_reduce(texp[:], past[:], axis=X, op=ALU.add))
                link(nc.vector.tensor_scalar(tile_expert[:], texp[:], float(E8 - 1), None, ALU.min))
                dve.wait_ge(exp_ready, 1)
                link(nc.vector.tensor_scalar(total[:], delta[:], 1.0, None, ALU.add))
                link(nc.vector.reciprocal(total[:], total[:]))
                link(nc.vector.tensor_tensor(delta[:], delta[:], total[:], ALU.mult))
                link(nc.vector.tensor_tensor(wsum[:], delta[:], total[:], ALU.add))


def expert_tiles(nc, ident, eps_pow, w, ew, spent, tile_expert, gathered_in, gathered_out):
    U = 4
    with ExitStack() as ctx:
        kit = Kit(nc, ctx, "ex_")
        sb, ps, sem = kit.sb, kit.ps, kit.sem
        turnstile = sem("turnstile")
        xg = [b[:].rearrange("p t e -> p (t e)") for b in spent] + [sb(f"xg{i}", [P, D]) for i in range(len(spent), U)]
        xb = [sb(f"xb{i}", [P, D]) for i in range(2)]
        xT = [sb(f"xT{i}", [P, HALVES, P]) for i in range(2)]
        hb = [sb(f"hb{i}", [P, F1]) for i in range(U)]
        stats, mv = sb("stats", [P, 2, 6]), sb("mv", [P, 2, 2])
        var, rstd = sb("var", [P, 2]), sb("rstd", [P, 2])
        hT = [sb(f"hT{i}", [P, FK, P]) for i in range(2)]
        xps = [ps(f"xps{i}", [P, F1]) for i in range(2)]
        hps = [ps(f"hps{i}", [P, F1]) for i in range(2)]
        tps = [ps(f"tps{i}", [P, F1]) for i in range(2)]
        yps = [ps(f"yps{i}", [P, F1]) for i in range(2)]
        x_loaded = [sem(f"x_loaded{i}") for i in range(U)]
        y_stored = [sem(f"y_stored{i}") for i in range(2)]
        xT_psum, xT_ready, h_psum, hb_ready, stats_done, ln_stats = (sem("xT_psum"), sem("xT_ready"), sem("h_psum"),
                                                                     sem("hb_ready"), sem("stats_done"), sem("ln_stats"))
        var_done, rstd_ready, hn_ready, hg_ready, hgb_ready, gelu_ready = (
            sem("var_done"), sem("rstd_ready"), sem("hn_ready"), sem("hg_ready"), sem("hgb_ready"), sem("gelu_ready"))
        hT_psum, hT_ready, y_psum, xb_ready, y_ready = (sem("hT_psum"), sem("hT_ready"), sem("y_psum"), sem("xb_ready"),
                                                        sem("y_ready"))

        def turns(eng, body):
            with eng.Fori(0, MT // U - 1) as i:
                for j in range(U):
                    body(i * U + j, i, j, True)
            for j in range(U):
                body(MT - U + j, MT // U - 1, j, j + 2 < U)

        def expert(eng, k):
            return eng.value_load(tile_expert[0:1, ds(k, 1)], min_val=0, max_val=E8 - 1)

        with nc.Block() as block:
            @block.sync
            def _(sp):
                def load(k, turn, j):
                    sp.dma_start(xg[j][:], gathered_in[ds(P * k, P), :]).then_inc(x_loaded[j], 16)

                def body(k, turn, j, ahead):
                    if ahead:
                        k2 = k + 2
                        sp.wait_ge(xb_ready, k + 1)
                        load(k2, turn, (j + 2) % U)
                    sp.wait_ge(y_ready, k + 3)
                    sp.dma_start(gathered_out[ds(P * k, P), :], xb[j % 2][:]).then_inc(y_stored[j % 2], 16)

                load(0, 0, 0)
                load(1, 0, 1)
                turns(sp, body)
                for i in range(2):
                    sp.wait_ge(y_stored[i], 16 * (MT // 2))

            @block.tensor
            def _(pe):
                def hidden(k, turn, j):
                    pe.wait_ge(x_loaded[j], 16 * (turn + 1))
                    if later(k, 1):
                        pe.wait_ge(xT_ready, k - 1)
                    for half in range(HALVES):
                        last = nc.tensor.transpose(xps[j % 2][:, half * P:(half + 1) * P], xg[j][:, half * P:(half + 1) * P],
                                                   ident[:])
                    last.then_inc(xT_psum, 1)
                    e = expert(pe, k)
                    pe.wait_ge(xT_ready, k + 1)
                    if later(k, 2):
                        pe.wait_ge(hb_ready, k - 1)
                    for half in range(HALVES):
                        last = nc.tensor.matmul(hps[j % 2][:], xT[j % 2][:, half], ew["w1"][:, half, ds(e, 1), :],
                                                start=(half == 0), stop=(half == HALVES - 1))
                    last.then_inc(h_psum, 1)

                def body(k, turn, j, ahead):
                    if ahead:
                        hidden(k + 2, turn + (j + 2) // U, (j + 2) % U)
                    pe.wait_ge(gelu_ready, k + 1)
                    for f in range(FK):
                        last = nc.tensor.transpose(tps[j % 2][:, f * P:(f + 1) * P], hb[j][:, f * P:(f + 1) * P], ident[:])
                    last.then_inc(hT_psum, 1)
                    e = expert(pe, k)
                    pe.wait_ge(hT_ready, k + 1)
                    pe.wait_ge(y_ready, k + 1)
                    for f in range(FK):
                        last = nc.tensor.matmul(yps[j % 2][:, 0:D], hT[j % 2][:, f], ew["w2"][:, f, ds(e, 1), :],
                                                start=(f == 0), stop=(f == FK - 1))
                    last.then_inc(y_psum, 1)

                pe.wait_ge(ew["w_loaded"], ew["w_count"])
                hidden(0, 0, 0)
                hidden(1, 0, 1)
                turns(pe, body)

            @block.scalar
            def _(act):
                def evacuate_xT(k, j):
                    act.wait_ge(xT_psum, k + 1)
                    if later(k, 2):
                        act.wait_ge(h_psum, k - 1)
                    nc.scalar.activation(xT[j % 2][:].rearrange("p k t -> p (k t)"), xps[j % 2][:, 0:D],
                                         ACT.Copy).then_inc(xT_ready, 1)

                def gelu(k, j):
                    act.wait_ge(hgb_ready, k + 1)
                    nc.scalar.activation(hb[j][:], hb[j][:], ACT.Gelu).then_inc(gelu_ready, 1)

                def body(k, turn, j, ahead):
                    if ahead:
                        evacuate_xT(k + 2, (j + 2) % U)
                    gelu(k, j)
                    act.wait_ge(hT_psum, k + 1)
                    act.wait_ge(y_psum, k)
                    nc.scalar.activation(hT[j % 2][:].rearrange("p f t -> p (f t)"), tps[j % 2][:],
                                         ACT.Copy).then_inc(hT_ready, 1)

                evacuate_xT(0, 0)
                evacuate_xT(1, 1)
                turns(act, body)

            @block.vector
            def _(dve):
                def normalize_hidden(k, j):
                    e = expert(dve, k)
                    dve.wait_ge(h_psum, k + 1)
                    nc.vector.tensor_tensor(hb[j][:], hps[j % 2][:], ew["b1"][:, ds(e, 1), :].rearrange("p o f -> p (o f)"),
                                            ALU.add).then_inc(hb_ready, 1)
                    dve.wait_ge(hb_ready, k + 1)
                    nc.vector.bn_stats(stats[:, j % 2], hb[j][:]).then_inc(stats_done, 1)
                    passed(dve, stats_done, k + 1, turnstile)
                    nc.vector.bn_aggr(mv[:, j % 2], stats[:, j % 2]).then_inc(ln_stats, 1)

                def apply_norm(k, j):
                    dve.wait_ge(rstd_ready, k + 1)
                    nc.vector.tensor_scalar(hb[j][:], hb[j][:], mv[:, j % 2, 0:1], rstd[:, j % 2:j % 2 + 1], ALU.subtract,
                                            ALU.mult).then_inc(hn_ready, 1)

                def finish(k, turn, j):
                    e = expert(dve, k)
                    dve.wait_ge(y_psum, k + 1)
                    dve.wait_ge(xb_ready, k + 3)
                    nc.vector.scalar_tensor_tensor(out=xb[j % 2][:], in0=yps[j % 2][:, 0:D], scalar=ew["rs"][:, ds(e, 1)],
                                                   in1=xb[j % 2][:], op0=ALU.mult, op1=ALU.add).then_inc(y_ready, 1)

                def body(k, turn, j, ahead):
                    if ahead:
                        normalize_hidden(k + 2, (j + 2) % U)
                        apply_norm(k + 2, (j + 2) % U)
                    finish(k, turn, j)

                nc.vector.tensor_tensor(ew["b2"][:], ew["b2"][:], bc(ew["rs"][:], 2, [P, E8, D]), ALU.mult).then_inc(ew["b2_scaled"], 1)
                dve.wait_ge(ew["b2_scaled"], 1)
                nc.vector.memset(var[:], 0.0).then_inc(xb_ready, 2)
                nc.vector.memset(rstd[:], 0.0).then_inc(y_ready, 2)
                for k in range(2):
                    normalize_hidden(k, k)
                    apply_norm(k, k)
                turns(dve, body)

            @block.gpsimd
            def _(pool):
                def make_rstd(k, j):
                    par = slice(j % 2, j % 2 + 1)
                    pool.wait_ge(ln_stats, k + 1)
                    nc.gpsimd.tensor_tensor(var[:, par], mv[:, j % 2, 1:2], eps_pow[:, 0, 0:1], ALU.add).then_inc(var_done, 1)
                    pool.wait_ge(var_done, k + 1)
                    nc.gpsimd.tensor_tensor(rstd[:, par], var[:, par], eps_pow[:, 1, 0:1], ALU.pow).then_inc(rstd_ready, 1)

                def affine(k, j):
                    e = expert(pool, k)
                    pool.wait_ge(hn_ready, k + 1)
                    nc.gpsimd.tensor_tensor(hb[j][:], hb[j][:], ew["g"][:, ds(e, 1), :].rearrange("p o f -> p (o f)"),
                                            ALU.mult).then_inc(hg_ready, 1)
                    pool.wait_ge(hg_ready, k + 1)
                    nc.gpsimd.tensor_tensor(hb[j][:], hb[j][:], ew["bt"][:, ds(e, 1), :].rearrange("p o f -> p (o f)"),
                                            ALU.add).then_inc(hgb_ready, 1)

                def body(k, turn, j, ahead):
                    if ahead:
                        make_rstd(k + 2, (j + 2) % U)
                    e = expert(pool, k)
                    pool.wait_ge(x_loaded[j], 16 * (turn + 1))
                    pool.wait_ge(y_stored[j % 2], 16 * (2 * turn + j // 2))
                    nc.gpsimd.tensor_tensor(xb[j % 2][:], xg[j][:], ew["b2"][:, ds(e, 1), :].rearrange("p o f -> p (o f)"),
                                            ALU.add).then_inc(xb_ready, 1)
                    if ahead:
                        affine(k + 2, (j + 2) % U)

                pool.wait_ge(ew["b2_scaled"], 1)
                pool.wait_ge(y_ready, 2)
                pool.wait_ge(xb_ready, 2)
                for k in range(2):
                    make_rstd(k, k)
                    affine(k, k)
                turns(pool, body)


def combine_experts(nc, x_sb, src_sb, eps_pow, w, wsum, slot_i, gathered_out):
    with ExitStack() as ctx:
        kit = Kit(nc, ctx, "co_")
        sb, sem = kit.sb, kit.sem
        turnstile = sem("turnstile")
        n2g, n2b = sb("n2g", [P, D]), sb("n2b", [P, D])
        yg = [sb(f"yg{i}", [P, CT, D]) for i in range(2)]
        z = sb("z", [P, CT, D])
        stats, mv = sb("stats", [P, CT, 6]), sb("mv", [P, CT, 2])
        var, rstd = sb("var", [P, CT]), sb("rstd", [P, CT])
        loaded, z_ready, stats_done, ln_stats = sem("loaded"), sem("z_ready"), sem("stats_done"), sem("ln_stats")
        gathered = [sem(f"gathered{i}") for i in range(2)]
        var_done, rstd_ready, zn_ready, zg_ready, x_biased, x_done = (sem("var_done"), sem("rstd_ready"), sem("zn_ready"),
                                                                      sem("zg_ready"), sem("x_biased"), sem("x_done"))
        with nc.Block() as block:
            @block.sync
            def _(sp):
                sp.dma_start(n2g[:], w["n2_g"].partition_broadcast(P)).then_inc(loaded, 16)
                sp.dma_start(n2b[:], w["n2_b"].partition_broadcast(P)).then_inc(loaded, 16)

            @block.gpsimd
            def _(pool):
                def gather(c, par):
                    if later(c, 2):
                        pool.wait_ge(z_ready, CT * (c - 1))
                    for t in range(CT):
                        pool.indirect_dma_start(out=yg[par][:, t, :], out_offset=None, in_=gathered_out,
                                                in_offset=bass.IndirectOffsetOnAxis(ap=slot_i[:, CT * c + t:CT * c + t + 1],
                                                                                    axis=0)).then_inc(gathered[par], 16)

                pool.wait_ge(loaded, 32)
                gather(0, 0)
                for c in range(CHUNKS):
                    if c + 1 < CHUNKS:
                        gather(c + 1, (c + 1) % 2)
                    nc.gpsimd.tensor_tensor(x_sb[:, CT * c:CT * (c + 1), :], x_sb[:, CT * c:CT * (c + 1), :],
                                            bc(n2b[:], 1, [P, CT, D]), ALU.add).then_inc(x_biased, 1)
                    pool.wait_ge(ln_stats, CT * (c + 1))
                    nc.gpsimd.tensor_tensor(var[:], mv[:, :, 1], eps_pow[:, 0], ALU.add).then_inc(var_done, 1)
                    pool.wait_ge(var_done, c + 1)
                    nc.gpsimd.tensor_tensor(rstd[:], var[:], eps_pow[:, 1], ALU.pow).then_inc(rstd_ready, 1)
                    pool.wait_ge(zn_ready, CT * (c + 1))
                    nc.gpsimd.tensor_tensor(z[:], z[:], bc(n2g[:], 1, [P, CT, D]), ALU.mult).then_inc(zg_ready, 1)

            @block.vector
            def _(dve):
                for c in range(CHUNKS):
                    dve.wait_ge(gathered[c % 2], 16 * CT * (c // 2 + 1))
                    if c:
                        dve.wait_ge(x_done, c)
                    for t in range(CT):
                        nc.vector.scalar_tensor_tensor(out=z[:, t], in0=yg[c % 2][:, t], scalar=wsum[:, CT * c + t:CT * c + t + 1],
                                                       in1=src_sb[:, CT * c + t], op0=ALU.mult, op1=ALU.add).then_inc(z_ready, 1)
                    for t in range(CT):
                        dve.wait_ge(z_ready, CT * c + t + 1)
                        nc.vector.bn_stats(stats[:, t], z[:, t]).then_inc(stats_done, 1)
                    passed(dve, stats_done, CT * (c + 1), turnstile)
                    for t in range(CT):
                        nc.vector.bn_aggr(mv[:, t], stats[:, t]).then_inc(ln_stats, 1)
                    dve.wait_ge(rstd_ready, c + 1)
                    dve.wait_ge(ln_stats, CT * (c + 1))
                    for t in range(CT):
                        nc.vector.tensor_scalar(z[:, t], z[:, t], mv[:, t, 0:1], rstd[:, t:t + 1], ALU.subtract,
                                                ALU.mult).then_inc(zn_ready, 1)
                    dve.wait_ge(zg_ready, c + 1)
                    dve.wait_ge(x_biased, c + 1)
                    nc.vector.tensor_tensor(x_sb[:, CT * c:CT * (c + 1), :], x_sb[:, CT * c:CT * (c + 1), :], z[:],
                                            ALU.add).then_inc(x_done, 1)


def make_constants(nc, kit):
    sb, made = kit.sb, kit.sem("constants_made")
    k = dict(ident=sb("ident", [P, P]), eps_pow=sb("eps_pow", [P, 2, CT]), headmask=sb("headmask", [P, HH]),
             trif=sb("trif", [P, P]), tri=sb("tri", [P, P], bf16), ones=sb("ones", [P, P], bf16))

    with nc.Block() as block:
        @block.gpsimd
        def _(pool):
            steps = [0]

            def link(instruction):
                steps[0] += 1
                instruction.then_inc(made, 1)
                pool.wait_ge(made, steps[0])

            link(nc.gpsimd.memset(k["eps_pow"][:, 0], EPS))
            link(nc.gpsimd.memset(k["eps_pow"][:, 1], -0.5))
            link(nc.gpsimd.memset(k["ident"][:], 0.0))
            link(nc.gpsimd.affine_select(out=k["ident"][:], in_=k["ident"][:], compare_op=ALU.not_equal, fill=1.0, base=0,
                                         pattern=[[-1, P]], channel_multiplier=1))
            link(nc.gpsimd.memset(k["headmask"][:], 1.0))
            link(nc.gpsimd.affine_select(out=k["headmask"][:], in_=k["headmask"][:], compare_op=ALU.is_ge, fill=0.0, base=0,
                                         pattern=[[-DK, HH]], channel_multiplier=1))
            link(nc.gpsimd.affine_select(out=k["headmask"][:], in_=k["headmask"][:], compare_op=ALU.is_ge, fill=0.0,
                                         base=DK - 1, pattern=[[DK, HH]], channel_multiplier=-1))
            link(nc.gpsimd.memset(k["trif"][:], 1.0))
            link(nc.gpsimd.affine_select(out=k["trif"][:], in_=k["trif"][:], compare_op=ALU.is_gt, fill=0.0, base=0,
                                         pattern=[[1, P]], channel_multiplier=-1))
            link(nc.gpsimd.tensor_copy(k["tri"][:], k["trif"][:]))
            link(nc.gpsimd.memset(k["ones"][:], 1.0))
    return k


def load_x(nc, kit, x_sb, x):
    loaded = kit.sem("x_loaded")
    with nc.Block() as block:
        @block.sync
        def _(sp):
            sp.dma_start(x_sb[:], x.rearrange("(t p) d -> p t d", p=P)).then_inc(loaded, 16)
            sp.wait_ge(loaded, 16)


def self_attention_moe(nc, kit, x_sb, k, w):
    q_parts = nc.dram_tensor("q_parts", (GROUPS, GH, KROWS, S), bf16, kind="Internal").ap()
    k_parts = nc.dram_tensor("k_parts", (GROUPS, GH, KROWS, S), bf16, kind="Internal").ap()
    v_dram = nc.dram_tensor("v_groups", (GROUPS, P, KT, GH * VW), fp32, kind="Internal").ap()
    m_dram = nc.dram_tensor("neg_maxima", (UNITS, MROWS, GH * CT, P), bf16, kind="Internal").ap()
    gathered_in = nc.dram_tensor("expert_in", (MT * P, D), fp32, kind="Internal").ap()
    gathered_out = nc.dram_tensor("expert_out", (MT * P, D), fp32, kind="Internal").ap()
    ident, eps_pow = k["ident"], k["eps_pow"]
    w = dict(w, headmask=k["headmask"])
    with ExitStack() as ctx:
        own = Kit(nc, ctx, "sm_")
        src_sb = own.sb("src", [P, TILES, D])
        self_projections(nc, x_sb, src_sb, ident, eps_pow, w, q_parts, k_parts, v_dram)
        wsum, slot_i = own.sb("wsum", [P, TILES]), own.sb("slot_i", [P, TILES], i32)
        tile_expert = own.sb("tile_expert", [1, MT], i32)
        logits, top = own.sb("logits", [P, TILES, E8]), own.sb("top", [P, TILES, E8])
        topi = own.sb("topi", [P, TILES, E8], u32)
        with ExitStack() as ctx2:
            attn = Kit(nc, ctx2, "at_").sb("attn", [P, UNITS + 1, CT * GH * DK])
            self_attention(nc, attn, ident, q_parts, k_parts, v_dram, m_dram)
            attention_out(nc, src_sb, attn, ident, eps_pow, w, logits, top, topi, gathered_in)
        with ExitStack() as ctx2:
            ek = Kit(nc, ctx2, "ew_")
            ew = dict(w1=ek.sb("w1", [P, HALVES, E8, F1]), w2=ek.sb("w2", [P, FK, E8, D]), b1=ek.sb("b1", [P, E8, F1]),
                      g=ek.sb("g", [P, E8, F1]), bt=ek.sb("bt", [P, E8, F1]), b2=ek.sb("b2", [P, E8, D]),
                      rs=ek.sb("rs", [P, E8]), b2_scaled=ek.sem("b2_scaled"), w_loaded=ek.sem("w_loaded"))
            with nc.Block() as block:
                @block.sync
                def _(sp):
                    ew["w_count"] = 0

                    def load(dst, src):
                        sp.dma_start(dst, src).then_inc(ew["w_loaded"], 16)
                        ew["w_count"] += 16

                    for half in range(HALVES):
                        load(ew["w1"][:, half], w["w1"][:, half * P:(half + 1) * P, :].rearrange("e p f -> p e f"))
                    for f in range(FK):
                        load(ew["w2"][:, f], w["w2"][:, f * P:(f + 1) * P, :].rearrange("e p d -> p e d"))
                    for dst, name in (("b1", "b1"), ("g", "ln_g"), ("bt", "ln_b"), ("b2", "b2")):
                        load(ew[dst][:].rearrange("p e f -> p (e f)"), w[name].partition_broadcast(P))
                    load(ew["rs"][:], w["res_scale"].partition_broadcast(P))
                    sp.wait_ge(ew["w_loaded"], ew["w_count"])
            route_tokens(nc, w, src_sb, logits, top, topi, k["tri"], k["ones"], wsum, slot_i, tile_expert, gathered_in)
            expert_tiles(nc, ident, eps_pow, w, ew, (logits, top), tile_expert, gathered_in, gathered_out)
        combine_experts(nc, x_sb, src_sb, eps_pow, w, wsum, slot_i, gathered_out)

CAP = TOKENS // E8
CAPT = CAP // P
NV = 5


def token_scores(nc, x_sb, ident, eps_pow, w, sc, xn_dram, out):
    with ExitStack() as ctx:
        kit = Kit(nc, ctx, "ts_")
        sb, ps, sem = kit.sb, kit.ps, kit.sem
        turnstile = sem("turnstile")
        wg = sb("wg", [P, HALVES, E8])
        stats, mv = sb("stats", [P, CT, 6]), sb("mv", [P, CT, 2])
        var, rstd = sb("var", [P, CT]), sb("rstd", [P, CT])
        xn = [sb(f"xn{i}", [P, CT, D]) for i in range(2)]
        xnT = [sb(f"xnT{i}", [P, HALVES, CW]) for i in range(2)]
        tps = [ps(f"tps{i}", [P, HALVES, CW]) for i in range(2)]
        sps = [ps(f"sps{i}", [P, CW]) for i in range(2)]
        loaded, x_stored = sem("loaded"), sem("x_stored")
        xn_stored = [sem(f"xn_stored{i}") for i in range(2)]
        stats_done, ln_stats, var_done, rstd_ready = sem("stats_done"), sem("ln_stats"), sem("var_done"), sem("rstd_ready")
        xn_ready, xnT_psum, xnT_ready, s_psum, s_ready = (sem("xn_ready"), sem("xnT_psum"), sem("xnT_ready"), sem("s_psum"),
                                                          sem("s_ready"))

        def turns(eng, body):
            with eng.Fori(0, CHUNKS // 2) as i:
                for par in range(2):
                    body(i, par, 2 * i + par)

        with nc.Block() as block:
            @block.sync
            def _(sp):
                sp.dma_start(wg[:], w["Wg"].rearrange("(k p) e -> p k e", p=P)).then_inc(loaded, 16)
                sp.dma_start(out.rearrange("(t p) d -> p t d", p=P), x_sb[:]).then_inc(x_stored, 16)
                xv = xn_dram.rearrange("(t p) d -> p t d", p=P)

                def body(i, par, c):
                    sp.wait_ge(xn_ready, CT * (c + 1))
                    sp.dma_start(xv[:, ds(CT * c, CT), :], xn[par][:]).then_inc(xn_stored[par], 16)

                turns(sp, body)
                sp.wait_ge(x_stored, 16)
                for par in range(2):
                    sp.wait_ge(xn_stored[par], 16 * (CHUNKS // 2))

            @block.vector
            def _(dve):
                def moments(c):
                    for t in range(CT):
                        nc.vector.bn_stats(stats[:, t], x_sb[:, ds(CT * c + t, 1), :]).then_inc(stats_done, 1)
                    passed(dve, stats_done, CT * (c + 1), turnstile)
                    for t in range(CT):
                        nc.vector.bn_aggr(mv[:, t], stats[:, t]).then_inc(ln_stats, 1)

                def body(i, par, c):
                    moments(c)
                    dve.wait_ge(rstd_ready, c + 1)
                    dve.wait_ge(ln_stats, CT * (c + 1))
                    dve.wait_ge(xn_stored[par], 16 * i)
                    dve.wait_ge(xnT_psum, c)
                    for t in range(CT):
                        nc.vector.tensor_scalar(xn[par][:, t], x_sb[:, ds(CT * c + t, 1), :], mv[:, t, 0:1], rstd[:, t:t + 1],
                                                ALU.subtract, ALU.mult).then_inc(xn_ready, 1)

                turns(dve, body)

            @block.gpsimd
            def _(pool):
                def body(i, par, c):
                    pool.wait_ge(ln_stats, CT * (c + 1))
                    nc.gpsimd.tensor_tensor(var[:], mv[:, :, 1], eps_pow[:, 0], ALU.add).then_inc(var_done, 1)
                    pool.wait_ge(var_done, c + 1)
                    nc.gpsimd.tensor_tensor(rstd[:], var[:], eps_pow[:, 1], ALU.pow).then_inc(rstd_ready, 1)

                turns(pool, body)

            @block.scalar
            def _(act):
                def body(i, par, c):
                    act.wait_ge(xnT_psum, c + 1)
                    nc.scalar.activation(xnT[par][:], tps[par][:], ACT.Copy).then_inc(xnT_ready, 1)
                    act.wait_ge(s_psum, c + 1)
                    nc.scalar.activation(sc[:, ds(CT * c, CT), :], sps[par][:, 0:CT * E8].rearrange("p (t e) -> p t e", t=CT),
                                         ACT.Copy).then_inc(s_ready, 1)

                turns(act, body)

            @block.tensor
            def _(pe):
                def body(i, par, c):
                    pe.wait_ge(xn_ready, CT * (c + 1))
                    for t in range(CT):
                        for half in range(HALVES):
                            last = nc.tensor.transpose(tps[par][:, half, t * P:(t + 1) * P],
                                                       xn[par][:, t, half * P:(half + 1) * P], ident[:])
                    last.then_inc(xnT_psum, 1)
                    pe.wait_ge(xnT_ready, c + 1)
                    pe.wait_ge(s_ready, c)
                    for t in range(CT):
                        for k in range(HALVES):
                            last = nc.tensor.matmul(sps[par][:, t * E8:(t + 1) * E8], xnT[par][:, k, t * P:(t + 1) * P],
                                                    wg[:, k], start=(k == 0), stop=(k == HALVES - 1))
                    last.then_inc(s_psum, 1)

                pe.wait_ge(loaded, 16)
                turns(pe, body)


def choose_tokens(nc, k, sc, idx, wt):
    BITS = 31
    with ExitStack() as ctx:
        kit = Kit(nc, ctx, "ct_")
        sb, sem = kit.sb, kit.sem
        turnstile = sem("turnstile")
        pf = make_prefix(nc, kit, k["tri"], k["ones"])
        cps, ips, zps = kit.ps("cps", [P, TILES * E8]), kit.ps("ips", [P, E8, CAPT, NV]), kit.ps("zps", [P, E8])
        ge = sb("ge", [P, TILES, E8], bf16)
        cnt = sb("cnt", [P, E8])
        met, key, flip, thr = (sb(n, [P, E8], i32) for n in ("met", "key", "flip", "thr"))
        onei, shift, bits = sb("onei", [P, BITS], i32), sb("shift", [P, BITS], i32), sb("bits", [P, BITS], i32)
        gt, eq = sb("gt", [P, TILES, E8]), sb("eq", [P, TILES, E8])
        sel, selb = sb("sel", [P, TILES, E8]), sb("selb", [P, TILES, E8], bf16)
        need, rank = sb("need", [P, E8]), sb("rank", [P, TILES, E8])
        rowmax, best = sb("rowmax", [P, E8]), sb("best", [P, E8])
        ex, rowsum, rz = sb("ex", [P, TILES, E8]), sb("rowsum", [P, E8]), sb("rz", [P, E8])
        onesf = sb("onesf", [P, P])
        slot_i, low_i, high_i = (sb(n, [P, TILES, E8], i32) for n in ("slot_i", "low_i", "high_i"))
        low, high = sb("low", [P, TILES, E8]), sb("high", [P, TILES, E8])
        iota4 = sb("iota4", [P, CAPT])
        iota128f, iota128 = sb("iota128f", [P, P]), sb("iota128", [P, P], bf16)
        val = sb("val", [P, TILES, E8, NV])
        part = sb("part", [P, TILES, E8], bf16)
        rest = sb("rest", [P, TILES, E8])
        hot4 = sb("hot4", [P, TILES, E8, CAPT])
        rhs = sb("rhs", [P, TILES, E8, CAPT, NV], bf16)
        GT = 8
        hot = [sb(f"hot{i}", [P, GT, P], bf16) for i in range(2)]
        got = sb("got", [P, E8, CAPT, NV])
        idf = sb("idf", [P, E8, CAPT])
        step, made, ge_ready, c_psum = sem("step"), sem("made"), sem("ge_ready"), sem("c_psum")
        rowmax_ready, best_ready, centered, exp_ready, rowsum_ready, z_psum = (
            sem("rowmax_ready"), sem("best_ready"), sem("centered"), sem("exp_ready"), sem("rowsum_ready"), sem("z_psum"))
        eqb_ready, selb_ready, products = sem("eqb_ready"), sem("selb_ready"), sem("products")
        rhs_ready, hot_ready, hot_used = sem("rhs_ready"), sem("hot_ready"), sem("hot_used")
        view = lambda b: b[:].rearrange("p t e -> p (t e)")
        per_expert = lambda b: bc(b[:], 1, [P, TILES, E8])
        SIGN = -2 ** 31

        with nc.Block() as block:
            @block.gpsimd
            def _(pool):
                n = [0]

                def link(instruction):
                    n[0] += 1
                    instruction.then_inc(made, 1)
                    pool.wait_ge(made, n[0])

                link(nc.gpsimd.iota(shift[:], [[-1, BITS]], base=BITS - 1, channel_multiplier=0))
                link(nc.gpsimd.iota(iota128f[:], [[1, P]], base=0, channel_multiplier=0, allow_small_or_imprecise_dtypes=True))
                link(nc.gpsimd.iota(iota4[:], [[1, CAPT]], base=0, channel_multiplier=0, allow_small_or_imprecise_dtypes=True))
                link(nc.gpsimd.iota(val[:, :, :, 0], [[1, TILES], [0, E8]], base=0, channel_multiplier=0,
                                    allow_small_or_imprecise_dtypes=True))
                link(nc.gpsimd.iota(val[:, :, :, 1], [[0, TILES], [0, E8]], base=0, channel_multiplier=1,
                                    allow_small_or_imprecise_dtypes=True))
                link(nc.gpsimd.memset(onesf[:], 1.0))
                pool.wait_ge(rowmax_ready, 1)
                nc.gpsimd.partition_all_reduce(best[:], rowmax[:], P, bass.bass_isa.ReduceOp.max).then_inc(best_ready, 1)

            @block.scalar
            def _(act):
                act.wait_ge(centered, 1)
                nc.scalar.activation(ex[:], ex[:], ACT.Exp).then_inc(exp_ready, 1)

            @block.tensor
            def _(pe):
                def count(value):
                    pe.wait_ge(ge_ready, value)
                    nc.tensor.matmul(cps[:], k["ones"][:], view(ge), start=True, stop=True).then_inc(c_psum, 1)

                count(1)
                with pe.Fori(0, BITS) as i:
                    count(i + 2)
                count(BITS + 2)
                pe.wait_ge(eqb_ready, 1)
                prefix_products(nc, pe, pf, selb, products)
                pe.wait_ge(selb_ready, 1)
                prefix_products(nc, pe, pf, selb, products)
                pe.wait_ge(rowsum_ready, 1)
                nc.tensor.matmul(zps[:], onesf[:], rowsum[:], start=True, stop=True).then_inc(z_psum, 1)
                pe.wait_ge(rhs_ready, 2)
                for e in range(E8):
                    for t in range(TILES):
                        n = e * TILES + t
                        if t % GT == 0:
                            pe.wait_ge(hot_ready, GT * (n // GT + 1))
                        last = nc.tensor.matmul(ips[:, e].rearrange("p a v -> p (a v)"), hot[n // GT % 2][:, t % GT],
                                                rhs[:, t, e].rearrange("p a v -> p (a v)"), start=(t == 0),
                                                stop=(t == TILES - 1))
                        if t % GT == GT - 1:
                            last.then_inc(hot_used, 1)

            @block.vector
            def _(dve):
                n = [0]

                def link(instruction):
                    n[0] += 1
                    instruction.then_inc(step, 1)
                    dve.wait_ge(step, n[0])

                def counted(done):
                    dve.wait_ge(c_psum, done)
                    return nc.vector.tensor_reduce(cnt[:], cps[:].rearrange("p (t e) -> p e t", e=E8), axis=X, op=ALU.add)

                nc.vector.tensor_reduce(rowmax[:], sc[:].rearrange("p t e -> p e t"), axis=X, op=ALU.max).then_inc(rowmax_ready, 1)
                nc.vector.tensor_scalar(ge[:], sc[:], 0.0, None, ALU.is_ge).then_inc(ge_ready, 1)
                dve.wait_ge(made, 6)
                link(nc.vector.memset(onei[:], 1))
                link(nc.vector.tensor_tensor(bits[:], onei[:], shift[:], ALU.logical_shift_left))
                link(nc.vector.tensor_copy(iota128[:], iota128f[:]))
                link(nc.vector.memset(pf["one"][:], 1.0))
                link(counted(1))
                link(nc.vector.tensor_scalar(met[:], cnt[:], float(CAP), -1.0, ALU.is_ge, ALU.mult))
                link(nc.vector.tensor_scalar(key[:], met[:], SIGN, None, ALU.bitwise_and))
                link(nc.vector.tensor_scalar(flip[:], met[:], -1, SIGN, ALU.bitwise_xor, ALU.bitwise_or))
                base = n[0]
                LINKS = 4
                with dve.Fori(0, BITS) as i:
                    bit = bits[:, ds(i, 1)]
                    at = base + LINKS * i
                    nc.vector.scalar_tensor_tensor(out=thr[:], in0=key[:], scalar=bit, in1=flip[:], op0=ALU.bitwise_or,
                                                   op1=ALU.bitwise_xor).then_inc(step, 1)
                    dve.wait_ge(step, at + 1)
                    nc.vector.tensor_tensor(ge[:], sc[:], per_expert(thr[:].bitcast(fp32)), ALU.is_ge).then_inc(ge_ready, 1)
                    counted(i + 2).then_inc(step, 1)
                    dve.wait_ge(step, at + 2)
                    nc.vector.tensor_scalar(met[:], cnt[:], float(CAP), -1.0, ALU.is_ge, ALU.mult).then_inc(step, 1)
                    dve.wait_ge(step, at + 3)
                    nc.vector.scalar_tensor_tensor(out=key[:], in0=met[:], scalar=bit, in1=key[:], op0=ALU.bitwise_and,
                                                   op1=ALU.bitwise_or).then_inc(step, 1)
                    dve.wait_ge(step, at + 4)
                n[0] = base + LINKS * BITS
                link(nc.vector.tensor_tensor(thr[:], key[:], flip[:], ALU.bitwise_xor))
                thrf = per_expert(thr[:].bitcast(fp32))
                nc.vector.tensor_tensor(ge[:], sc[:], thrf, ALU.is_gt).then_inc(ge_ready, 1)
                link(nc.vector.tensor_tensor(gt[:], sc[:], thrf, ALU.is_gt))
                link(nc.vector.tensor_tensor(eq[:], sc[:], thrf, ALU.is_equal))
                nc.vector.tensor_copy(selb[:], eq[:]).then_inc(eqb_ready, 1)
                link(counted(BITS + 2))
                link(nc.vector.tensor_scalar(need[:], cnt[:], -1.0, float(CAP), ALU.mult, ALU.add))

                def ranks(done):
                    dve.wait_ge(products, done)
                    link(nc.vector.tensor_copy(view(pf["tot_sb"]), pf["tot"][:]))
                    for e in range(E8):
                        link(nc.vector.tensor_tensor_scan(pf["incl"][:, :, e], pf["one"][:], pf["tot_sb"][:, :, e], 0.0,
                                                          ALU.mult, ALU.add))
                    link(nc.vector.tensor_tensor(rank[:], pf["pre"][:].rearrange("p (t e) -> p t e", e=E8), pf["incl"][:],
                                                 ALU.add))
                    link(nc.vector.tensor_tensor(rank[:], rank[:], pf["tot_sb"][:], ALU.subtract))

                ranks(1)
                link(nc.vector.tensor_tensor(rank[:], rank[:], per_expert(need), ALU.is_lt))
                link(nc.vector.tensor_tensor(rank[:], rank[:], eq[:], ALU.mult))
                link(nc.vector.tensor_tensor(sel[:], rank[:], gt[:], ALU.add))
                nc.vector.tensor_copy(selb[:], sel[:]).then_inc(selb_ready, 1)
                dve.wait_ge(best_ready, 1)
                nc.vector.tensor_tensor(ex[:], sc[:], per_expert(best), ALU.subtract).then_inc(centered, 1)
                ranks(2)
                dve.wait_ge(exp_ready, 1)
                link(nc.vector.tensor_tensor(ex[:], ex[:], sel[:], ALU.mult))
                nc.vector.tensor_reduce(rowsum[:], ex[:].rearrange("p t e -> p e t"), axis=X, op=ALU.add).then_inc(rowsum_ready, 1)
                link(nc.vector.tensor_copy(slot_i[:], rank[:]))
                link(nc.vector.tensor_scalar(low_i[:], slot_i[:], P - 1, None, ALU.bitwise_and))
                link(nc.vector.tensor_scalar(high_i[:], slot_i[:], 7, None, ALU.arith_shift_right))
                link(nc.vector.tensor_copy(high[:], high_i[:]))
                link(nc.vector.tensor_scalar(low[:], low_i[:], 1.0, None, ALU.add))
                link(nc.vector.tensor_tensor(low[:], low[:], sel[:], ALU.mult))
                link(nc.vector.tensor_scalar(low[:], low[:], 1.0, None, ALU.subtract))
                dve.wait_ge(z_psum, 1)
                link(nc.vector.reciprocal(rz[:], zps[:]))
                link(nc.vector.tensor_tensor(rest[:], ex[:], per_expert(rz), ALU.mult))
                for i in range(3):
                    link(nc.vector.tensor_copy(part[:], rest[:]))
                    link(nc.vector.tensor_copy(val[:, :, :, 2 + i], part[:]))
                    link(nc.vector.tensor_tensor(rest[:], rest[:], part[:], ALU.subtract))
                link(nc.vector.tensor_tensor(hot4[:], bc(high[:], 3, [P, TILES, E8, CAPT]),
                                             iota4[:].unsqueeze(1).unsqueeze(1).broadcast_to([P, TILES, E8, CAPT]), ALU.is_equal))
                h4 = hot4[:].rearrange("p t e a -> p (t e) a")
                v5 = val[:].rearrange("p t e v -> p (t e) v")
                r5 = rhs[:].rearrange("p t e a v -> p (t e) a v")
                TE = TILES * E8
                for part_of in range(2):
                    rows = slice(part_of * TE // 2, (part_of + 1) * TE // 2)
                    nc.vector.tensor_tensor(r5[:, rows], bc(h4[:, rows], 3, [P, TE // 2, CAPT, NV]),
                                            bc(v5[:, rows], 2, [P, TE // 2, CAPT, NV]), ALU.mult).then_inc(rhs_ready, 1)
                for e in range(E8):
                    for t in range(TILES):
                        m = e * TILES + t
                        if t % GT == 0 and m // GT >= 2:
                            dve.wait_ge(hot_used, m // GT - 1)
                        nc.vector.tensor_scalar(hot[m // GT % 2][:, t % GT], iota128[:], low[:, t, e:e + 1], None,
                                                ALU.is_equal).then_inc(hot_ready, 1)
                dve.wait_ge(hot_used, E8 * TILES // GT)
                link(nc.vector.tensor_copy(got[:], ips[:]))
                link(nc.vector.scalar_tensor_tensor(out=idf[:], in0=got[:, :, :, 0], scalar=float(P), in1=got[:, :, :, 1],
                                                    op0=ALU.mult, op1=ALU.add))
                link(nc.vector.tensor_copy(idx[:], idf[:]))
                link(nc.vector.tensor_tensor(wt[:], got[:, :, :, 2], got[:, :, :, 3], ALU.add))
                link(nc.vector.tensor_tensor(wt[:], wt[:], got[:, :, :, 4], ALU.add))


def swiglu_experts(nc, ident, w, idx, wt, xn_dram, out):
    with ExitStack() as ctx:
        kit = Kit(nc, ctx, "sw_")
        sb, ps, sem = kit.sb, kit.ps, kit.sem
        turnstile = sem("turnstile")
        w1 = [sb(f"w1{i}", [P, HALVES, F1]) for i in range(2)]
        w3 = [sb(f"w3{i}", [P, HALVES, F1]) for i in range(2)]
        w2 = [sb(f"w2{i}", [P, FK, D]) for i in range(2)]
        ids = [sb(f"ids{i}", [P, CAPT], i32) for i in range(2)]
        xg = [sb(f"xg{i}", [P, CAPT, D]) for i in range(2)]
        xT = sb("xT", [P, HALVES, CAP])
        act1 = [sb(f"act1{i}", [P, CAP]) for i in range(2)]
        hT = sb("hT", [P, FK, CAP])
        yo = [sb(f"yo{i}", [P, CAPT, D]) for i in range(2)]
        tps, yps = ps("tps", [P, HALVES, CAP]), ps("yps", [P, 2, CAP])
        p1 = [ps(f"p1{i}", [P, CAP]) for i in range(2)]
        p3 = [ps(f"p3{i}", [P, CAP]) for i in range(2)]
        w_loaded = [sem(f"w_loaded{i}") for i in range(2)]
        gathered = [sem(f"gathered{i}") for i in range(2)]
        ids_ready, scattered = sem("ids_ready"), sem("scattered")
        xT_psum, xT_ready, h_psum, silu_ready, h_ready = (sem("xT_psum"), sem("xT_ready"), sem("h_psum"), sem("silu_ready"),
                                                          sem("h_ready"))
        y_psum, y_ready = sem("y_psum"), sem("y_ready")

        def experts(eng, body):
            with eng.Fori(0, E8 // 2 - 1) as i:
                for par in range(2):
                    body(2 * i + par, i, par, False)
            for par in range(2):
                body(E8 - 2 + par, E8 // 2 - 1, par, par == 1)

        with nc.Block() as block:
            @block.sync
            def _(sp):
                def load(e, par):
                    for dst, name in ((w1, "W1"), (w3, "W3"), (w2, "W2")):
                        sp.dma_start(dst[par][:], w[name][ds(e, 1)].rearrange("e (k p) n -> p (e k) n", p=P)).then_inc(w_loaded[par], 16)

                def body(e, turn, par, last):
                    if not last:
                        sp.wait_ge(y_psum, 2 * e)
                        load(e + 1, (par + 1) % 2)

                load(0, 0)
                experts(sp, body)

            @block.gpsimd
            def _(pool):
                def gather(e, turn, par):
                    if later(e, 1):
                        pool.wait_ge(xT_psum, e - 1)
                        pool.wait_ge(scattered, 16 * CAPT * (e - 1))
                    nc.gpsimd.tensor_copy(ids[par][:], idx[:, ds(e, 1), :].rearrange("p o a -> p (o a)")).then_inc(ids_ready, 1)
                    passed(pool, ids_ready, e + 1, turnstile)
                    for a in range(CAPT):
                        pool.indirect_dma_start(out=xg[par][:, a, :], out_offset=None, in_=xn_dram,
                                                in_offset=bass.IndirectOffsetOnAxis(ap=ids[par][:, a:a + 1], axis=0)
                                                ).then_inc(gathered[par], 16)

                def body(e, turn, par, last):
                    if not last:
                        gather(e + 1, turn + (par + 1) // 2, (par + 1) % 2)
                    pool.wait_ge(y_ready, CAPT * (e + 1))
                    pool.wait_ge(scattered, 16 * CAPT * e)
                    passed(pool, y_ready, 1, turnstile)
                    for a in range(CAPT):
                        pool.indirect_dma_start(out=out, out_offset=bass.IndirectOffsetOnAxis(ap=ids[par][:, a:a + 1], axis=0),
                                                in_=yo[par][:, a, :], in_offset=None, compute_op=ALU.add).then_inc(scattered, 16)

                gather(0, 0, 0)
                experts(pool, body)
                pool.wait_ge(scattered, 16 * CAPT * E8)

            @block.tensor
            def _(pe):
                def transpose_x(e, turn, par):
                    pe.wait_ge(gathered[par], 16 * CAPT * (turn + 1))
                    for a in range(CAPT):
                        for half in range(HALVES):
                            last = nc.tensor.transpose(tps[:, half, a * P:(a + 1) * P], xg[par][:, a, half * P:(half + 1) * P],
                                                       ident[:])
                    last.then_inc(xT_psum, 1)

                def body(e, turn, par, final):
                    pe.wait_ge(w_loaded[par], 48 * (turn + 1))
                    pe.wait_ge(xT_ready, e + 1)
                    for f in range(FK):
                        pe.wait_ge(h_ready, FK * e + f + 1)
                        for wt_, bank in ((w1, p1), (w3, p3)):
                            for half in range(HALVES):
                                last = nc.tensor.matmul(bank[f % 2][:], wt_[par][:, half, f * P:(f + 1) * P], xT[:, half],
                                                        start=(half == 0), stop=(half == HALVES - 1))
                            last.then_inc(h_psum, 1)
                    if not final:
                        transpose_x(e + 1, turn + (par + 1) // 2, (par + 1) % 2)
                    pe.wait_ge(h_ready, FK * (e + 1) + 2)
                    pe.wait_ge(y_ready, CAPT * e)
                    for bank in range(2):
                        for a in (2 * bank, 2 * bank + 1):
                            for f in range(FK):
                                last = nc.tensor.matmul(yps[:, bank, (a % 2) * D:(a % 2 + 1) * D], hT[:, f, a * P:(a + 1) * P],
                                                        w2[par][:, f], start=(f == 0), stop=(f == FK - 1))
                        last.then_inc(y_psum, 1)

                transpose_x(0, 0, 0)
                experts(pe, body)

            @block.scalar
            def _(act):
                def evacuate_xT(e):
                    act.wait_ge(xT_psum, e + 1)
                    act.wait_ge(h_psum, 2 * FK * e)
                    nc.scalar.activation(xT[:], tps[:], ACT.Copy).then_inc(xT_ready, 1)

                def body(e, turn, par, last):
                    for f in range(FK):
                        act.wait_ge(h_psum, 2 * (FK * e + f) + 1)
                        act.wait_ge(h_ready, FK * e + f + 1)
                        nc.scalar.activation(act1[f % 2][:], p1[f % 2][:], ACT.Silu).then_inc(silu_ready, 1)
                    if not last:
                        evacuate_xT(e + 1)

                evacuate_xT(0)
                experts(act, body)

            @block.vector
            def _(dve):
                def body(e, turn, par, last):
                    dve.wait_ge(y_psum, 2 * e)
                    for f in range(FK):
                        dve.wait_ge(silu_ready, FK * e + f + 1)
                        dve.wait_ge(h_psum, 2 * (FK * e + f) + 2)
                        nc.vector.tensor_tensor(hT[:, f], p3[f % 2][:], act1[f % 2][:], ALU.mult).then_inc(h_ready, 1)
                    for a in range(CAPT):
                        dve.wait_ge(y_psum, 2 * e + a // 2 + 1)
                        nc.vector.tensor_scalar(yo[par][:, a], yps[:, a // 2, (a % 2) * D:(a % 2 + 1) * D],
                                                wt[:, ds(e, 1), a], None, ALU.mult).then_inc(y_ready, 1)

                nc.vector.memset(yo[0][:], 0.0).then_inc(h_ready, 2)
                experts(dve, body)


def token_choice_moe(nc, x_sb, k, w, out):
    xn_dram = nc.dram_tensor("normalized", (TOKENS, D), fp32, kind="Internal").ap()
    with ExitStack() as ctx:
        own = Kit(nc, ctx, "tc_")
        sc = own.sb("sc", [P, TILES, E8])
        idx, wt = own.sb("idx", [P, E8, CAPT], i32), own.sb("wt", [P, E8, CAPT])
        token_scores(nc, x_sb, k["ident"], k["eps_pow"], w, sc, xn_dram, out)
        choose_tokens(nc, k, sc, idx, wt)
        swiglu_experts(nc, k["ident"], w, idx, wt, xn_dram, out)


def decoder(nc, a, out):
    with ExitStack() as ctx:
        kit = Kit(nc, ctx, "x_")
        x_sb = kit.sb("x", [P, TILES, D])
        k = make_constants(nc, kit)
        load_x(nc, kit, x_sb, a["x"])
        of = lambda layer: {name[len(layer):]: ap for name, ap in a.items() if name.startswith(layer)}
        shared = dict(ctxT=a["ctxT"], mask=a["mask"])
        cross_attention(nc, x_sb, k["ident"], k["eps_pow"], dict(of("L0_xattn_"), **shared), "xa0", True)
        self_attention_moe(nc, kit, x_sb, k, of("L0_ffn_"))
        cross_attention(nc, x_sb, k["ident"], k["eps_pow"], dict(of("L1_xattn_"), **shared), "xa1", False)
        token_choice_moe(nc, x_sb, k, of("L1_ffn_"), out)



def kernel(**inputs):
    import numpy as np
    import concourse.bacc as bacc
    from concourse.bass_utils import run_bass_kernel_spmd

    def take(name):
        return np.asarray(inputs[name])

    def columns(v):
        return v.reshape(2, 128).T

    arrays = {"x": take("x").reshape(4096, 256), "ctxT": take("ctx_1024").transpose(2, 0, 1),
              "mask": take("mask_Bx1xSxS2_ik0").reshape(4096, 64)}
    for layer, transposed in (("L0_xattn_", True), ("L1_xattn_", False)):
        weights = [take(layer + "W" + n) for n in "qkvo"]
        arrays[layer + "wts"] = np.stack([m.T if transposed else m for m in weights])
        arrays[layer + "bqk"] = np.stack([columns(take(layer + "b" + n)) for n in "qk"], 1)
        arrays[layer + "bv"], arrays[layer + "bo"] = take(layer + "bv"), take(layer + "bo")
    f = "L0_ffn_"
    arrays[f + "ffn_qkv"] = np.stack([take(f + n + "_w") for n in "qkv"])
    for n in ("scale_w", "gate_b"):
        arrays[f + n] = columns(take(f + n))
    for n in ("gate_w", "out_w", "n1_g", "n1_b", "n2_g", "n2_b", "moe_gate_w", "moe_gate_b", "w1", "w2", "res_scale"):
        arrays[f + n] = take(f + n)
    for n in ("b1", "ln_g", "ln_b", "b2"):
        arrays[f + n] = take(f + n).reshape(-1)
    f = "L1_ffn_"
    arrays[f + "Wg"] = take(f + "Wg").T
    for n in ("W1", "W2", "W3"):
        arrays[f + n] = take(f + n).transpose(0, 2, 1)

    nc = bacc.Bacc("TRN2", target_bir_lowering=False, num_devices=1)
    feeds, aps = {}, {}
    for name, array in arrays.items():
        array = np.ascontiguousarray(array)
        feeds["in_" + name] = array
        aps[name] = nc.dram_tensor("in_" + name, array.shape, mybir.dt.from_np(array.dtype), kind="ExternalInput").ap()
    out = nc.dram_tensor("out_x", (4096, 256), fp32, kind="ExternalOutput").ap()
    decoder(nc, aps, out)
    result = run_bass_kernel_spmd(nc, [feeds], core_ids=[0])
    return result.results[0]["out_x"].reshape(4, 1024, 256)
```

```python
import concourse.bass as bass
from concourse import mybir
from contextlib import ExitStack

fp32 = mybir.dt.float32
bf16 = mybir.dt.bfloat16
i32 = mybir.dt.int32
u32 = mybir.dt.uint32
ALU = mybir.AluOpType
ACT = mybir.ActivationFunctionType
X = mybir.AxisListType.X
ds = bass.ds

P = 128
B, S, D = 4, 1024, 256
SC = 64
H = 16
DK = D // H
HALVES = D // P
TOKENS = B * S
TILES = TOKENS // P
CT = 4
CW = CT * P
CHUNKS = TOKENS // CW
HH = H // HALVES
EPS = 1e-5
FILL = -2.0 ** 60
SCALE = 1.0 / DK ** 0.5


class Kit:

    def __init__(self, nc, ctx, prefix):
        self.nc, self.ctx, self.prefix = nc, ctx, prefix
        self.numbers = []
        ctx.callback(self.clear_semaphores)

    def clear_semaphores(self):
        if not self.numbers:
            return
        with self.nc.Block() as block:
            @block.gpsimd
            def _(pool):
                first = 0
                for i, number in enumerate(self.numbers):
                    if i + 1 == len(self.numbers) or self.numbers[i + 1] != number + 1:
                        pool.sem_clear(range(self.numbers[first], number + 1))
                        first = i + 1

    def sb(self, name, shape, dt=fp32):
        return self.ctx.enter_context(self.nc.sbuf_tensor(self.prefix + name, shape, dt))

    def ps(self, name, shape):
        return self.ctx.enter_context(self.nc.psum_tensor(self.prefix + name, shape, fp32))

    def sem(self, name):
        semaphore = self.ctx.enter_context(self.nc.semaphore(self.prefix + name))
        self.numbers.append(semaphore.num)
        return semaphore


def bc(ap, axis, shape):
    return ap.unsqueeze(axis).broadcast_to(shape)


def later(k, first):
    return not isinstance(k, int) or k >= first


def passed(eng, semaphore, value, turnstile):
    eng.wait_ge(semaphore, value)
    eng.sem_inc(turnstile, 1)


def cross_attention(nc, x_sb, ident, eps_pow, w, name, masked):
    with ExitStack() as ctx:
        kit = Kit(nc, ctx, name + "_")
        sb, ps, sem = kit.sb, kit.ps, kit.sem
        turnstile = sem("turnstile")
        wts = sb("wts", [P, 4, HALVES, D])
        ctxT = sb("ctxT", [P, HALVES, B, 2, SC])
        bqk = sb("bqk", [P, 2, HALVES])
        bv = sb("bv", [P, D])
        bo = sb("bo", [P, D])
        headmask = sb("headmask", [P, HH])
        identb = sb("identb", [P, P], bf16)
        pairmask = sb("pairmask", [P, H // 2, 2, DK])
        kT = sb("kT", [P, HALVES, B, SC])
        kblk = sb("kblk", [P, B, HALVES, HH, SC])
        vblk = sb("vblk", [P, B, H // 2, 2, DK])
        vst = sb("vst", [P, D])
        if masked:
            mask_i = sb("mask_i", [P, TILES, SC], i32)
            fill = sb("fill", [P, TILES, SC], bf16)
        stats, mv = sb("stats", [P, CT, 6]), sb("mv", [P, CT, 2])
        var, rstd = sb("var", [P, CT]), sb("rstd", [P, CT])
        xn = sb("xn", [P, CT, D])
        xnT = sb("xnT", [P, HALVES, CW])
        qT = sb("qT", [P, HALVES, TOKENS])
        qst = sb("qst", [P, HALVES, CW])
        prob = sb("prob", [P, CT, H, SC])
        mx, den, rden = (sb(n, [P, CT, H]) for n in ("mx", "den", "rden"))
        pT = sb("pT", [P, H // 2, CW])
        oT = sb("oT", [P, HALVES, CW])
        front = ps("front", [P, HALVES, CW])
        score = [ps(f"score{i}", [P, H, SC]) for i in range(2)]
        ptps = [ps(f"ptps{i}", [P, CW]) for i in range(2)]

        loaded = sem("loaded")
        masks_made, pair_made = sem("masks_made"), sem("pair_made")
        k_psum, k_made = sem("k_psum"), sem("k_made")
        v_psum, v_made = sem("v_psum"), sem("v_made")
        kblk_made, mask_step = sem("kblk_made"), sem("mask_step")

        with nc.Block() as block:
            @block.sync
            def _(sp):
                sp.dma_start(wts[:], w["wts"].rearrange("f (k p) n -> p f k n", p=P)).then_inc(loaded, 16)
                for twice in range(2):
                    for k in range(HALVES):
                        sp.dma_start(ctxT[:, k, :, twice, :], w["ctxT"][k * P:(k + 1) * P]).then_inc(loaded, 16)
                sp.dma_start(bqk[:], w["bqk"].rearrange("p f k -> p f k")).then_inc(loaded, 16)
                sp.dma_start(bv[:], w["bv"].partition_broadcast(P)).then_inc(loaded, 16)
                sp.dma_start(bo[:], w["bo"].partition_broadcast(P)).then_inc(loaded, 16)
                if masked:
                    sp.dma_start(mask_i[:], w["mask"].rearrange("(t p) k -> p t k", p=P)).then_inc(loaded, 16)

            LOADS = 16 * (9 if masked else 8)

            @block.gpsimd
            def _(pool):
                nc.gpsimd.memset(headmask[:], 1.0).then_inc(masks_made, 1)
                pool.wait_ge(masks_made, 1)
                nc.gpsimd.affine_select(out=headmask[:], in_=headmask[:], compare_op=ALU.is_ge, fill=0.0, base=0,
                                        pattern=[[-DK, HH]], channel_multiplier=1).then_inc(masks_made, 1)
                pool.wait_ge(masks_made, 2)
                nc.gpsimd.affine_select(out=headmask[:], in_=headmask[:], compare_op=ALU.is_ge, fill=0.0,
                                        base=DK - 1, pattern=[[DK, HH]], channel_multiplier=-1).then_inc(masks_made, 1)

            @block.tensor
            def _(pe):
                pe.wait_ge(loaded, LOADS)
                for half in range(HALVES):
                    for k in range(HALVES):
                        last = nc.tensor.matmul(front[:, half, 0:B * SC], wts[:, 1, k, half * P:(half + 1) * P],
                                                ctxT[:, k, :, 0, :], start=(k == 0), stop=(k == HALVES - 1))
                    last.then_inc(k_psum, 1)
                for b in range(B):
                    for k in range(HALVES):
                        last = nc.tensor.matmul(score[b // 2][:].rearrange("p h k -> p (h k)")[:, 512 * (b % 2):512 * (b % 2) + D],
                                                ctxT[:, k, b, :, :], wts[:, 2, k, :],
                                                start=(k == 0), stop=(k == HALVES - 1))
                    last.then_inc(v_psum, 1)

            @block.scalar
            def _(act):
                for half in range(HALVES):
                    act.wait_ge(k_psum, half + 1)
                    nc.scalar.activation(kT[:, half], front[:, half, 0:B * SC], ACT.Identity,
                                         bias=bqk[:, 1, half:half + 1]).then_inc(k_made, 1)

            @block.vector
            def _(dve):
                dve.wait_ge(loaded, LOADS)
                if masked:
                    nc.vector.tensor_scalar(fill[:], mask_i[:], 0.0, FILL, ALU.is_equal, ALU.mult).then_inc(mask_step, 1)
                nc.vector.tensor_copy(identb[:], ident[:])
                for rows in range(2):
                    for a in range(2):
                        nc.vector.memset(pairmask[SC * rows:SC * rows + SC, :, a, :],
                                         1.0 if a == rows else 0.0).then_inc(pair_made, 1)
                dve.wait_ge(pair_made, 4)
                dve.wait_ge(masks_made, 3)
                for b in range(B):
                    values = vblk[:, b]
                    split = lambda ap: ap.rearrange("p (j a d) -> p j a d", a=2, d=DK)
                    dve.wait_ge(v_psum, b + 1)
                    nc.vector.tensor_tensor(values, split(score[b // 2][:].rearrange("p h k -> p (h k)")[:, 512 * (b % 2):512 * (b % 2) + D]),
                                            split(bv[:]), ALU.add).then_inc(v_made, 1)
                    dve.wait_ge(v_made, 2 * b + 1)
                    nc.vector.tensor_tensor(values, values, pairmask[:], ALU.mult).then_inc(v_made, 1)
                for half in range(HALVES):
                    dve.wait_ge(k_made, half + 1)
                    for b in range(B):
                        nc.vector.tensor_tensor(kblk[:, b, half], bc(kT[:, half, b, :], 1, [P, HH, SC]),
                                                bc(headmask[:], 2, [P, HH, SC]), ALU.mult).then_inc(kblk_made, 1)

        stats_done, ln_stats, var_done, rstd_ready = sem("stats_done"), sem("ln_stats"), sem("var_done"), sem("rstd_ready")
        xn_ready, xnT_psum, xnT_ready = sem("xn_ready"), sem("xnT_psum"), sem("xnT_ready")
        q_psum, qT_ready, bo_added = sem("q_psum"), sem("qT_ready"), sem("bo_added")
        scores_ready, max_done, centered, exp_ready = sem("scores_ready"), sem("max_done"), sem("centered"), sem("exp_ready")
        den_ready, rden_ready, probs_ready = sem("den_ready"), sem("rden_ready"), sem("probs_ready")
        qst_ready, pT_psum, pT_ready, vst_ready = sem("qst_ready"), sem("pT_psum"), sem("pT_ready"), sem("vst_ready")
        o_psum, oT_ready, y_psum, y_added = sem("o_psum"), sem("oT_ready"), sem("y_psum"), sem("y_added")
        q_banks = [score[half][:].rearrange("p h k -> p (h k)")[:, 0:CW] for half in range(HALVES)]

        def chunks(eng, body):
            body(0, True)
            with eng.Fori(1, CHUNKS - 1) as c:
                body(c, True)
            body(CHUNKS - 1, False)

        def after(c, t):
            return c + t // CT, t % CT

        def steps(c, more, body):
            for t in range(CT):
                ahead = after(c, t + 3) if more or t == 0 else None
                body(t, ahead)

        with nc.Block() as block:
            @block.vector
            def _(dve):
                def moments(c):
                    for t in range(CT):
                        nc.vector.bn_stats(stats[:, t], x_sb[:, ds(CT * c + t, 1), :]).then_inc(stats_done, 1)
                    if later(c, 1):
                        dve.wait_ge(xn_ready, CT * c)
                        dve.wait_ge(var_done, c)
                    passed(dve, stats_done, CT * (c + 1), turnstile)
                    for t in range(CT):
                        nc.vector.bn_aggr(mv[:, t], stats[:, t]).then_inc(ln_stats, 1)

                def normalize_x(c, more):
                    dve.wait_ge(rstd_ready, c + 1)
                    dve.wait_ge(ln_stats, CT * (c + 1))
                    if later(c, 1):
                        dve.wait_ge(xnT_psum, c)
                    for t in range(CT):
                        nc.vector.tensor_scalar(xn[:, t], x_sb[:, ds(CT * c + t, 1), :], mv[:, t, 0:1], rstd[:, t:t + 1],
                                                ALU.subtract, ALU.mult).then_inc(xn_ready, 1)
                    if more:
                        moments(c + 1)

                def center(c, t):
                    n = CT * c + t
                    dve.wait_ge(scores_ready, n + 1)
                    if later(c, 1):
                        dve.wait_ge(pT_psum, 2 * (n - CT + 1))
                        if t == 0:
                            dve.wait_ge(centered, n)
                    nc.vector.tensor_reduce(mx[:, t], score[t % 2][:], axis=X, op=ALU.max).then_inc(max_done, 1)
                    dve.wait_ge(max_done, n + 1)
                    nc.vector.tensor_tensor(prob[:, t], score[t % 2][:], bc(mx[:, t], 2, [P, H, SC]),
                                            ALU.subtract).then_inc(centered, 1)

                def normalizer(c, t):
                    n = CT * c + t
                    dve.wait_ge(exp_ready, n + 1)
                    nc.vector.tensor_reduce(den[:, t], prob[:, t], axis=X, op=ALU.add).then_inc(den_ready, 1)
                    dve.wait_ge(den_ready, n + 1)
                    if later(c, 1):
                        dve.wait_ge(probs_ready, n - CT + 1)
                    nc.vector.reciprocal(rden[:, t], den[:, t]).then_inc(rden_ready, 1)

                def add_residual(c):
                    dve.wait_ge(bo_added, c + 1)
                    for bank in range(2):
                        dve.wait_ge(y_psum, 2 * c + bank + 1)
                        xs = x_sb[:, ds(CT * c + 2 * bank, 2), :]
                        nc.vector.tensor_tensor(xs, front[:, bank].rearrange("p (t d) -> p t d", t=2), xs,
                                                ALU.add).then_inc(y_added, 1)

                def attend(c, more):
                    def step(t, ahead):
                        if ahead:
                            center(*ahead)
                        if more or t < 2:
                            normalizer(*after(c, t + 2))
                        if t == 2 and later(c, 1):
                            add_residual(c - 1)

                    steps(c, more, step)

                moments(0)
                chunks(dve, normalize_x)
                for t in range(3):
                    center(0, t)
                for t in range(2):
                    normalizer(0, t)
                chunks(dve, attend)
                add_residual(CHUNKS - 1)

            @block.gpsimd
            def _(pool):
                def make_rstd(c):
                    pool.wait_ge(ln_stats, CT * (c + 1))
                    nc.gpsimd.tensor_tensor(var[:], mv[:, :, 1], eps_pow[:, 0], ALU.add).then_inc(var_done, 1)
                    pool.wait_ge(var_done, c + 1)
                    if later(c, 1):
                        pool.wait_ge(xn_ready, CT * c)
                    nc.gpsimd.tensor_tensor(rstd[:], var[:], eps_pow[:, 1], ALU.pow).then_inc(rstd_ready, 1)

                def norm_chunk(c, more):
                    if more:
                        make_rstd(c + 1)
                    pool.wait_ge(xn_ready, CT * (c + 1))
                    xs = x_sb[:, ds(CT * c, CT), :]
                    nc.gpsimd.tensor_tensor(xs, xs, bc(bo[:], 1, [P, CT, D]), ALU.add).then_inc(bo_added, 1)

                def divide(c, t):
                    pool.wait_ge(rden_ready, CT * c + t + 1)
                    nc.gpsimd.tensor_tensor(prob[:, t], prob[:, t], bc(rden[:, t], 2, [P, H, SC]),
                                            ALU.mult).then_inc(probs_ready, 1)

                def attend(c, more):
                    for t in range(CT):
                        if t == 1:
                            if later(c, 1):
                                pool.wait_ge(o_psum, 2 * c)
                            nc.gpsimd.tensor_copy(vst[:], vblk[:, ds(c // 2, 1)]).then_inc(vst_ready, 1)
                        if more or t < 2:
                            divide(*after(c, t + 2))

                make_rstd(0)
                chunks(pool, norm_chunk)
                divide(0, 0)
                divide(0, 1)
                chunks(pool, attend)

            @block.scalar
            def _(act):
                def evacuate_xnT(c):
                    act.wait_ge(xnT_psum, c + 1)
                    if later(c, 1):
                        act.wait_ge(q_psum, 2 * c)
                    nc.scalar.activation(xnT[:], front[:], ACT.Copy).then_inc(xnT_ready, 1)

                def evacuate_qT(c, half):
                    act.wait_ge(q_psum, 2 * c + half + 1)
                    nc.scalar.activation(qT[:, half, ds(CW * c, CW)], q_banks[half], ACT.Identity,
                                         bias=bqk[:, 0, half:half + 1]).then_inc(qT_ready, 1)

                def q_chunk(c, more):
                    evacuate_qT(c, 0)
                    if more:
                        evacuate_xnT(c + 1)
                    evacuate_qT(c, 1)

                def fix_qT(c):
                    if later(c, 1):
                        act.wait_ge(scores_ready, CT * c)
                    nc.scalar.activation(qst[:], qT[:, :, ds(CW * c, CW)], ACT.Copy).then_inc(qst_ready, 1)

                def exponential(c, t):
                    act.wait_ge(centered, CT * c + t + 1)
                    nc.scalar.activation(prob[:, t], prob[:, t], ACT.Exp, scale=SCALE).then_inc(exp_ready, 1)

                def evacuate_pT(c, t):
                    for part in range(2):
                        act.wait_ge(pT_psum, 2 * (CT * c + t) + part + 1)
                        nc.scalar.activation(pT[:, 4 * part:4 * part + 4, t * P:(t + 1) * P],
                                             ptps[part][:].rearrange("p (j t) -> p j t", j=4), ACT.Copy).then_inc(pT_ready, 1)

                def evacuate_oT(c):
                    if later(c, 1):
                        act.wait_ge(y_psum, 2 * c)
                    for half in range(HALVES):
                        act.wait_ge(o_psum, 2 * c + half + 1)
                        nc.scalar.activation(oT[:, half], front[:, half], ACT.Copy).then_inc(oT_ready, 1)

                def attend(c, more):
                    def step(t, ahead):
                        if t == 0:
                            if more:
                                fix_qT(c + 1)
                            if later(c, 1):
                                evacuate_oT(c - 1)
                        evacuate_pT(c, t)
                        if ahead:
                            exponential(*ahead)

                    steps(c, more, step)

                evacuate_xnT(0)
                chunks(act, q_chunk)
                act.wait_ge(qT_ready, 2 * CHUNKS)
                fix_qT(0)
                for t in range(3):
                    exponential(0, t)
                chunks(act, attend)
                evacuate_oT(CHUNKS - 1)

            @block.tensor
            def _(pe):
                def transpose_xn(c):
                    pe.wait_ge(xn_ready, CT * (c + 1))
                    if later(c, 1):
                        pe.wait_ge(xnT_ready, c)
                    for t in range(CT):
                        for half in range(HALVES):
                            last = nc.tensor.transpose(front[:, half, t * P:(t + 1) * P],
                                                       xn[:, t, half * P:(half + 1) * P], ident[:])
                    last.then_inc(xnT_psum, 1)

                def project_q(c, more):
                    if more:
                        transpose_xn(c + 1)
                    pe.wait_ge(xnT_ready, c + 1)
                    for half in range(HALVES):
                        if later(c, 1):
                            pe.wait_ge(qT_ready, 2 * c + half - 1)
                        for k in range(HALVES):
                            last = nc.tensor.matmul(q_banks[half], wts[:, 0, k, half * P:(half + 1) * P], xnT[:, k],
                                                    start=(k == 0), stop=(k == HALVES - 1))
                        last.then_inc(q_psum, 1)

                def scores(c, t):
                    if t == 0:
                        pe.wait_ge(qst_ready, c + 1)
                    if later(c, 1) or t >= 2:
                        pe.wait_ge(centered, CT * c + t - 1)
                    for half in range(HALVES):
                        bank = score[t % 2][:, half * HH:(half + 1) * HH, :]
                        last = nc.tensor.matmul(bank, qst[:, half, t * P:(t + 1) * P],
                                                kblk[:, ds(c // 2, 1), half].rearrange("p o h k -> p (o h k)"),
                                                start=True, stop=not masked)
                        if masked:
                            last = nc.tensor.matmul(bank, identb[:], fill[:, ds(CT * c + t, 1), :].broadcast_to([P, HH, SC]),
                                                    start=False, stop=True)
                    last.then_inc(scores_ready, 1)

                def transpose_probs(c, t):
                    pe.wait_ge(probs_ready, CT * c + t + 1)
                    for part in range(2):
                        if later(c, 1) or t:
                            pe.wait_ge(pT_ready, 2 * (CT * c + t) + part - 1)
                        for j in range(4):
                            pair = 4 * part + j
                            last = nc.tensor.transpose(ptps[part][:, j * P:(j + 1) * P], prob[:, t, 2 * pair:2 * pair + 2, :],
                                                       ident[:])
                        last.then_inc(pT_psum, 1)

                def weigh_values(c):
                    pe.wait_ge(vst_ready, c + 1)
                    pe.wait_ge(pT_ready, 2 * CT * (c + 1))
                    if later(c, 1):
                        pe.wait_ge(y_added, 2 * c)
                    for half in range(HALVES):
                        for j in range(4):
                            last = nc.tensor.matmul(front[32 * j:32 * j + 32, half],
                                                    vst[:, half * P + 32 * j:half * P + 32 * j + 32],
                                                    pT[:, half * 4 + j], start=True, stop=True)
                        last.then_inc(o_psum, 1)

                def project_out(c):
                    pe.wait_ge(oT_ready, 2 * (c + 1))
                    for bank in range(2):
                        for t in (2 * bank, 2 * bank + 1):
                            for k in range(HALVES):
                                last = nc.tensor.matmul(front[:, bank, (t % 2) * D:(t % 2 + 1) * D],
                                                        oT[:, k, t * P:(t + 1) * P], wts[:, 3, k],
                                                        start=(k == 0), stop=(k == HALVES - 1))
                        last.then_inc(y_psum, 1)

                def attend(c, more):
                    def step(t, ahead):
                        if ahead:
                            scores(*ahead)
                        if t == 0 and later(c, 1):
                            weigh_values(c - 1)
                        if t == 1 and later(c, 1):
                            project_out(c - 1)
                        transpose_probs(c, t)

                    steps(c, more, step)

                transpose_xn(0)
                chunks(pe, project_q)
                pe.wait_ge(qT_ready, 2 * CHUNKS)
                for t in range(3):
                    scores(0, t)
                chunks(pe, attend)
                weigh_values(CHUNKS - 1)
                project_out(CHUNKS - 1)

PAIRS = ((0, 0), (1, 0), (2, 0), (0, 1), (1, 1), (0, 2))
KROWS = len(PAIRS) * DK
MROWS = 2
GH = 4
GROUPS = B * H // GH
KT = S // P
VW = DK + 1
UNITS = GROUPS * 2


def self_projections(nc, x_sb, src_sb, ident, eps_pow, w, q_parts, k_parts, v_dram):
    with ExitStack() as ctx:
        kit = Kit(nc, ctx, "sp_")
        sb, ps, sem = kit.sb, kit.ps, kit.sem
        turnstile = sem("turnstile")
        wts = sb("wts", [P, 3, HALVES, D])
        swcol = sb("swcol", [P, HALVES])
        swblk = sb("swblk", [P, HALVES, P])
        stats, mv = sb("stats", [P, CT, 6]), sb("mv", [P, CT, 2])
        var, rstd = sb("var", [P, CT]), sb("rstd", [P, CT])
        xn = sb("xn", [P, CT, D])
        srcT = sb("srcT", [P, HALVES, CW])
        qT, th = sb("qT", [P, HALVES, CW]), sb("th", [P, HALVES, CW])
        qrest, krest = sb("qrest", [P, HALVES, CW]), sb("krest", [P, HALVES, CW])
        qpart = [sb(f"qpart{i}", [P, 3, HALVES, CW], bf16) for i in range(2)]
        kpart = [sb(f"kpart{i}", [P, 3, HALVES, CW], bf16) for i in range(2)]
        vt = [sb(f"vt{i}", [P, H // GH, CT, GH, VW]) for i in range(2)]
        vps, qps, kps, zps = (ps(n, [P, HALVES, CW]) for n in ("vps", "qps", "kps", "zps"))

        loaded, blk_made = sem("loaded"), sem("blk_made")
        stats_done, ln_stats, var_done, rstd_ready = sem("stats_done"), sem("ln_stats"), sem("var_done"), sem("rstd_ready")
        xn_ready, xnT_psum, srcT_ready = sem("xn_ready"), sem("xnT_psum"), sem("srcT_ready")
        v_psum, v_ready, q_psum, k_psum, z_psum = (sem("v_psum"), sem("v_ready"), sem("q_psum"), sem("k_psum"),
                                                   sem("z_psum"))
        qT_ready, th_ready, q_scaled = sem("qT_ready"), sem("th_ready"), sem("q_scaled")
        k1, krest_made, k2, k3 = sem("k1"), sem("krest_made"), sem("k2"), sem("k3")
        q1, qrest_made, q2, q3 = sem("q1"), sem("qrest_made"), sem("q2"), sem("q3")
        src_kept = sem("src_kept")
        q_stored, k_stored, v_stored = ([sem(f"{n}_stored{i}") for i in range(2)] for n in "qkv")

        RUNS = 3 * HALVES

        def batches(eng, chunk, flags=False):
            def pair(i, last):
                for par in range(2):
                    if flags:
                        chunk(i, par, last and par == 1)
                    else:
                        chunk(i, par)

            pair(0, False)
            with eng.Fori(1, B - 1) as i:
                pair(i, False)
            pair(B - 1, True)

        with nc.Block() as block:
            @block.sync
            def _(sp):
                sp.dma_start(wts[:], w["ffn_qkv"].rearrange("f (k p) n -> p f k n", p=P)).then_inc(loaded, 16)
                sp.dma_start(swcol[:], w["scale_w"]).then_inc(loaded, 16)

                q_runs = ((0, 3, 0, False), (3, 2, 0, False), (5, 1, 0, False))
                k_runs = ((0, 3, 0, True), (3, 2, 1, True), (5, 1, 2, True))

                def store(i, par):
                    c = 2 * i + par
                    sp.wait_ge(v_ready, 2 * (c + 1))
                    sp.dma_start(v_dram[ds(4 * i, 4), :, CT * par:CT * (par + 1), :].rearrange("g p k x -> p g (k x)"),
                                 vt[par][:].rearrange("p g t h v -> p g (t h v)")).then_inc(v_stored[par], 16)
                    for parts, dram, ready, stored, runs in ((kpart, k_parts, k3, k_stored, k_runs),
                                                             (qpart, q_parts, q3, q_stored, q_runs)):
                        sp.wait_ge(ready, c + 1)
                        for half in range(HALVES):
                            rows = dram[ds(4 * i + 2 * half, 2)].rearrange("g h (d r) t -> (g h d) r t", r=len(PAIRS))
                            for pair, pairs, part, same in runs:
                                src = (parts[par][:, part:part + 1, half].broadcast_to([P, pairs, CW]) if same else
                                       parts[par][:, part:part + pairs, half])
                                sp.dma_start(rows[:, pair:pair + pairs, par * CW:(par + 1) * CW], src).then_inc(stored[par], 16)

                batches(sp, store)
                for par in range(2):
                    sp.wait_ge(v_stored[par], 16 * B)
                    for stored in (q_stored, k_stored):
                        sp.wait_ge(stored[par], 16 * B * RUNS)

            @block.vector
            def _(dve):
                dve.wait_ge(loaded, 32)
                for half in range(HALVES):
                    nc.vector.tensor_tensor(swblk[:, half].rearrange("p (h d) -> p h d", d=DK),
                                            bc(w["headmask"][:], 2, [P, HH, DK]),
                                            bc(swcol[:, half:half + 1].broadcast_to([P, HH]), 2, [P, HH, DK]),
                                            ALU.mult).then_inc(blk_made, 1)
                for i in range(2):
                    nc.vector.memset(vt[i][:, :, :, :, DK:], 1.0).then_inc(blk_made, 1)

                def layernorm(c):
                    for t in range(CT):
                        nc.vector.bn_stats(stats[:, t], x_sb[:, ds(CT * c + t, 1), :]).then_inc(stats_done, 1)
                    if later(c, 1):
                        dve.wait_ge(var_done, c)
                        dve.wait_ge(xn_ready, CT * c)
                    passed(dve, stats_done, CT * (c + 1), turnstile)
                    for t in range(CT):
                        nc.vector.bn_aggr(mv[:, t], stats[:, t]).then_inc(ln_stats, 1)

                def ln_apply(c):
                    dve.wait_ge(rstd_ready, c + 1)
                    dve.wait_ge(ln_stats, CT * (c + 1))
                    if later(c, 1):
                        dve.wait_ge(xnT_psum, c)
                    if later(c, 1):
                        dve.wait_ge(src_kept, c)
                    for t in range(CT):
                        nc.vector.tensor_scalar(xn[:, t], x_sb[:, ds(CT * c + t, 1), :], mv[:, t, 0:1], rstd[:, t:t + 1],
                                                ALU.subtract, ALU.mult).then_inc(xn_ready, 1)

                def chunk(i, par, last):
                    c = 2 * i + par
                    if not last:
                        ln_apply(c + 1)
                    if not isinstance(i, int) or c + 2 < CHUNKS:
                        layernorm(c + 2)
                    dve.wait_ge(k1, c + 1)
                    if later(c, 1):
                        dve.wait_ge(k3, c)
                    nc.vector.tensor_tensor(krest[:], kps[:], kpart[par][:, 0], ALU.subtract).then_inc(krest_made, 1)
                    dve.wait_ge(th_ready, c + 1)
                    dve.wait_ge(qT_ready, c + 1)
                    nc.vector.scalar_tensor_tensor(out=qT[:], in0=th[:], scalar=1.0, in1=qT[:], op0=ALU.add,
                                                   op1=ALU.mult).then_inc(q_scaled, 1)
                    dve.wait_ge(q1, c + 1)
                    if later(c, 1):
                        dve.wait_ge(q3, c)
                    nc.vector.tensor_tensor(qrest[:], qT[:], qpart[par][:, 0], ALU.subtract).then_inc(qrest_made, 1)

                layernorm(0)
                ln_apply(0)
                layernorm(1)
                batches(dve, chunk, True)

            @block.gpsimd
            def _(pool):
                def make_rstd(c):
                    pool.wait_ge(ln_stats, CT * (c + 1))
                    nc.gpsimd.tensor_tensor(var[:], mv[:, :, 1], eps_pow[:, 0], ALU.add).then_inc(var_done, 1)
                    pool.wait_ge(var_done, c + 1)
                    if later(c, 1):
                        pool.wait_ge(xn_ready, CT * c)
                    nc.gpsimd.tensor_tensor(rstd[:], var[:], eps_pow[:, 1], ALU.pow).then_inc(rstd_ready, 1)

                def chunk(i, par, last):
                    c = 2 * i + par
                    pool.wait_ge(k2, c + 1)
                    nc.gpsimd.tensor_tensor(kpart[par][:, 2], krest[:], kpart[par][:, 1], ALU.subtract).then_inc(k3, 1)
                    if not isinstance(i, int) or c + 2 < CHUNKS:
                        make_rstd(c + 2)
                    pool.wait_ge(q2, c + 1)
                    nc.gpsimd.tensor_tensor(qpart[par][:, 2], qrest[:], qpart[par][:, 1], ALU.subtract).then_inc(q3, 1)

                make_rstd(0)
                make_rstd(1)
                batches(pool, chunk, True)

            @block.scalar
            def _(act):
                def keep_src(c):
                    act.wait_ge(xn_ready, CT * (c + 1))
                    nc.scalar.activation(src_sb[:, ds(CT * c, CT), :], xn[:], ACT.Copy).then_inc(src_kept, 1)

                def evacuate_srcT(c):
                    act.wait_ge(xnT_psum, c + 1)
                    if later(c, 1):
                        act.wait_ge(k_psum, c)
                    nc.scalar.activation(srcT[:], vps[:], ACT.Copy).then_inc(srcT_ready, 1)

                def chunk(i, par, last):
                    c = 2 * i + par
                    act.wait_ge(blk_made, 4)
                    if later(i, 1):
                        act.wait_ge(v_stored[par], 16 * i)
                    for bank in range(2):
                        act.wait_ge(v_psum, 2 * c + bank + 1)
                        for t in range(2):
                            copied = nc.scalar.activation(vt[par][:, :, 2 * bank + t, :, 0:DK],
                                                        vps[:, bank, t * D:(t + 1) * D].rearrange("p (g h d) -> p g h d", h=GH,
                                                                                                  d=DK), ACT.Copy)
                        copied.then_inc(v_ready, 1)
                    act.wait_ge(q_psum, c + 1)
                    if later(c, 1):
                        act.wait_ge(qrest_made, c)
                    nc.scalar.activation(qT[:], qps[:], ACT.Copy).then_inc(qT_ready, 1)
                    act.wait_ge(k_psum, c + 1)
                    if later(i, 1):
                        act.wait_ge(k_stored[par], 16 * RUNS * i)
                    nc.scalar.activation(kpart[par][:, 0], kps[:], ACT.Copy).then_inc(k1, 1)
                    if not last:
                        evacuate_srcT(c + 1)
                    act.wait_ge(krest_made, c + 1)
                    nc.scalar.activation(kpart[par][:, 1], krest[:], ACT.Copy).then_inc(k2, 1)
                    if not last:
                        keep_src(c + 1)
                    act.wait_ge(z_psum, c + 1)
                    if later(c, 1):
                        act.wait_ge(q_scaled, c)
                    nc.scalar.activation(th[:], zps[:], ACT.Tanh, scale=0.5).then_inc(th_ready, 1)
                    act.wait_ge(q_scaled, c + 1)
                    if later(i, 1):
                        act.wait_ge(q_stored[par], 16 * RUNS * i)
                    nc.scalar.activation(qpart[par][:, 0], qT[:], ACT.Copy).then_inc(q1, 1)
                    act.wait_ge(qrest_made, c + 1)
                    nc.scalar.activation(qpart[par][:, 1], qrest[:], ACT.Copy).then_inc(q2, 1)

                evacuate_srcT(0)
                keep_src(0)
                batches(act, chunk, True)

            @block.tensor
            def _(pe):
                def transpose_xn(c):
                    pe.wait_ge(xn_ready, CT * (c + 1))
                    if later(c, 1):
                        pe.wait_ge(v_ready, 2 * c)
                    for t in range(CT):
                        for half in range(HALVES):
                            last = nc.tensor.transpose(vps[:, half, t * P:(t + 1) * P],
                                                       xn[:, t, half * P:(half + 1) * P], ident[:])
                    last.then_inc(xnT_psum, 1)

                def chunk(i, par, last_chunk):
                    c = 2 * i + par
                    pe.wait_ge(srcT_ready, c + 1)
                    for bank in range(2):
                        for t in (2 * bank, 2 * bank + 1):
                            for k in range(HALVES):
                                last = nc.tensor.matmul(vps[:, bank, (t % 2) * D:(t % 2 + 1) * D],
                                                        srcT[:, k, t * P:(t + 1) * P], wts[:, 2, k],
                                                        start=(k == 0), stop=(k == HALVES - 1))
                        last.then_inc(v_psum, 1)
                    if later(c, 1):
                        pe.wait_ge(qT_ready, c)
                    for half in range(HALVES):
                        for k in range(HALVES):
                            last = nc.tensor.matmul(qps[:, half], wts[:, 0, k, half * P:(half + 1) * P], srcT[:, k],
                                                    start=(k == 0), stop=(k == HALVES - 1))
                    last.then_inc(q_psum, 1)
                    if later(c, 1):
                        pe.wait_ge(krest_made, c)
                    for half in range(HALVES):
                        for k in range(HALVES):
                            last = nc.tensor.matmul(kps[:, half], wts[:, 1, k, half * P:(half + 1) * P], srcT[:, k],
                                                    start=(k == 0), stop=(k == HALVES - 1))
                    last.then_inc(k_psum, 1)
                    if not last_chunk:
                        transpose_xn(c + 1)
                    pe.wait_ge(qT_ready, c + 1)
                    if later(c, 1):
                        pe.wait_ge(th_ready, c)
                    for half in range(HALVES):
                        last = nc.tensor.matmul(zps[:, half], swblk[:, half], qT[:, half], start=True, stop=True)
                    last.then_inc(z_psum, 1)

                pe.wait_ge(loaded, 32)
                pe.wait_ge(blk_made, 4)
                transpose_xn(0)
                batches(pe, chunk, True)


def self_attention(nc, attn, ident, q_parts, k_parts, v_dram, m_dram):
    SETS = 3
    with ExitStack() as ctx:
        kit = Kit(nc, ctx, "sa_")
        sb, ps, sem = kit.sb, kit.ps, kit.sem
        turnstile = sem("turnstile")
        qs = [sb(f"q{i}", [KROWS + MROWS, GH, S], bf16) for i in range(SETS)]
        ks = [sb(f"k{i}", [KROWS + MROWS, GH, S], bf16) for i in range(SETS)]
        vs = [sb(f"v{i}", [P, KT, GH, VW]) for i in range(SETS)]
        ex = [[sb(f"e{i}{p}", [P, 2, CW]) for p in range(2)] for i in range(2)]
        mpart = [sb(f"mpart{i}", [P, GH, CT, 2]) for i in range(2)]
        mfull = sb("mfull", [P, GH, CT])
        negm = sb("negm", [GH * CT, MROWS, P], bf16)
        o_sb = sb("o", [P, CW])
        rden = sb("rden", [P, CT, GH])
        bps = [ps(f"b{p}", [P, 2, CW]) for p in range(2)]
        aps = [ps(f"a{i}", [P, CW]) for i in range(2)]
        ops = ps("ops", [P, CW])
        misc = ps("misc", [P, CT, P])

        q_loaded, k_loaded, v_loaded = ([sem(f"{n}_loaded{i}") for i in range(SETS)] for n in "qkv")
        ones_made, b_scores, exp_done, pv_done = sem("ones_made"), sem("b_scores"), sem("exp_done"), sem("pv_done")
        a_scores, max_done, m_full, m_psum = sem("a_scores"), sem("max_done"), sem("m_full"), sem("m_psum")
        negm_hi, negm_ready, m_stored, m_loaded = sem("negm_hi"), sem("negm_ready"), sem("m_stored"), sem("m_loaded")
        o_evacuated, o_psum, rden_made, o_done = sem("o_evacuated"), sem("o_psum"), sem("rden_made"), sem("o_done")
        AM = GH * CT * 2

        def groups(eng, body):
            with eng.Fori(0, GROUPS // SETS - 1) as i:
                for j in range(SETS):
                    body(i * SETS + j, i, j)
            for g in range(GROUPS - SETS - 1, GROUPS):
                body(g, g // SETS, g % SETS)

        with nc.Block() as block:
            @block.sync
            def _(sp):
                def load(g, turn, s):
                    sp.dma_start(qs[s][0:KROWS], q_parts[ds(g, 1)].rearrange("g h r t -> r (g h) t")).then_inc(q_loaded[s], 16)
                    sp.dma_start(ks[s][0:KROWS], k_parts[ds(g, 1)].rearrange("g h r t -> r (g h) t")).then_inc(k_loaded[s], 16)
                    sp.dma_start(vs[s][:].rearrange("p k h v -> p k (h v)"),
                                 v_dram[ds(g, 1)].rearrange("g p k x -> p (g k) x")).then_inc(v_loaded[s], 16)

                def pass_max(a, s, qc):
                    sp.wait_ge(negm_ready, a + 1)
                    sp.dma_start(m_dram[ds(a, 1)].rearrange("a r c q -> (a c) r q"), negm[:]).then_inc(m_stored, 16)
                    sp.wait_ge(m_stored, 16 * (a + 1))
                    sp.dma_start(qs[s][KROWS:, :, qc * CW:(qc + 1) * CW],
                                 m_dram[ds(a, 1)].rearrange("a r (h t) q -> r (a h) (t q)", h=GH)).then_inc(m_loaded, 16)

                def body(g, turn, j):
                    for qc in range(2):
                        n = 2 * g + qc
                        if qc == 0 and not (isinstance(g, int) and g + 2 >= GROUPS):
                            sp.wait_ge(pv_done, 16 * n + 4)
                            load(g + 2, turn, (j + 2) % SETS)
                        a = n + 1
                        if not (isinstance(a, int) and a >= UNITS):
                            pass_max(a, (j + (a_is_next(qc))) % SETS, (qc + 1) % 2)

                def a_is_next(qc):
                    return 1 if qc == 1 else 0

                load(0, 0, 0)
                load(1, 0, 1)
                pass_max(0, 0, 0)
                groups(sp, body)

            @block.gpsimd
            def _(pool):
                for s in range(SETS):
                    nc.gpsimd.memset(ks[s][KROWS:], 1.0).then_inc(ones_made, 1)

            @block.vector
            def _(dve):
                def maxima(a, k, par):
                    head, rest = k // (CT * 2), k % (CT * 2)
                    dve.wait_ge(a_scores, AM * a + k + 1)
                    nc.vector.tensor_reduce(mpart[par][:, head, rest // 2, rest % 2:rest % 2 + 1], aps[k % 2][:], axis=X,
                                            op=ALU.max).then_inc(max_done, 1)

                def combine(a, par):
                    dve.wait_ge(max_done, AM * (a + 1))
                    dve.wait_ge(m_psum, a)
                    nc.vector.tensor_tensor(mfull[:], mpart[par][:, :, :, 0], mpart[par][:, :, :, 1],
                                            ALU.max).then_inc(m_full, 1)

                def split_max(a):
                    src = misc[:].rearrange("p a b -> p (a b)")[0:GH * CT, 0:P]
                    dve.wait_ge(m_psum, a + 1)
                    dve.wait_ge(m_stored, 16 * a)
                    nc.vector.tensor_scalar(negm[:, 0], src, -1.0, None, ALU.mult).then_inc(negm_hi, 1)
                    dve.wait_ge(negm_hi, a + 1)
                    nc.vector.scalar_tensor_tensor(out=negm[:, 1], in0=src, scalar=-1.0, in1=negm[:, 0], op0=ALU.mult,
                                                   op1=ALU.subtract).then_inc(negm_ready, 1)

                def normalize(n):
                    view = misc[:].rearrange("p t (h x) -> p t h x", h=GH)
                    dve.wait_ge(o_psum, n + 1)
                    nc.vector.reciprocal(rden[:], view[:, :, :, DK]).then_inc(rden_made, 1)
                    dve.wait_ge(rden_made, n + 1)
                    nc.vector.tensor_tensor(attn[:, ds(n, 1)].rearrange("p o (t h d) -> p (o t) h d", t=CT, h=GH),
                                            view[:, :, :, 0:DK], bc(rden[:], 3, [P, CT, GH, DK]),
                                            ALU.mult).then_inc(o_done, 1)

                def body(g, turn, j):
                    for qc in range(2):
                        n = 2 * g + qc
                        known = isinstance(g, int)
                        for kt in range(KT):
                            if not (known and g + 1 >= GROUPS):
                                for k in range(4 * kt, 4 * kt + 4):
                                    maxima(n + 2, k, qc)
                            if kt == 1 and not (known and n + 1 >= UNITS):
                                split_max(n + 1)
                            if kt == 4:
                                normalize(n)
                        if not (known and n + 2 >= UNITS):
                            combine(n + 2, qc)

                nc.vector.memset(o_sb[:], 1.0).then_inc(ones_made, 1)
                nc.vector.memset(ops[:], 0.0).then_inc(ones_made, 1)
                nc.vector.memset(rden[:], 0.0).then_inc(exp_done, 2)
                nc.vector.memset(mfull[:], 0.0).then_inc(pv_done, 4)
                dve.wait_ge(exp_done, 2)
                dve.wait_ge(pv_done, 4)
                for a in range(2):
                    for k in range(AM):
                        maxima(a, k, a)
                    combine(a, a)
                    if a == 0:
                        split_max(0)
                groups(dve, body)
                normalize(UNITS)

            @block.scalar
            def _(act):
                def body(g, turn, j):
                    for qc in range(2):
                        n = 2 * g + qc
                        for kt in range(KT):
                            for p in range(2):
                                act.wait_ge(b_scores, 16 * n + 2 * kt + p + 1)
                                act.wait_ge(pv_done, 16 * n + 2 * kt + p + 1)
                                nc.scalar.activation(ex[kt % 2][p][:], bps[p][:], ACT.Exp, scale=SCALE).then_inc(exp_done, 1)
                        act.wait_ge(pv_done, 16 * (n + 1) + 4)
                        act.wait_ge(o_psum, n + 1)
                        nc.scalar.activation(o_sb[:], ops[:], ACT.Copy).then_inc(o_evacuated, 1)

                act.wait_ge(ones_made, SETS + 2)
                groups(act, body)

            @block.tensor
            def _(pe):
                def first_scores(a, k, s, turn, qc):
                    head, rest = k // (CT * 2), k % (CT * 2)
                    if k == 0:
                        pe.wait_ge(q_loaded[s], 16 * (turn + 1))
                        pe.wait_ge(k_loaded[s], 16 * (turn + 1))
                    if not (isinstance(a, int) and a == 0 and k < 2):
                        pe.wait_ge(max_done, AM * a + k - 1)
                    q0 = (qc * CT + rest // 2) * P
                    nc.tensor.matmul(aps[k % 2][:], qs[s][0:KROWS, head, q0:q0 + P],
                                     ks[s][0:KROWS, head, (rest % 2) * CW:(rest % 2 + 1) * CW],
                                     start=True, stop=True).then_inc(a_scores, 1)

                def transpose_max(a):
                    pe.wait_ge(m_full, a + 1)
                    if not (isinstance(a, int) and a == 0):
                        pe.wait_ge(o_done, a - 1)
                    nc.tensor.transpose(misc[:].rearrange("p a b -> p (a b)")[0:GH * CT, 0:P],
                                        mfull[:].rearrange("p h t -> p (h t)"), ident[:]).then_inc(m_psum, 1)

                def transpose_out(n):
                    pe.wait_ge(o_evacuated, n)
                    if not (isinstance(n, int) and n >= UNITS - 1):
                        pe.wait_ge(negm_ready, n + 2)
                    else:
                        pe.wait_ge(o_done, n)
                    for t in range(CT):
                        last = nc.tensor.transpose(misc[:, t], o_sb[:, t * P:(t + 1) * P], ident[:])
                    last.then_inc(o_psum, 1)

                def scores(n, kt, p, s, qc):
                    if kt == 0 and p == 0:
                        pe.wait_ge(m_loaded, 16 * (n + 1))
                    pe.wait_ge(exp_done, 16 * n + 2 * kt + p + 1)
                    for head in (2 * p, 2 * p + 1):
                        last = nc.tensor.matmul(bps[p][:, head % 2], ks[s][:, head, kt * P:(kt + 1) * P],
                                                qs[s][:, head, qc * CW:(qc + 1) * CW], start=True, stop=True)
                    last.then_inc(b_scores, 1)

                def weigh_values(n, kt, p, s, turn):
                    if kt == 0 and p == 0:
                        pe.wait_ge(o_evacuated, n)
                        pe.wait_ge(v_loaded[s], 16 * (turn + 1))
                    pe.wait_ge(exp_done, 16 * n + 2 * kt + p + 3)
                    for head in (2 * p, 2 * p + 1):
                        last = nc.tensor.matmul(ops[32 * head:32 * head + VW], vs[s][:, kt, head], ex[kt % 2][p][:, head % 2],
                                                start=(kt == 0), stop=(kt == KT - 1))
                    last.then_inc(pv_done, 1)

                def body(g, turn, j):
                    known = isinstance(g, int)
                    s1 = (j + 1) % SETS
                    turn1 = turn + (j + 1) // SETS
                    for qc in range(2):
                        n = 2 * g + qc

                        def ahead(k):
                            if not (known and g + 1 >= GROUPS):
                                first_scores(n + 2, k, s1, turn1, qc)

                        for kt in range(KT):
                            scores(n, kt, 0, j, qc)
                            ahead(4 * kt)
                            scores(n, kt, 1, j, qc)
                            ahead(4 * kt + 1)
                            if kt:
                                for p in range(2):
                                    weigh_values(n, kt - 1, p, j, turn)
                            ahead(4 * kt + 2)
                            ahead(4 * kt + 3)
                            if kt == 1 and not (known and n + 1 >= UNITS):
                                transpose_max(n + 1)
                            if kt == 3:
                                transpose_out(n)
                        for p in range(2):
                            weigh_values(n, KT - 1, p, j, turn)

                pe.wait_ge(ones_made, SETS + 2)
                for a in range(2):
                    for k in range(AM):
                        first_scores(a, k, 0, 0, a)
                    if a == 0:
                        transpose_max(0)
                groups(pe, body)
                transpose_out(UNITS)

E8 = 8
MT = TILES + E8
F1 = 512
FK = F1 // P


def attention_out(nc, src_sb, attn, ident, eps_pow, w, logits, top, topi, gathered_in, load_vectors):
    with ExitStack() as ctx:
        kit = Kit(nc, ctx, "ao_")
        sb, ps, sem = kit.sb, kit.ps, kit.sem
        turnstile = sem("turnstile")
        wg, wo = sb("wg", [P, HALVES, D]), sb("wo", [P, HALVES, D])
        wr, br = sb("wr", [P, HALVES, E8]), sb("br", [P, E8])
        gb, n1g, n1b = sb("gb", [P, HALVES]), sb("n1g", [P, D]), sb("n1b", [P, D])
        gbh = sb("gbh", [P, HALVES])
        zero = sb("zero", [P, D])
        ao = sb("ao", [P, CT, D])
        outT, th, ogT = sb("outT", [P, HALVES, CW]), sb("th", [P, HALVES, CW]), sb("ogT", [P, HALVES, CW])
        y = sb("y", [P, CT, D])
        stats, mv = sb("stats", [P, CT, 6]), sb("mv", [P, CT, 2])
        var, rstd = sb("var", [P, CT]), sb("rstd", [P, CT])
        xr = sb("xr", [P, CT, D])
        xrT = sb("xrT", [P, HALVES, CW])
        tps, gps, yps, xps = (ps(n, [P, HALVES, CW]) for n in ("tps", "gps", "yps", "xps"))

        loaded, cleared, zero_made, gbh_made = sem("loaded"), sem("cleared"), sem("zero_made"), sem("gbh_made")
        ao_ready, outT_psum, outT_ready = sem("ao_ready"), sem("outT_psum"), sem("outT_ready")
        gate_psum, th_ready, og_ready, y_psum, y_ready = (sem("gate_psum"), sem("th_ready"), sem("og_ready"),
                                                          sem("y_psum"), sem("y_ready"))
        stats_done, ln_stats, var_done, rstd_ready = sem("stats_done"), sem("ln_stats"), sem("var_done"), sem("rstd_ready")
        yn_ready, yg_ready, xr_ready, src_ready = sem("yn_ready"), sem("yg_ready"), sem("xr_ready"), sem("src_ready")
        xrT_psum, xrT_ready, lg_psum, lg_ready, top_done = (
            sem("xrT_psum"), sem("xrT_ready"), sem("lg_psum"), sem("lg_ready"), sem("top_done"))

        def chunks(eng, body):
            body(0, True)
            with eng.Fori(1, CHUNKS - 1) as c:
                body(c, True)
            body(CHUNKS - 1, False)

        with nc.Block() as block:
            @block.sync
            def _(sp):
                for dst, name in ((wg, "gate_w"), (wo, "out_w"), (wr, "moe_gate_w")):
                    sp.dma_start(dst[:], w[name].rearrange("(k p) n -> p k n", p=P)).then_inc(loaded, 16)
                for dst, name in ((br, "moe_gate_b"), (n1g, "n1_g"), (n1b, "n1_b")):
                    sp.dma_start(dst[:], w[name].partition_broadcast(P)).then_inc(loaded, 16)
                sp.dma_start(gb[:], w["gate_b"]).then_inc(loaded, 16)
                load_vectors(sp)
                sp.wait_ge(zero_made, 1)
                sp.dma_start(gathered_in.rearrange("(k p) d -> p k d", p=P),
                             bc(zero[:], 1, [P, MT, D])).then_inc(cleared, 16)
                sp.wait_ge(cleared, 16)

            @block.gpsimd
            def _(pool):
                def body(c, more):
                    pool.wait_ge(ln_stats, CT * (c + 1))
                    nc.gpsimd.tensor_tensor(var[:], mv[:, :, 1], eps_pow[:, 0], ALU.add).then_inc(var_done, 1)
                    pool.wait_ge(var_done, c + 1)
                    if later(c, 1):
                        pool.wait_ge(yn_ready, CT * c)
                    nc.gpsimd.tensor_tensor(rstd[:], var[:], eps_pow[:, 1], ALU.pow).then_inc(rstd_ready, 1)
                    pool.wait_ge(yn_ready, CT * (c + 1))
                    nc.gpsimd.tensor_tensor(xr[:], xr[:], bc(n1g[:], 1, [P, CT, D]), ALU.mult).then_inc(yg_ready, 1)
                    pool.wait_ge(yg_ready, c + 1)
                    nc.gpsimd.tensor_tensor(xr[:], xr[:], bc(n1b[:], 1, [P, CT, D]), ALU.add).then_inc(xr_ready, 1)

                pool.wait_ge(loaded, 16 * 7)
                chunks(pool, body)

            @block.scalar
            def _(act):
                def copy_attention(c):
                    if later(c, 1):
                        act.wait_ge(outT_psum, c)
                    units = attn[:, ds(c + 6 * (c // 2) + 1, 7), :][:, 0:7:2, :]
                    nc.scalar.activation(ao[:].rearrange("p t (g x) -> p g t x", g=4),
                                         units.rearrange("p g (t x) -> p g t x", t=CT), ACT.Copy).then_inc(ao_ready, 1)

                def evacuate_outT(c):
                    act.wait_ge(outT_psum, c + 1)
                    if later(c, 1):
                        act.wait_ge(og_ready, c)
                    nc.scalar.activation(outT[:], tps[:], ACT.Copy).then_inc(outT_ready, 1)

                def gate(c):
                    act.wait_ge(gate_psum, c + 1)
                    for half in range(HALVES):
                        nc.scalar.activation(th[:, half], gps[:, half], ACT.Tanh, bias=gbh[:, half:half + 1],
                                             scale=0.5).then_inc(th_ready, 1)

                def keep_and_evacuate(c):
                    act.wait_ge(xr_ready, c + 1)
                    nc.scalar.activation(src_sb[:, ds(CT * c, CT), :], xr[:], ACT.Copy).then_inc(src_ready, 1)
                    act.wait_ge(xrT_psum, c + 1)
                    if later(c, 1):
                        act.wait_ge(lg_psum, c)
                    nc.scalar.activation(xrT[:], xps[:], ACT.Copy).then_inc(xrT_ready, 1)

                def body(c, more):
                    if more:
                        evacuate_outT(c + 1)
                    if later(c, 1):
                        keep_and_evacuate(c - 1)
                    if more:
                        gate(c + 1)
                    if more and (not isinstance(c, int) or c + 2 < CHUNKS):
                        copy_attention(c + 2)

                act.wait_ge(gbh_made, 1)
                copy_attention(0)
                evacuate_outT(0)
                copy_attention(1)
                gate(0)
                body(0, True)
                with act.Fori(1, CHUNKS - 2) as c:
                    body(c, True)
                body(CHUNKS - 2, True)
                body(CHUNKS - 1, False)
                keep_and_evacuate(CHUNKS - 1)

            @block.vector
            def _(dve):
                nc.vector.memset(zero[:], 0.0).then_inc(zero_made, 1)
                dve.wait_ge(loaded, 16 * 7)
                nc.vector.tensor_scalar(gbh[:], gb[:], 0.5, None, ALU.mult).then_inc(gbh_made, 1)

                def apply_gate(c):
                    dve.wait_ge(th_ready, 2 * (c + 1))
                    dve.wait_ge(outT_ready, c + 1)
                    if later(c, 1):
                        dve.wait_ge(y_psum, 2 * c)
                    nc.vector.scalar_tensor_tensor(out=ogT[:], in0=th[:], scalar=1.0, in1=outT[:], op0=ALU.add,
                                                   op1=ALU.mult).then_inc(og_ready, 1)

                def add_router_bias(c):
                    dve.wait_ge(lg_psum, c + 1)
                    nc.vector.tensor_tensor(logits[:, ds(CT * c, CT), :],
                                            xps[:, 0, 0:CT * E8].rearrange("p (t e) -> p t e", t=CT),
                                            bc(br[:], 1, [P, CT, E8]), ALU.add).then_inc(lg_ready, 1)

                def body(c, more):
                    for bank in range(2):
                        dve.wait_ge(y_psum, 2 * c + bank + 1)
                        nc.vector.scalar_tensor_tensor(
                            out=y[:, 2 * bank:2 * bank + 2], in0=yps[:, bank].rearrange("p (t d) -> p t d", t=2), scalar=0.5,
                            in1=src_sb[:, ds(CT * c + 2 * bank, 2), :], op0=ALU.mult, op1=ALU.add).then_inc(y_ready, 1)
                    for t in range(CT):
                        if t % 2 == 0:
                            dve.wait_ge(y_ready, 2 * c + t // 2 + 1)
                        nc.vector.bn_stats(stats[:, t], y[:, t]).then_inc(stats_done, 1)
                    passed(dve, stats_done, CT * (c + 1), turnstile)
                    for t in range(CT):
                        nc.vector.bn_aggr(mv[:, t], stats[:, t]).then_inc(ln_stats, 1)
                    if later(c, 1):
                        dve.wait_ge(src_ready, c)
                        dve.wait_ge(xrT_psum, c)
                    dve.wait_ge(rstd_ready, c + 1)
                    dve.wait_ge(ln_stats, CT * (c + 1))
                    for t in range(CT):
                        nc.vector.tensor_scalar(xr[:, t], y[:, t], mv[:, t, 0:1], rstd[:, t:t + 1], ALU.subtract,
                                                ALU.mult).then_inc(yn_ready, 1)
                    if later(c, 1):
                        add_router_bias(c - 1)
                    if more:
                        apply_gate(c + 1)

                apply_gate(0)
                chunks(dve, body)
                add_router_bias(CHUNKS - 1)
                dve.wait_ge(lg_ready, CHUNKS)
                for t in range(TILES):
                    nc.vector.max(out=top[:, t], in_=logits[:, t]).then_inc(top_done, 1)
                for t in range(TILES):
                    dve.wait_ge(top_done, t + 1)
                    nc.vector.max_index(out=topi[:, t], in_max=top[:, t], in_values=logits[:, t])

            @block.tensor
            def _(pe):
                def transpose_attention(c):
                    pe.wait_ge(ao_ready, c + 1)
                    if later(c, 1):
                        pe.wait_ge(outT_ready, c)
                    for t in range(CT):
                        for half in range(HALVES):
                            last = nc.tensor.transpose(tps[:, half, t * P:(t + 1) * P], ao[:, t, half * P:(half + 1) * P],
                                                       ident[:])
                    last.then_inc(outT_psum, 1)

                def gate(c):
                    pe.wait_ge(outT_ready, c + 1)
                    if later(c, 1):
                        pe.wait_ge(th_ready, 2 * c)
                    for half in range(HALVES):
                        for k in range(HALVES):
                            last = nc.tensor.matmul(gps[:, half], wg[:, k, half * P:(half + 1) * P], outT[:, k],
                                                    start=(k == 0), stop=(k == HALVES - 1))
                    last.then_inc(gate_psum, 1)

                def project(c):
                    pe.wait_ge(og_ready, c + 1)
                    if later(c, 1):
                        pe.wait_ge(y_ready, 2 * c)
                    for bank in range(2):
                        for t in (2 * bank, 2 * bank + 1):
                            for k in range(HALVES):
                                last = nc.tensor.matmul(yps[:, bank, (t % 2) * D:(t % 2 + 1) * D],
                                                        ogT[:, k, t * P:(t + 1) * P], wo[:, k],
                                                        start=(k == 0), stop=(k == HALVES - 1))
                        last.then_inc(y_psum, 1)

                def transpose_xr(c):
                    pe.wait_ge(xr_ready, c + 1)
                    if later(c, 1):
                        pe.wait_ge(lg_ready, c)
                    for t in range(CT):
                        for half in range(HALVES):
                            last = nc.tensor.transpose(xps[:, half, t * P:(t + 1) * P], xr[:, t, half * P:(half + 1) * P],
                                                       ident[:])
                    last.then_inc(xrT_psum, 1)

                def route(c):
                    pe.wait_ge(xrT_ready, c + 1)
                    for t in range(CT):
                        for k in range(HALVES):
                            last = nc.tensor.matmul(xps[:, 0, t * E8:(t + 1) * E8], xrT[:, k, t * P:(t + 1) * P], wr[:, k],
                                                    start=(k == 0), stop=(k == HALVES - 1))
                    last.then_inc(lg_psum, 1)

                def body(c, more):
                    if more:
                        transpose_attention(c + 1)
                    project(c)
                    if later(c, 1):
                        transpose_xr(c - 1)
                    if more:
                        gate(c + 1)
                    if later(c, 1):
                        route(c - 1)

                pe.wait_ge(loaded, 16 * 7)
                transpose_attention(0)
                gate(0)
                chunks(pe, body)
                transpose_xr(CHUNKS - 1)
                route(CHUNKS - 1)


def make_prefix(nc, kit, tri, ones):
    return dict(pre=kit.ps("prefix", [P, TILES * E8]), tot=kit.ps("totals", [P, TILES * E8]),
                tot_sb=kit.sb("tot_sb", [P, TILES, E8]), incl=kit.sb("incl", [P, TILES, E8]),
                one=kit.sb("one", [P, TILES]), tri=tri, ones=ones)


def prefix_products(nc, pe, pf, marks, done):
    nc.tensor.matmul(pf["pre"][:], pf["tri"][:], marks[:].rearrange("p t e -> p (t e)"), start=True, stop=True)
    nc.tensor.matmul(pf["tot"][:], pf["ones"][:], marks[:].rearrange("p t e -> p (t e)"), start=True,
                     stop=True).then_inc(done, 1)


def route_tokens(nc, w, src_sb, logits, top, topi, tri, ones, wsum, slot_i, tile_expert, gathered_in,
                 load_weights):
    with ExitStack() as ctx:
        kit = Kit(nc, ctx, "rt_")
        sb, sem = kit.sb, kit.sem
        turnstile = sem("turnstile")
        pf = make_prefix(nc, kit, tri, ones)
        chosen = sb("chosen", [P, TILES])
        iota8 = sb("iota8", [P, E8])
        mark, markb = sb("mark", [P, TILES, E8]), sb("markb", [P, TILES, E8], bf16)
        rank = sb("rank", [P, TILES, E8])
        count_i, tiles, end, start = sb("count_i", [P, E8], i32), sb("tiles", [P, E8]), sb("end", [P, E8]), sb("start", [P, E8])
        delta, total = sb("delta", [P, TILES]), sb("total", [P, TILES])
        slot = sb("slot", [P, TILES])
        iotam = sb("iotam", [1, MT])
        past = sb("past", [1, MT, E8])
        texp = sb("texp", [1, MT])
        iota_made, step, marks_ready, products = sem("iota_made"), sem("step"), sem("marks_ready"), sem("products")
        delta_ready, exp_ready, slots_ready, scattered = sem("delta_ready"), sem("exp_ready"), sem("slots_ready"), sem("scattered")

        with nc.Block() as block:
            @block.sync
            def _(sp):
                load_weights(sp)

            @block.gpsimd
            def _(pool):
                nc.gpsimd.iota(iota8[:], [[1, E8]], base=0, channel_multiplier=0,
                               allow_small_or_imprecise_dtypes=True).then_inc(iota_made, 1)
                pool.wait_ge(iota_made, 1)
                nc.gpsimd.iota(iotam[:], [[1, MT]], base=0, channel_multiplier=0,
                               allow_small_or_imprecise_dtypes=True).then_inc(iota_made, 1)
                pool.wait_ge(slots_ready, 1)
                for t in range(TILES):
                    pool.indirect_dma_start(out=gathered_in, out_offset=bass.IndirectOffsetOnAxis(ap=slot_i[:, t:t + 1], axis=0),
                                            in_=src_sb[:, t, :], in_offset=None).then_inc(scattered, 16)
                pool.wait_ge(scattered, 16 * TILES)

            @block.scalar
            def _(act):
                act.wait_ge(delta_ready, 1)
                nc.scalar.activation(delta[:], delta[:], ACT.Exp).then_inc(exp_ready, 1)

            @block.tensor
            def _(pe):
                pe.wait_ge(marks_ready, 1)
                prefix_products(nc, pe, pf, markb, products)

            @block.vector
            def _(dve):
                at = [0]

                def link(instruction):
                    at[0] += 1
                    instruction.then_inc(step, 1)
                    dve.wait_ge(step, at[0])

                nc.vector.tensor_tensor(delta[:], top[:, :, 1], top[:, :, 0], ALU.subtract).then_inc(delta_ready, 1)
                link(nc.vector.tensor_tensor(chosen[:], topi[:, :, 0], topi[:, :, 1], ALU.max))
                dve.wait_ge(iota_made, 2)
                link(nc.vector.tensor_tensor(mark[:], bc(chosen[:], 2, [P, TILES, E8]), bc(iota8[:], 1, [P, TILES, E8]),
                                             ALU.is_equal))
                nc.vector.tensor_copy(markb[:], mark[:]).then_inc(marks_ready, 1)
                link(nc.vector.memset(pf["one"][:], 1.0))
                dve.wait_ge(products, 1)
                link(nc.vector.tensor_copy(pf["tot_sb"][:], pf["tot"][:].rearrange("p (t e) -> p t e", e=E8)))
                for e in range(E8):
                    last = nc.vector.tensor_tensor_scan(pf["incl"][:, :, e], pf["one"][:], pf["tot_sb"][:, :, e], 0.0,
                                                        ALU.mult, ALU.add)
                    link(last)
                link(nc.vector.tensor_tensor(rank[:], pf["pre"][:].rearrange("p (t e) -> p t e", e=E8), pf["incl"][:], ALU.add))
                link(nc.vector.tensor_tensor(rank[:], rank[:], pf["tot_sb"][:], ALU.subtract))
                link(nc.vector.tensor_scalar(count_i[:], pf["incl"][:, TILES - 1], float(P - 1), None, ALU.add))
                link(nc.vector.tensor_scalar(count_i[:], count_i[:], 7, None, ALU.arith_shift_right))
                link(nc.vector.tensor_copy(tiles[:], count_i[:]))
                link(nc.vector.tensor_tensor_scan(end[:], pf["one"][:, 0:E8], tiles[:], 0.0, ALU.mult, ALU.add))
                link(nc.vector.tensor_tensor(start[:], end[:], tiles[:], ALU.subtract))
                link(nc.vector.tensor_scalar(start[:], start[:], float(P), None, ALU.mult))
                link(nc.vector.tensor_tensor(rank[:], rank[:], bc(start[:], 1, [P, TILES, E8]), ALU.add))
                link(nc.vector.tensor_tensor(rank[:], rank[:], mark[:], ALU.mult))
                link(nc.vector.tensor_reduce(slot[:], rank[:], axis=X, op=ALU.add))
                nc.vector.tensor_copy(slot_i[:], slot[:]).then_inc(slots_ready, 1)
                link(nc.vector.tensor_tensor(past[:], bc(iotam[:], 2, [1, MT, E8]), bc(end[0:1, :], 1, [1, MT, E8]), ALU.is_ge))
                link(nc.vector.tensor_reduce(texp[:], past[:], axis=X, op=ALU.add))
                link(nc.vector.tensor_scalar(tile_expert[:], texp[:], float(E8 - 1), None, ALU.min))
                dve.wait_ge(exp_ready, 1)
                link(nc.vector.tensor_scalar(total[:], delta[:], 1.0, None, ALU.add))
                link(nc.vector.reciprocal(total[:], total[:]))
                link(nc.vector.tensor_tensor(delta[:], delta[:], total[:], ALU.mult))
                link(nc.vector.tensor_tensor(wsum[:], delta[:], total[:], ALU.add))


def expert_tiles(nc, ident, eps_pow, w, ew, spent, tile_expert, gathered_in, gathered_out):
    U, AHEAD = 4, 3
    with ExitStack() as ctx:
        kit = Kit(nc, ctx, "ex_")
        sb, ps, sem = kit.sb, kit.ps, kit.sem
        turnstile = sem("turnstile")
        xg = [b[:].rearrange("p t e -> p (t e)") for b in spent] + [sb(f"xg{i}", [P, D]) for i in range(len(spent), U)]
        xb = [sb(f"xb{i}", [P, D]) for i in range(U)]
        xT = [sb(f"xT{i}", [P, HALVES, P]) for i in range(2)]
        hb = [sb(f"hb{i}", [P, F1]) for i in range(U)]
        stats, mv = sb("stats", [P, 2, 6]), sb("mv", [P, 2, 2])
        var, rstd = sb("var", [P, 2]), sb("rstd", [P, 2])
        hT = [sb(f"hT{i}", [P, FK, P]) for i in range(2)]
        xps = [ps(f"xps{i}", [P, F1]) for i in range(2)]
        hps = [ps(f"hps{i}", [P, F1]) for i in range(2)]
        tps = [ps(f"tps{i}", [P, F1]) for i in range(2)]
        yps = [ps(f"yps{i}", [P, F1]) for i in range(2)]
        x_loaded = [sem(f"x_loaded{i}") for i in range(U)]
        y_stored = [sem(f"y_stored{i}") for i in range(U)]
        xT_psum, xT_ready, h_psum, hb_ready, stats_done, ln_stats = (sem("xT_psum"), sem("xT_ready"), sem("h_psum"),
                                                                     sem("hb_ready"), sem("stats_done"), sem("ln_stats"))
        var_done, rstd_ready, hn_ready = sem("var_done"), sem("rstd_ready"), sem("hn_ready")
        hT_psum, hT_ready, y_psum, xb_ready, y_ready = (sem("hT_psum"), sem("hT_ready"), sem("y_psum"), sem("xb_ready"),
                                                        sem("y_ready"))

        def turns(eng, body):
            for j in range(U):
                body(j, 0, j, True)
            with eng.Fori(1, MT // U - 1) as i:
                for j in range(U):
                    body(i * U + j, i, j, True)
            for j in range(U):
                body(MT - U + j, MT // U - 1, j, j + AHEAD < U)

        def expert(eng, k):
            return eng.value_load(tile_expert[0:1, ds(k, 1)], min_val=0, max_val=E8 - 1)

        with nc.Block() as block:
            @block.sync
            def _(sp):
                def load(k, j):
                    sp.dma_start(xg[j][:], gathered_in[ds(P * k, P), :]).then_inc(x_loaded[j], 16)

                def body(k, turn, j, ahead):
                    if ahead:
                        if later(k, 1):
                            passed(sp, xb_ready, k + 2, turnstile)
                            passed(sp, xT_psum, k, turnstile)
                        load(k + AHEAD, (j + AHEAD) % U)

                for k in range(AHEAD):
                    load(k, k)
                turns(sp, body)
                for i in range(U):
                    sp.wait_ge(y_stored[i], 16 * (MT // U))

            @block.tensor
            def _(pe):
                def transpose_x(k, turn, j):
                    pe.wait_ge(x_loaded[j], 16 * (turn + 1))
                    if later(k, 2):
                        pe.wait_ge(xT_ready, k - 1)
                    for half in range(HALVES):
                        last = nc.tensor.transpose(xps[j % 2][:, half * P:(half + 1) * P], xg[j][:, half * P:(half + 1) * P],
                                                   ident[:])
                    last.then_inc(xT_psum, 1)

                def hidden(k, j):
                    e = expert(pe, k)
                    pe.wait_ge(xT_ready, k + 1)
                    if later(k, 2):
                        pe.wait_ge(hb_ready, k - 1)
                    for half in range(HALVES):
                        last = nc.tensor.matmul(hps[j % 2][:], xT[j % 2][:, half], ew["w1"][:, half, ds(e, 1), :],
                                                start=(half == 0), stop=(half == HALVES - 1))
                    last.then_inc(h_psum, 1)

                def body(k, turn, j, ahead):
                    if ahead:
                        transpose_x(k + AHEAD, turn + (j + AHEAD) // U, (j + AHEAD) % U)
                    pe.wait_ge(hn_ready, k + 1)
                    if later(k, 2):
                        pe.wait_ge(hT_ready, k - 1)
                    for f in range(FK):
                        last = nc.tensor.transpose(tps[j % 2][:, f * P:(f + 1) * P], hb[j][:, f * P:(f + 1) * P], ident[:])
                    last.then_inc(hT_psum, 1)
                    if ahead:
                        hidden(k + AHEAD, (j + AHEAD) % U)
                    e = expert(pe, k)
                    pe.wait_ge(hT_ready, k + 1)
                    pe.wait_ge(y_ready, k + 1)
                    for f in range(FK):
                        last = nc.tensor.matmul(yps[j % 2][:, 0:D], hT[j % 2][:, f], ew["w2"][:, f, ds(e, 1), :],
                                                start=(f == 0), stop=(f == FK - 1))
                    last.then_inc(y_psum, 1)

                pe.wait_ge(ew["w_loaded"], ew["w_count"])
                for k in range(AHEAD):
                    transpose_x(k, 0, k)
                    hidden(k, k)
                turns(pe, body)

            @block.scalar
            def _(act):
                def evacuate_xT(k, j):
                    act.wait_ge(xT_psum, k + 1)
                    if later(k, 2):
                        act.wait_ge(h_psum, k - 1)
                    nc.scalar.activation(xT[j % 2][:].rearrange("p k t -> p (k t)"), xps[j % 2][:, 0:D],
                                         ACT.Copy).then_inc(xT_ready, 1)

                def gelu(k, j):
                    e = expert(act, k)
                    act.wait_ge(hT_psum, k + 1)
                    if later(k, 2):
                        act.wait_ge(y_psum, k - 1)
                    for f in range(FK):
                        last = nc.scalar.activation(hT[j % 2][:, f], tps[j % 2][:, f * P:(f + 1) * P], ACT.Gelu,
                                                    bias=ew["bt"][:, f, ds(e, 1)], scale=ew["g"][:, f, ds(e, 1)])
                    last.then_inc(hT_ready, 1)

                def store(k, j):
                    act.wait_ge(y_ready, k + 3)
                    act.dma_start(gathered_out[ds(P * k, P), :], xb[j][:]).then_inc(y_stored[j], 16)

                def body(k, turn, j, ahead):
                    if ahead:
                        evacuate_xT(k + AHEAD, (j + AHEAD) % U)
                    gelu(k, j)
                    if later(k, 2):
                        store(k - 2, (j - 2) % U)

                for k in range(AHEAD):
                    evacuate_xT(k, k)
                act.wait_ge(ew["b_loaded"], ew["b_count"])
                turns(act, body)
                for k in (MT - 2, MT - 1):
                    store(k, k % U)

            @block.vector
            def _(dve):
                def add_b1(k, j, e):
                    dve.wait_ge(h_psum, k + 1)
                    nc.vector.tensor_tensor(hb[j][:], hps[j % 2][:], ew["b1"][:, ds(e, 1), :].rearrange("p o f -> p (o f)"),
                                            ALU.add).then_inc(hb_ready, 1)
                    dve.wait_ge(hb_ready, k + 1)
                    nc.vector.bn_stats(stats[:, j % 2], hb[j][:]).then_inc(stats_done, 1)
                    passed(dve, stats_done, k + 1, turnstile)
                    nc.vector.bn_aggr(mv[:, j % 2], stats[:, j % 2]).then_inc(ln_stats, 1)

                def apply_norm(k, j):
                    dve.wait_ge(rstd_ready, k + 1)
                    nc.vector.tensor_scalar(hb[j][:], hb[j][:], mv[:, j % 2, 0:1], rstd[:, j % 2:j % 2 + 1], ALU.subtract,
                                            ALU.mult).then_inc(hn_ready, 1)

                def finish(k, j):
                    e = expert(dve, k)
                    dve.wait_ge(y_psum, k + 1)
                    dve.wait_ge(xb_ready, k + 3)
                    nc.vector.scalar_tensor_tensor(out=xb[j][:], in0=yps[j % 2][:, 0:D], scalar=ew["rs"][:, ds(e, 1)],
                                                   in1=xb[j][:], op0=ALU.mult, op1=ALU.add).then_inc(y_ready, 1)

                def body(k, turn, j, ahead):
                    if ahead:
                        add_b1(k + AHEAD, (j + AHEAD) % U, expert(dve, k + AHEAD))
                    if later(k, 1):
                        finish(k - 1, (j - 1) % U)
                    if ahead:
                        apply_norm(k + AHEAD, (j + AHEAD) % U)

                dve.wait_ge(ew["b_loaded"], ew["b_count"])
                nc.vector.tensor_tensor(ew["b2"][:], ew["b2"][:], bc(ew["rs"][:], 2, [P, E8, D]), ALU.mult).then_inc(ew["b2_scaled"], 1)
                dve.wait_ge(ew["b2_scaled"], 1)
                nc.vector.memset(var[:], 0.0).then_inc(xb_ready, 2)
                nc.vector.memset(rstd[:], 0.0).then_inc(y_ready, 2)
                for k in range(AHEAD):
                    add_b1(k, k, expert(dve, k))
                    apply_norm(k, k)
                turns(dve, body)
                finish(MT - 1, (MT - 1) % U)

            @block.gpsimd
            def _(pool):
                def make_rstd(k, j):
                    par = slice(j % 2, j % 2 + 1)
                    pool.wait_ge(ln_stats, k + 1)
                    nc.gpsimd.tensor_tensor(var[:, par], mv[:, j % 2, 1:2], eps_pow[:, 0, 0:1], ALU.add).then_inc(var_done, 1)
                    pool.wait_ge(var_done, k + 1)
                    nc.gpsimd.tensor_tensor(rstd[:, par], var[:, par], eps_pow[:, 1, 0:1], ALU.pow).then_inc(rstd_ready, 1)

                def add_b2(k, turn, j):
                    e = expert(pool, k)
                    pool.wait_ge(x_loaded[j], 16 * (turn + 1))
                    if later(k, U):
                        pool.wait_ge(y_stored[j], 16 * turn)
                    nc.gpsimd.tensor_tensor(xb[j][:], xg[j][:], ew["b2"][:, ds(e, 1), :].rearrange("p o f -> p (o f)"),
                                            ALU.add).then_inc(xb_ready, 1)

                def body(k, turn, j, ahead):
                    if not isinstance(k, int) or k + 1 < MT:
                        add_b2(k + 1, turn + (j + 1) // U, (j + 1) % U)
                    if ahead:
                        make_rstd(k + AHEAD, (j + AHEAD) % U)

                pool.wait_ge(ew["b2_scaled"], 1)
                pool.wait_ge(y_ready, 2)
                pool.wait_ge(xb_ready, 2)
                add_b2(0, 0, 0)
                for k in range(AHEAD):
                    make_rstd(k, k)
                turns(pool, body)


def combine_experts(nc, x_sb, src_sb, eps_pow, w, wsum, slot_i, gathered_out):
    with ExitStack() as ctx:
        kit = Kit(nc, ctx, "co_")
        sb, sem = kit.sb, kit.sem
        n2g, n2b = sb("n2g", [P, D]), sb("n2b", [P, D])
        yg = sb("yg", [P, TILES, D])
        z = [sb(f"z{i}", [P, CT, D]) for i in range(2)]
        stats, mv = sb("stats", [P, CT, 6]), sb("mv", [P, CT, 2])
        var, rstd = sb("var", [P, CT]), sb("rstd", [P, CT])
        loaded, z_ready, stats_done, ln_stats = sem("loaded"), sem("z_ready"), sem("stats_done"), sem("ln_stats")
        gathered = [sem(f"gathered{c}") for c in range(CHUNKS)]
        var_done, rstd_ready, zn_ready, zg_ready, x_biased, x_done = (sem("var_done"), sem("rstd_ready"), sem("zn_ready"),
                                                                      sem("zg_ready"), sem("x_biased"), sem("x_done"))
        with nc.Block() as block:
            @block.sync
            def _(sp):
                sp.dma_start(n2g[:], w["n2_g"].partition_broadcast(P)).then_inc(loaded, 16)
                sp.dma_start(n2b[:], w["n2_b"].partition_broadcast(P)).then_inc(loaded, 16)

            @block.gpsimd
            def _(pool):
                def gather(c):
                    for t in range(CT * c, CT * (c + 1)):
                        pool.indirect_dma_start(out=yg[:, t, :], out_offset=None, in_=gathered_out,
                                                in_offset=bass.IndirectOffsetOnAxis(ap=slot_i[:, t:t + 1], axis=0)
                                                ).then_inc(gathered[c], 16)

                gather(0)
                gather(1)
                pool.wait_ge(loaded, 32)
                for c in range(CHUNKS):
                    pool.wait_ge(ln_stats, CT * (c + 1))
                    nc.gpsimd.tensor_tensor(var[:], mv[:, :, 1], eps_pow[:, 0], ALU.add).then_inc(var_done, 1)
                    pool.wait_ge(var_done, c + 1)
                    nc.gpsimd.tensor_tensor(rstd[:], var[:], eps_pow[:, 1], ALU.pow).then_inc(rstd_ready, 1)
                    if c + 2 < CHUNKS:
                        gather(c + 2)
                    pool.wait_ge(zn_ready, CT * (c + 1))
                    nc.gpsimd.tensor_tensor(z[c % 2][:], z[c % 2][:], bc(n2g[:], 1, [P, CT, D]), ALU.mult).then_inc(zg_ready, 1)

            @block.vector
            def _(dve):
                def moments(c):
                    dve.wait_ge(gathered[c], 16 * CT)
                    if c >= 2:
                        dve.wait_ge(x_done, c - 1)
                    for t in range(CT):
                        nc.vector.scalar_tensor_tensor(out=z[c % 2][:, t], in0=yg[:, CT * c + t],
                                                       scalar=wsum[:, CT * c + t:CT * c + t + 1], in1=src_sb[:, CT * c + t],
                                                       op0=ALU.mult, op1=ALU.add).then_inc(z_ready, 1)
                    for t in range(CT):
                        dve.wait_ge(z_ready, CT * c + t + 1)
                        nc.vector.bn_stats(stats[:, t], z[c % 2][:, t]).then_inc(stats_done, 1)
                    for t in range(CT):
                        dve.wait_ge(stats_done, CT * c + t + 1)
                        nc.vector.bn_aggr(mv[:, t], stats[:, t]).then_inc(ln_stats, 1)

                dve.wait_ge(loaded, 32)
                moments(0)
                for c in range(CHUNKS):
                    xs = x_sb[:, CT * c:CT * (c + 1), :]
                    nc.vector.tensor_tensor(xs, xs, bc(n2b[:], 1, [P, CT, D]), ALU.add).then_inc(x_biased, 1)
                    dve.wait_ge(rstd_ready, c + 1)
                    dve.wait_ge(ln_stats, CT * (c + 1))
                    for t in range(CT):
                        nc.vector.tensor_scalar(z[c % 2][:, t], z[c % 2][:, t], mv[:, t, 0:1], rstd[:, t:t + 1], ALU.subtract,
                                                ALU.mult).then_inc(zn_ready, 1)
                    if c + 1 < CHUNKS:
                        dve.wait_ge(zn_ready, CT * (c + 1))
                        moments(c + 1)
                    dve.wait_ge(zg_ready, c + 1)
                    dve.wait_ge(x_biased, c + 1)
                    nc.vector.tensor_tensor(xs, xs, z[c % 2][:], ALU.add).then_inc(x_done, 1)


def make_constants(nc, kit):
    sb, made = kit.sb, kit.sem("constants_made")
    k = dict(ident=sb("ident", [P, P]), eps_pow=sb("eps_pow", [P, 2, CT]), headmask=sb("headmask", [P, HH]),
             trif=sb("trif", [P, P]), tri=sb("tri", [P, P], bf16), ones=sb("ones", [P, P], bf16))

    with nc.Block() as block:
        @block.gpsimd
        def _(pool):
            steps = [0]

            def link(instruction):
                steps[0] += 1
                instruction.then_inc(made, 1)
                pool.wait_ge(made, steps[0])

            link(nc.gpsimd.memset(k["eps_pow"][:, 0], EPS))
            link(nc.gpsimd.memset(k["eps_pow"][:, 1], -0.5))
            link(nc.gpsimd.memset(k["ident"][:], 0.0))
            link(nc.gpsimd.affine_select(out=k["ident"][:], in_=k["ident"][:], compare_op=ALU.not_equal, fill=1.0, base=0,
                                         pattern=[[-1, P]], channel_multiplier=1))
            link(nc.gpsimd.memset(k["headmask"][:], 1.0))
            link(nc.gpsimd.affine_select(out=k["headmask"][:], in_=k["headmask"][:], compare_op=ALU.is_ge, fill=0.0, base=0,
                                         pattern=[[-DK, HH]], channel_multiplier=1))
            link(nc.gpsimd.affine_select(out=k["headmask"][:], in_=k["headmask"][:], compare_op=ALU.is_ge, fill=0.0,
                                         base=DK - 1, pattern=[[DK, HH]], channel_multiplier=-1))
            link(nc.gpsimd.memset(k["trif"][:], 1.0))
            link(nc.gpsimd.affine_select(out=k["trif"][:], in_=k["trif"][:], compare_op=ALU.is_gt, fill=0.0, base=0,
                                         pattern=[[1, P]], channel_multiplier=-1))
            link(nc.gpsimd.tensor_copy(k["tri"][:], k["trif"][:]))
            link(nc.gpsimd.memset(k["ones"][:], 1.0))
    return k


def load_x(nc, kit, x_sb, x):
    loaded = kit.sem("x_loaded")
    with nc.Block() as block:
        @block.sync
        def _(sp):
            sp.dma_start(x_sb[:], x.rearrange("(t p) d -> p t d", p=P)).then_inc(loaded, 16)
            sp.wait_ge(loaded, 16)


def self_attention_moe(nc, kit, x_sb, k, w):
    q_parts = nc.dram_tensor("q_parts", (GROUPS, GH, KROWS, S), bf16, kind="Internal").ap()
    k_parts = nc.dram_tensor("k_parts", (GROUPS, GH, KROWS, S), bf16, kind="Internal").ap()
    v_dram = nc.dram_tensor("v_groups", (GROUPS, P, KT, GH * VW), fp32, kind="Internal").ap()
    m_dram = nc.dram_tensor("neg_maxima", (UNITS, MROWS, GH * CT, P), bf16, kind="Internal").ap()
    gathered_in = nc.dram_tensor("expert_in", (MT * P, D), fp32, kind="Internal").ap()
    gathered_out = nc.dram_tensor("expert_out", (MT * P, D), fp32, kind="Internal").ap()
    ident, eps_pow = k["ident"], k["eps_pow"]
    w = dict(w, headmask=k["headmask"])
    with ExitStack() as ctx:
        own = Kit(nc, ctx, "sm_")
        src_sb = own.sb("src", [P, TILES, D])
        self_projections(nc, x_sb, src_sb, ident, eps_pow, w, q_parts, k_parts, v_dram)
        wsum, slot_i = own.sb("wsum", [P, TILES]), own.sb("slot_i", [P, TILES], i32)
        tile_expert = own.sb("tile_expert", [1, MT], i32)
        logits, top = own.sb("logits", [P, TILES, E8]), own.sb("top", [P, TILES, E8])
        topi = own.sb("topi", [P, TILES, E8], u32)
        ew = dict(b1=own.sb("b1", [P, E8, F1]), b2=own.sb("b2", [P, E8, D]), rs=own.sb("rs", [P, E8]),
                  g=own.sb("g", [P, FK, E8]), bt=own.sb("bt", [P, FK, E8]), b_loaded=own.sem("b_loaded"), b2_scaled=own.sem("b2_scaled"))

        def issue(sp, loads, semaphore):
            for dst, source in loads:
                sp.dma_start(dst, source).then_inc(semaphore, 16)
            return 16 * len(loads)

        def load_vectors(sp):
            ew["b_count"] = issue(sp, [(ew["b1"][:].rearrange("p e f -> p (e f)"), w["b1"].partition_broadcast(P)),
                                      (ew["b2"][:].rearrange("p e f -> p (e f)"), w["b2"].partition_broadcast(P)),
                                      (ew["g"][:], w["ln_g"]), (ew["bt"][:], w["ln_b"]), (ew["rs"][:], w["res_scale"].partition_broadcast(P))], ew["b_loaded"])

        with ExitStack() as ctx2:
            attn = Kit(nc, ctx2, "at_").sb("attn", [P, UNITS + 1, CT * GH * DK])
            self_attention(nc, attn, ident, q_parts, k_parts, v_dram, m_dram)
            attention_out(nc, src_sb, attn, ident, eps_pow, w, logits, top, topi, gathered_in,
                          load_vectors)
        with ExitStack() as ctx2:
            ek = Kit(nc, ctx2, "ew_")
            ew.update(w1=ek.sb("w1", [P, HALVES, E8, F1]), w2=ek.sb("w2", [P, FK, E8, D]), w_loaded=ek.sem("w_loaded"))

            def load_weights(sp):
                loads = [(ew["w1"][:, half], w["w1"][:, half * P:(half + 1) * P, :].rearrange("e p f -> p e f"))
                         for half in range(HALVES)]
                loads += [(ew["w2"][:, f], w["w2"][:, f * P:(f + 1) * P, :].rearrange("e p d -> p e d")) for f in range(FK)]
                ew["w_count"] = issue(sp, loads, ew["w_loaded"])

            route_tokens(nc, w, src_sb, logits, top, topi, k["tri"], k["ones"], wsum, slot_i, tile_expert, gathered_in,
                         load_weights)
            expert_tiles(nc, ident, eps_pow, w, ew, (logits, top), tile_expert, gathered_in, gathered_out)
        combine_experts(nc, x_sb, src_sb, eps_pow, w, wsum, slot_i, gathered_out)

CAP = TOKENS // E8
CAPT = CAP // P
NV = 5


def token_scores(nc, x_sb, ident, eps_pow, w, sc, xn_dram, out):
    with ExitStack() as ctx:
        kit = Kit(nc, ctx, "ts_")
        sb, ps, sem = kit.sb, kit.ps, kit.sem
        turnstile = sem("turnstile")
        wg = sb("wg", [P, HALVES, E8])
        stats, mv = sb("stats", [P, CT, 6]), sb("mv", [P, CT, 2])
        var, rstd = sb("var", [P, CT]), sb("rstd", [P, CT])
        xn = [sb(f"xn{i}", [P, CT, D]) for i in range(2)]
        xnT = [sb(f"xnT{i}", [P, HALVES, CW]) for i in range(2)]
        tps = [ps(f"tps{i}", [P, HALVES, CW]) for i in range(2)]
        sps = [ps(f"sps{i}", [P, CW]) for i in range(2)]
        loaded, x_stored = sem("loaded"), sem("x_stored")
        xn_stored = [sem(f"xn_stored{i}") for i in range(2)]
        stats_done, ln_stats, var_done, rstd_ready = sem("stats_done"), sem("ln_stats"), sem("var_done"), sem("rstd_ready")
        xn_ready, xnT_psum, xnT_ready, s_psum, s_ready = (sem("xn_ready"), sem("xnT_psum"), sem("xnT_ready"), sem("s_psum"),
                                                          sem("s_ready"))

        def turns(eng, body):
            with eng.Fori(0, CHUNKS // 2) as i:
                for par in range(2):
                    body(i, par, 2 * i + par)

        with nc.Block() as block:
            @block.sync
            def _(sp):
                sp.dma_start(wg[:], w["Wg"].rearrange("(k p) e -> p k e", p=P)).then_inc(loaded, 16)
                sp.dma_start(out.rearrange("(t p) d -> p t d", p=P), x_sb[:]).then_inc(x_stored, 16)
                xv = xn_dram.rearrange("(t p) d -> p t d", p=P)

                def body(i, par, c):
                    sp.wait_ge(xn_ready, CT * (c + 1))
                    sp.dma_start(xv[:, ds(CT * c, CT), :], xn[par][:]).then_inc(xn_stored[par], 16)

                turns(sp, body)
                sp.wait_ge(x_stored, 16)
                for par in range(2):
                    sp.wait_ge(xn_stored[par], 16 * (CHUNKS // 2))

            @block.vector
            def _(dve):
                def moments(c):
                    for t in range(CT):
                        nc.vector.bn_stats(stats[:, t], x_sb[:, ds(CT * c + t, 1), :]).then_inc(stats_done, 1)
                    passed(dve, stats_done, CT * (c + 1), turnstile)
                    for t in range(CT):
                        nc.vector.bn_aggr(mv[:, t], stats[:, t]).then_inc(ln_stats, 1)

                def body(i, par, c):
                    moments(c)
                    dve.wait_ge(rstd_ready, c + 1)
                    dve.wait_ge(ln_stats, CT * (c + 1))
                    dve.wait_ge(xn_stored[par], 16 * i)
                    dve.wait_ge(xnT_psum, c)
                    for t in range(CT):
                        nc.vector.tensor_scalar(xn[par][:, t], x_sb[:, ds(CT * c + t, 1), :], mv[:, t, 0:1], rstd[:, t:t + 1],
                                                ALU.subtract, ALU.mult).then_inc(xn_ready, 1)

                turns(dve, body)

            @block.gpsimd
            def _(pool):
                def body(i, par, c):
                    pool.wait_ge(ln_stats, CT * (c + 1))
                    nc.gpsimd.tensor_tensor(var[:], mv[:, :, 1], eps_pow[:, 0], ALU.add).then_inc(var_done, 1)
                    pool.wait_ge(var_done, c + 1)
                    nc.gpsimd.tensor_tensor(rstd[:], var[:], eps_pow[:, 1], ALU.pow).then_inc(rstd_ready, 1)

                turns(pool, body)

            @block.scalar
            def _(act):
                def body(i, par, c):
                    act.wait_ge(xnT_psum, c + 1)
                    nc.scalar.activation(xnT[par][:], tps[par][:], ACT.Copy).then_inc(xnT_ready, 1)
                    act.wait_ge(s_psum, c + 1)
                    nc.scalar.activation(sc[:, ds(CT * c, CT), :], sps[par][:, 0:CT * E8].rearrange("p (t e) -> p t e", t=CT),
                                         ACT.Copy).then_inc(s_ready, 1)

                turns(act, body)

            @block.tensor
            def _(pe):
                def body(i, par, c):
                    pe.wait_ge(xn_ready, CT * (c + 1))
                    for t in range(CT):
                        for half in range(HALVES):
                            last = nc.tensor.transpose(tps[par][:, half, t * P:(t + 1) * P],
                                                       xn[par][:, t, half * P:(half + 1) * P], ident[:])
                    last.then_inc(xnT_psum, 1)
                    pe.wait_ge(xnT_ready, c + 1)
                    pe.wait_ge(s_ready, c)
                    for t in range(CT):
                        for k in range(HALVES):
                            last = nc.tensor.matmul(sps[par][:, t * E8:(t + 1) * E8], xnT[par][:, k, t * P:(t + 1) * P],
                                                    wg[:, k], start=(k == 0), stop=(k == HALVES - 1))
                    last.then_inc(s_psum, 1)

                pe.wait_ge(loaded, 16)
                turns(pe, body)


def choose_tokens(nc, k, sc, idx, wt):
    BITS = 31
    with ExitStack() as ctx:
        kit = Kit(nc, ctx, "ct_")
        sb, sem = kit.sb, kit.sem
        turnstile = sem("turnstile")
        pf = make_prefix(nc, kit, k["tri"], k["ones"])
        cps, ips, zps = kit.ps("cps", [P, TILES * E8]), kit.ps("ips", [P, E8, CAPT, NV]), kit.ps("zps", [P, E8])
        ge = sb("ge", [P, TILES, E8], bf16)
        cnt = sb("cnt", [P, E8])
        met, key, flip, thr = (sb(n, [P, E8], i32) for n in ("met", "key", "flip", "thr"))
        onei, shift, bits = sb("onei", [P, BITS], i32), sb("shift", [P, BITS], i32), sb("bits", [P, BITS], i32)
        gt, eq = sb("gt", [P, TILES, E8]), sb("eq", [P, TILES, E8])
        sel, selb = sb("sel", [P, TILES, E8]), sb("selb", [P, TILES, E8], bf16)
        need, rank = sb("need", [P, E8]), sb("rank", [P, TILES, E8])
        rowmax, best = sb("rowmax", [P, E8]), sb("best", [P, E8])
        ex, rowsum, rz = sb("ex", [P, TILES, E8]), sb("rowsum", [P, E8]), sb("rz", [P, E8])
        onesf = sb("onesf", [P, P])
        slot_i, low_i, high_i = (sb(n, [P, TILES, E8], i32) for n in ("slot_i", "low_i", "high_i"))
        low, high = sb("low", [P, TILES, E8]), sb("high", [P, TILES, E8])
        iota4 = sb("iota4", [P, CAPT])
        iota128f, iota128 = sb("iota128f", [P, P]), sb("iota128", [P, P], bf16)
        val = sb("val", [P, TILES, E8, NV])
        part = sb("part", [P, TILES, E8], bf16)
        rest = sb("rest", [P, TILES, E8])
        hot4 = sb("hot4", [P, TILES, E8, CAPT])
        rhs = sb("rhs", [P, TILES, E8, CAPT, NV], bf16)
        GT = 8
        hot = [sb(f"hot{i}", [P, GT, P], bf16) for i in range(2)]
        got = sb("got", [P, E8, CAPT, NV])
        idf = sb("idf", [P, E8, CAPT])
        step, made, ge_ready, c_psum = sem("step"), sem("made"), sem("ge_ready"), sem("c_psum")
        rowmax_ready, best_ready, centered, exp_ready, rowsum_ready, z_psum = (
            sem("rowmax_ready"), sem("best_ready"), sem("centered"), sem("exp_ready"), sem("rowsum_ready"), sem("z_psum"))
        eqb_ready, selb_ready, products = sem("eqb_ready"), sem("selb_ready"), sem("products")
        rhs_ready, hot_ready, hot_used = sem("rhs_ready"), sem("hot_ready"), sem("hot_used")
        view = lambda b: b[:].rearrange("p t e -> p (t e)")
        per_expert = lambda b: bc(b[:], 1, [P, TILES, E8])
        SIGN = -2 ** 31

        with nc.Block() as block:
            @block.gpsimd
            def _(pool):
                n = [0]

                def link(instruction):
                    n[0] += 1
                    instruction.then_inc(made, 1)
                    pool.wait_ge(made, n[0])

                link(nc.gpsimd.iota(shift[:], [[-1, BITS]], base=BITS - 1, channel_multiplier=0))
                link(nc.gpsimd.iota(iota128f[:], [[1, P]], base=0, channel_multiplier=0, allow_small_or_imprecise_dtypes=True))
                link(nc.gpsimd.iota(iota4[:], [[1, CAPT]], base=0, channel_multiplier=0, allow_small_or_imprecise_dtypes=True))
                link(nc.gpsimd.iota(val[:, :, :, 0], [[1, TILES], [0, E8]], base=0, channel_multiplier=0,
                                    allow_small_or_imprecise_dtypes=True))
                link(nc.gpsimd.iota(val[:, :, :, 1], [[0, TILES], [0, E8]], base=0, channel_multiplier=1,
                                    allow_small_or_imprecise_dtypes=True))
                link(nc.gpsimd.memset(onesf[:], 1.0))
                pool.wait_ge(rowmax_ready, 1)
                nc.gpsimd.partition_all_reduce(best[:], rowmax[:], P, bass.bass_isa.ReduceOp.max).then_inc(best_ready, 1)

            @block.scalar
            def _(act):
                act.wait_ge(centered, 1)
                nc.scalar.activation(ex[:], ex[:], ACT.Exp).then_inc(exp_ready, 1)

            @block.tensor
            def _(pe):
                def count(value):
                    pe.wait_ge(ge_ready, value)
                    nc.tensor.matmul(cps[:], k["ones"][:], view(ge), start=True, stop=True).then_inc(c_psum, 1)

                count(1)
                with pe.Fori(0, BITS) as i:
                    count(i + 2)
                count(BITS + 2)
                pe.wait_ge(eqb_ready, 1)
                prefix_products(nc, pe, pf, selb, products)
                pe.wait_ge(selb_ready, 1)
                prefix_products(nc, pe, pf, selb, products)
                pe.wait_ge(rowsum_ready, 1)
                nc.tensor.matmul(zps[:], onesf[:], rowsum[:], start=True, stop=True).then_inc(z_psum, 1)
                pe.wait_ge(rhs_ready, 2)
                for e in range(E8):
                    for t in range(TILES):
                        n = e * TILES + t
                        if t % GT == 0:
                            pe.wait_ge(hot_ready, GT * (n // GT + 1))
                        last = nc.tensor.matmul(ips[:, e].rearrange("p a v -> p (a v)"), hot[n // GT % 2][:, t % GT],
                                                rhs[:, t, e].rearrange("p a v -> p (a v)"), start=(t == 0),
                                                stop=(t == TILES - 1))
                        if t % GT == GT - 1:
                            last.then_inc(hot_used, 1)

            @block.vector
            def _(dve):
                n = [0]

                def link(instruction):
                    n[0] += 1
                    instruction.then_inc(step, 1)
                    dve.wait_ge(step, n[0])

                def counted(done):
                    dve.wait_ge(c_psum, done)
                    return nc.vector.tensor_reduce(cnt[:], cps[:].rearrange("p (t e) -> p e t", e=E8), axis=X, op=ALU.add)

                nc.vector.tensor_reduce(rowmax[:], sc[:].rearrange("p t e -> p e t"), axis=X, op=ALU.max).then_inc(rowmax_ready, 1)
                nc.vector.tensor_scalar(ge[:], sc[:], 0.0, None, ALU.is_ge).then_inc(ge_ready, 1)
                dve.wait_ge(made, 6)
                link(nc.vector.memset(onei[:], 1))
                link(nc.vector.tensor_tensor(bits[:], onei[:], shift[:], ALU.logical_shift_left))
                link(nc.vector.tensor_copy(iota128[:], iota128f[:]))
                link(nc.vector.memset(pf["one"][:], 1.0))
                link(counted(1))
                link(nc.vector.tensor_scalar(met[:], cnt[:], float(CAP), -1.0, ALU.is_ge, ALU.mult))
                link(nc.vector.tensor_scalar(key[:], met[:], SIGN, None, ALU.bitwise_and))
                link(nc.vector.tensor_scalar(flip[:], met[:], -1, SIGN, ALU.bitwise_xor, ALU.bitwise_or))
                base = n[0]
                LINKS = 4
                with dve.Fori(0, BITS) as i:
                    bit = bits[:, ds(i, 1)]
                    at = base + LINKS * i
                    nc.vector.scalar_tensor_tensor(out=thr[:], in0=key[:], scalar=bit, in1=flip[:], op0=ALU.bitwise_or,
                                                   op1=ALU.bitwise_xor).then_inc(step, 1)
                    dve.wait_ge(step, at + 1)
                    nc.vector.tensor_tensor(ge[:], sc[:], per_expert(thr[:].bitcast(fp32)), ALU.is_ge).then_inc(ge_ready, 1)
                    counted(i + 2).then_inc(step, 1)
                    dve.wait_ge(step, at + 2)
                    nc.vector.tensor_scalar(met[:], cnt[:], float(CAP), -1.0, ALU.is_ge, ALU.mult).then_inc(step, 1)
                    dve.wait_ge(step, at + 3)
                    nc.vector.scalar_tensor_tensor(out=key[:], in0=met[:], scalar=bit, in1=key[:], op0=ALU.bitwise_and,
                                                   op1=ALU.bitwise_or).then_inc(step, 1)
                    dve.wait_ge(step, at + 4)
                n[0] = base + LINKS * BITS
                link(nc.vector.tensor_tensor(thr[:], key[:], flip[:], ALU.bitwise_xor))
                thrf = per_expert(thr[:].bitcast(fp32))
                nc.vector.tensor_tensor(ge[:], sc[:], thrf, ALU.is_gt).then_inc(ge_ready, 1)
                link(nc.vector.tensor_tensor(gt[:], sc[:], thrf, ALU.is_gt))
                link(nc.vector.tensor_tensor(eq[:], sc[:], thrf, ALU.is_equal))
                nc.vector.tensor_copy(selb[:], eq[:]).then_inc(eqb_ready, 1)
                link(counted(BITS + 2))
                link(nc.vector.tensor_scalar(need[:], cnt[:], -1.0, float(CAP), ALU.mult, ALU.add))

                def ranks(done):
                    dve.wait_ge(products, done)
                    link(nc.vector.tensor_copy(view(pf["tot_sb"]), pf["tot"][:]))
                    for e in range(E8):
                        link(nc.vector.tensor_tensor_scan(pf["incl"][:, :, e], pf["one"][:], pf["tot_sb"][:, :, e], 0.0,
                                                          ALU.mult, ALU.add))
                    link(nc.vector.tensor_tensor(rank[:], pf["pre"][:].rearrange("p (t e) -> p t e", e=E8), pf["incl"][:],
                                                 ALU.add))
                    link(nc.vector.tensor_tensor(rank[:], rank[:], pf["tot_sb"][:], ALU.subtract))

                ranks(1)
                link(nc.vector.tensor_tensor(rank[:], rank[:], per_expert(need), ALU.is_lt))
                link(nc.vector.tensor_tensor(rank[:], rank[:], eq[:], ALU.mult))
                link(nc.vector.tensor_tensor(sel[:], rank[:], gt[:], ALU.add))
                nc.vector.tensor_copy(selb[:], sel[:]).then_inc(selb_ready, 1)
                dve.wait_ge(best_ready, 1)
                nc.vector.tensor_tensor(ex[:], sc[:], per_expert(best), ALU.subtract).then_inc(centered, 1)
                ranks(2)
                dve.wait_ge(exp_ready, 1)
                link(nc.vector.tensor_tensor(ex[:], ex[:], sel[:], ALU.mult))
                nc.vector.tensor_reduce(rowsum[:], ex[:].rearrange("p t e -> p e t"), axis=X, op=ALU.add).then_inc(rowsum_ready, 1)
                link(nc.vector.tensor_copy(slot_i[:], rank[:]))
                link(nc.vector.tensor_scalar(low_i[:], slot_i[:], P - 1, None, ALU.bitwise_and))
                link(nc.vector.tensor_scalar(high_i[:], slot_i[:], 7, None, ALU.arith_shift_right))
                link(nc.vector.tensor_copy(high[:], high_i[:]))
                link(nc.vector.tensor_scalar(low[:], low_i[:], 1.0, None, ALU.add))
                link(nc.vector.tensor_tensor(low[:], low[:], sel[:], ALU.mult))
                link(nc.vector.tensor_scalar(low[:], low[:], 1.0, None, ALU.subtract))
                dve.wait_ge(z_psum, 1)
                link(nc.vector.reciprocal(rz[:], zps[:]))
                link(nc.vector.tensor_tensor(rest[:], ex[:], per_expert(rz), ALU.mult))
                for i in range(3):
                    link(nc.vector.tensor_copy(part[:], rest[:]))
                    link(nc.vector.tensor_copy(val[:, :, :, 2 + i], part[:]))
                    link(nc.vector.tensor_tensor(rest[:], rest[:], part[:], ALU.subtract))
                link(nc.vector.tensor_tensor(hot4[:], bc(high[:], 3, [P, TILES, E8, CAPT]),
                                             iota4[:].unsqueeze(1).unsqueeze(1).broadcast_to([P, TILES, E8, CAPT]), ALU.is_equal))
                h4 = hot4[:].rearrange("p t e a -> p (t e) a")
                v5 = val[:].rearrange("p t e v -> p (t e) v")
                r5 = rhs[:].rearrange("p t e a v -> p (t e) a v")
                TE = TILES * E8
                for part_of in range(2):
                    rows = slice(part_of * TE // 2, (part_of + 1) * TE // 2)
                    nc.vector.tensor_tensor(r5[:, rows], bc(h4[:, rows], 3, [P, TE // 2, CAPT, NV]),
                                            bc(v5[:, rows], 2, [P, TE // 2, CAPT, NV]), ALU.mult).then_inc(rhs_ready, 1)
                for e in range(E8):
                    for t in range(TILES):
                        m = e * TILES + t
                        if t % GT == 0 and m // GT >= 2:
                            dve.wait_ge(hot_used, m // GT - 1)
                        nc.vector.tensor_scalar(hot[m // GT % 2][:, t % GT], iota128[:], low[:, t, e:e + 1], None,
                                                ALU.is_equal).then_inc(hot_ready, 1)
                dve.wait_ge(hot_used, E8 * TILES // GT)
                link(nc.vector.tensor_copy(got[:], ips[:]))
                link(nc.vector.scalar_tensor_tensor(out=idf[:], in0=got[:, :, :, 0], scalar=float(P), in1=got[:, :, :, 1],
                                                    op0=ALU.mult, op1=ALU.add))
                link(nc.vector.tensor_copy(idx[:], idf[:]))
                link(nc.vector.tensor_tensor(wt[:], got[:, :, :, 2], got[:, :, :, 3], ALU.add))
                link(nc.vector.tensor_tensor(wt[:], wt[:], got[:, :, :, 4], ALU.add))


def swiglu_experts(nc, ident, w, idx, wt, xn_dram, out):
    with ExitStack() as ctx:
        kit = Kit(nc, ctx, "sw_")
        sb, ps, sem = kit.sb, kit.ps, kit.sem
        turnstile = sem("turnstile")
        w1 = [sb(f"w1{i}", [P, HALVES, F1]) for i in range(2)]
        w3 = [sb(f"w3{i}", [P, HALVES, F1]) for i in range(2)]
        w2 = [sb(f"w2{i}", [P, FK, D]) for i in range(2)]
        ids = [sb(f"ids{i}", [P, CAPT], i32) for i in range(2)]
        xg = [sb(f"xg{i}", [P, CAPT, D]) for i in range(2)]
        xT = sb("xT", [P, HALVES, CAP])
        act1 = [sb(f"act1{i}", [P, CAP]) for i in range(2)]
        hT = sb("hT", [P, FK, CAP])
        yo = [sb(f"yo{i}", [P, CAPT, D]) for i in range(2)]
        tps, yps = ps("tps", [P, HALVES, CAP]), ps("yps", [P, 2, CAP])
        p1 = [ps(f"p1{i}", [P, CAP]) for i in range(2)]
        p3 = [ps(f"p3{i}", [P, CAP]) for i in range(2)]
        w_loaded = [sem(f"w_loaded{i}") for i in range(2)]
        gathered = [sem(f"gathered{i}") for i in range(2)]
        ids_ready, scattered = sem("ids_ready"), sem("scattered")
        xT_psum, xT_ready, h_psum, silu_ready, h_ready = (sem("xT_psum"), sem("xT_ready"), sem("h_psum"), sem("silu_ready"),
                                                          sem("h_ready"))
        y_psum, y_ready = sem("y_psum"), sem("y_ready")

        def experts(eng, body):
            with eng.Fori(0, E8 // 2 - 1) as i:
                for par in range(2):
                    body(2 * i + par, i, par, False)
            for par in range(2):
                body(E8 - 2 + par, E8 // 2 - 1, par, par == 1)

        with nc.Block() as block:
            @block.sync
            def _(sp):
                def load(e, par):
                    for dst, name in ((w1, "W1"), (w3, "W3"), (w2, "W2")):
                        sp.dma_start(dst[par][:], w[name][ds(e, 1)].rearrange("e (k p) n -> p (e k) n", p=P)).then_inc(w_loaded[par], 16)

                def body(e, turn, par, last):
                    if not last:
                        sp.wait_ge(y_psum, 2 * e)
                        load(e + 1, (par + 1) % 2)

                load(0, 0)
                experts(sp, body)

            @block.gpsimd
            def _(pool):
                def gather(e, turn, par):
                    if later(e, 1):
                        pool.wait_ge(xT_psum, e - 1)
                        pool.wait_ge(scattered, 16 * CAPT * (e - 1))
                    nc.gpsimd.tensor_copy(ids[par][:], idx[:, ds(e, 1), :].rearrange("p o a -> p (o a)")).then_inc(ids_ready, 1)
                    passed(pool, ids_ready, e + 1, turnstile)
                    for a in range(CAPT):
                        pool.indirect_dma_start(out=xg[par][:, a, :], out_offset=None, in_=xn_dram,
                                                in_offset=bass.IndirectOffsetOnAxis(ap=ids[par][:, a:a + 1], axis=0)
                                                ).then_inc(gathered[par], 16)

                def body(e, turn, par, last):
                    if not last:
                        gather(e + 1, turn + (par + 1) // 2, (par + 1) % 2)
                    pool.wait_ge(y_ready, CAPT * (e + 1))
                    pool.wait_ge(scattered, 16 * CAPT * e)
                    passed(pool, y_ready, 1, turnstile)
                    for a in range(CAPT):
                        pool.indirect_dma_start(out=out, out_offset=bass.IndirectOffsetOnAxis(ap=ids[par][:, a:a + 1], axis=0),
                                                in_=yo[par][:, a, :], in_offset=None, compute_op=ALU.add).then_inc(scattered, 16)

                gather(0, 0, 0)
                experts(pool, body)
                pool.wait_ge(scattered, 16 * CAPT * E8)

            @block.tensor
            def _(pe):
                def transpose_x(e, turn, par):
                    pe.wait_ge(gathered[par], 16 * CAPT * (turn + 1))
                    for a in range(CAPT):
                        for half in range(HALVES):
                            last = nc.tensor.transpose(tps[:, half, a * P:(a + 1) * P], xg[par][:, a, half * P:(half + 1) * P],
                                                       ident[:])
                    last.then_inc(xT_psum, 1)

                def body(e, turn, par, final):
                    pe.wait_ge(w_loaded[par], 48 * (turn + 1))
                    pe.wait_ge(xT_ready, e + 1)
                    for f in range(FK):
                        pe.wait_ge(h_ready, FK * e + f + 1)
                        for wt_, bank in ((w1, p1), (w3, p3)):
                            for half in range(HALVES):
                                last = nc.tensor.matmul(bank[f % 2][:], wt_[par][:, half, f * P:(f + 1) * P], xT[:, half],
                                                        start=(half == 0), stop=(half == HALVES - 1))
                            last.then_inc(h_psum, 1)
                    if not final:
                        transpose_x(e + 1, turn + (par + 1) // 2, (par + 1) % 2)
                    pe.wait_ge(h_ready, FK * (e + 1) + 2)
                    pe.wait_ge(y_ready, CAPT * e)
                    for bank in range(2):
                        for a in (2 * bank, 2 * bank + 1):
                            for f in range(FK):
                                last = nc.tensor.matmul(yps[:, bank, (a % 2) * D:(a % 2 + 1) * D], hT[:, f, a * P:(a + 1) * P],
                                                        w2[par][:, f], start=(f == 0), stop=(f == FK - 1))
                        last.then_inc(y_psum, 1)

                transpose_x(0, 0, 0)
                experts(pe, body)

            @block.scalar
            def _(act):
                def evacuate_xT(e):
                    act.wait_ge(xT_psum, e + 1)
                    act.wait_ge(h_psum, 2 * FK * e)
                    nc.scalar.activation(xT[:], tps[:], ACT.Copy).then_inc(xT_ready, 1)

                def body(e, turn, par, last):
                    for f in range(FK):
                        act.wait_ge(h_psum, 2 * (FK * e + f) + 1)
                        act.wait_ge(h_ready, FK * e + f + 1)
                        nc.scalar.activation(act1[f % 2][:], p1[f % 2][:], ACT.Silu).then_inc(silu_ready, 1)
                    if not last:
                        evacuate_xT(e + 1)

                evacuate_xT(0)
                experts(act, body)

            @block.vector
            def _(dve):
                def body(e, turn, par, last):
                    dve.wait_ge(y_psum, 2 * e)
                    for f in range(FK):
                        dve.wait_ge(silu_ready, FK * e + f + 1)
                        dve.wait_ge(h_psum, 2 * (FK * e + f) + 2)
                        nc.vector.tensor_tensor(hT[:, f], p3[f % 2][:], act1[f % 2][:], ALU.mult).then_inc(h_ready, 1)
                    for a in range(CAPT):
                        dve.wait_ge(y_psum, 2 * e + a // 2 + 1)
                        nc.vector.tensor_scalar(yo[par][:, a], yps[:, a // 2, (a % 2) * D:(a % 2 + 1) * D],
                                                wt[:, ds(e, 1), a], None, ALU.mult).then_inc(y_ready, 1)

                nc.vector.memset(yo[0][:], 0.0).then_inc(h_ready, 2)
                experts(dve, body)


def token_choice_moe(nc, x_sb, k, w, out):
    xn_dram = nc.dram_tensor("normalized", (TOKENS, D), fp32, kind="Internal").ap()
    with ExitStack() as ctx:
        own = Kit(nc, ctx, "tc_")
        sc = own.sb("sc", [P, TILES, E8])
        idx, wt = own.sb("idx", [P, E8, CAPT], i32), own.sb("wt", [P, E8, CAPT])
        token_scores(nc, x_sb, k["ident"], k["eps_pow"], w, sc, xn_dram, out)
        choose_tokens(nc, k, sc, idx, wt)
        swiglu_experts(nc, k["ident"], w, idx, wt, xn_dram, out)


def decoder(nc, a, out):
    with ExitStack() as ctx:
        kit = Kit(nc, ctx, "x_")
        x_sb = kit.sb("x", [P, TILES, D])
        k = make_constants(nc, kit)
        load_x(nc, kit, x_sb, a["x"])
        of = lambda layer: {name[len(layer):]: ap for name, ap in a.items() if name.startswith(layer)}
        shared = dict(ctxT=a["ctxT"], mask=a["mask"])
        cross_attention(nc, x_sb, k["ident"], k["eps_pow"], dict(of("L0_xattn_"), **shared), "xa0", True)
        self_attention_moe(nc, kit, x_sb, k, of("L0_ffn_"))
        cross_attention(nc, x_sb, k["ident"], k["eps_pow"], dict(of("L1_xattn_"), **shared), "xa1", False)
        token_choice_moe(nc, x_sb, k, of("L1_ffn_"), out)



def kernel(**inputs):
    import numpy as np
    import concourse.bacc as bacc
    from concourse.bass_utils import run_bass_kernel_spmd

    def take(name):
        return np.asarray(inputs[name])

    def columns(v):
        return v.reshape(2, 128).T

    arrays = {"x": take("x").reshape(4096, 256), "ctxT": take("ctx_1024").transpose(2, 0, 1),
              "mask": take("mask_Bx1xSxS2_ik0").reshape(4096, 64)}
    for layer, transposed in (("L0_xattn_", True), ("L1_xattn_", False)):
        weights = [take(layer + "W" + n) for n in "qkvo"]
        arrays[layer + "wts"] = np.stack([m.T if transposed else m for m in weights])
        arrays[layer + "bqk"] = np.stack([columns(take(layer + "b" + n)) for n in "qk"], 1)
        arrays[layer + "bv"], arrays[layer + "bo"] = take(layer + "bv"), take(layer + "bo")
    f = "L0_ffn_"
    arrays[f + "ffn_qkv"] = np.stack([take(f + n + "_w") for n in "qkv"])
    for n in ("scale_w", "gate_b"):
        arrays[f + n] = columns(take(f + n))
    for n in ("gate_w", "out_w", "n1_g", "n1_b", "n2_g", "n2_b", "moe_gate_w", "moe_gate_b", "w1", "w2", "res_scale"):
        arrays[f + n] = take(f + n)
    for n in ("b1", "b2"):
        arrays[f + n] = take(f + n).reshape(-1)
    for n in ("ln_g", "ln_b"):
        arrays[f + n] = take(f + n).reshape(8, 4, 128).transpose(2, 1, 0)
    f = "L1_ffn_"
    arrays[f + "Wg"] = take(f + "Wg").T
    for n in ("W1", "W2", "W3"):
        arrays[f + n] = take(f + n).transpose(0, 2, 1)

    nc = bacc.Bacc("TRN2", target_bir_lowering=False, num_devices=1)
    feeds, aps = {}, {}
    for name, array in arrays.items():
        array = np.ascontiguousarray(array)
        feeds["in_" + name] = array
        aps[name] = nc.dram_tensor("in_" + name, array.shape, mybir.dt.from_np(array.dtype), kind="ExternalInput").ap()
    out = nc.dram_tensor("out_x", (4096, 256), fp32, kind="ExternalOutput").ap()
    decoder(nc, aps, out)
    result = run_bass_kernel_spmd(nc, [feeds], core_ids=[0])
    return result.results[0]["out_x"].reshape(4, 1024, 256)
```

```python
import concourse.bass as bass
from concourse import mybir
from contextlib import ExitStack

fp32 = mybir.dt.float32
bf16 = mybir.dt.bfloat16
i32 = mybir.dt.int32
u32 = mybir.dt.uint32
ALU = mybir.AluOpType
ACT = mybir.ActivationFunctionType
X = mybir.AxisListType.X
ds = bass.ds

P = 128
B, S, D = 4, 1024, 256
SC = 64
H = 16
DK = D // H
HALVES = D // P
TOKENS = B * S
TILES = TOKENS // P
CT = 4
CW = CT * P
CHUNKS = TOKENS // CW
HH = H // HALVES
EPS = 1e-5
FILL = -2.0 ** 60
SCALE = 1.0 / DK ** 0.5


class Kit:

    def __init__(self, nc, ctx, prefix):
        self.nc, self.ctx, self.prefix = nc, ctx, prefix
        self.numbers = []
        ctx.callback(self.clear_semaphores)

    def clear_semaphores(self):
        if not self.numbers:
            return
        with self.nc.Block() as block:
            @block.gpsimd
            def _(pool):
                first = 0
                for i, number in enumerate(self.numbers):
                    if i + 1 == len(self.numbers) or self.numbers[i + 1] != number + 1:
                        pool.sem_clear(range(self.numbers[first], number + 1))
                        first = i + 1

    def sb(self, name, shape, dt=fp32):
        return self.ctx.enter_context(self.nc.sbuf_tensor(self.prefix + name, shape, dt))

    def ps(self, name, shape):
        return self.ctx.enter_context(self.nc.psum_tensor(self.prefix + name, shape, fp32))

    def sem(self, name):
        semaphore = self.ctx.enter_context(self.nc.semaphore(self.prefix + name))
        self.numbers.append(semaphore.num)
        return semaphore


def bc(ap, axis, shape):
    return ap.unsqueeze(axis).broadcast_to(shape)


def later(k, first):
    return not isinstance(k, int) or k >= first


def passed(eng, semaphore, value, turnstile):
    eng.wait_ge(semaphore, value)
    eng.sem_inc(turnstile, 1)


class Context:

    def __init__(self, kit, w):
        self.w, self.loaded, self.issued = w, kit.sem("loaded"), False
        self.x_rest_loaded = None
        self.wts = kit.sb("wts", [P, 4, HALVES, D])
        self.ctxT = kit.sb("ctxT", [P, HALVES, B, 2, SC])
        self.bqk, self.bv, self.bo = kit.sb("bqk", [P, 2, HALVES]), kit.sb("bv", [P, D]), kit.sb("bo", [P, D])

    def issue(self, sp):
        w = self.w
        loads = [(self.wts[:], w["wts"].rearrange("f (k p) n -> p f k n", p=P))]
        loads += [(self.ctxT[:, k, :, twice, :], w["ctxT"][k * P:(k + 1) * P]) for twice in range(2) for k in range(HALVES)]
        loads += [(self.bqk[:], w["bqk"]), (self.bv[:], w["bv"].partition_broadcast(P)),
                  (self.bo[:], w["bo"].partition_broadcast(P))]
        for dst, source in loads:
            sp.dma_start(dst, source).then_inc(self.loaded, 16)
        self.issued, self.count = True, 16 * len(loads)


def cross_attention(nc, x_sb, ident, eps_pow, headmask, context, mask, name):
    masked, rest_loaded = mask is not None, context.x_rest_loaded
    wts, ctxT, bqk, bv, bo = context.wts, context.ctxT, context.bqk, context.bv, context.bo
    with ExitStack() as ctx:
        kit = Kit(nc, ctx, name + "_")
        sb, ps, sem = kit.sb, kit.ps, kit.sem
        turnstile = sem("turnstile")
        identb = sb("identb", [P, P], bf16)
        pairmask = sb("pairmask", [P, H // 2, 2, DK])
        kT = sb("kT", [P, HALVES, B, SC])
        kblk = sb("kblk", [P, B, HALVES, HH, SC])
        vblk = sb("vblk", [P, B, H // 2, 2, DK])
        vst = sb("vst", [P, D])
        if masked:
            mask_i = sb("mask_i", [P, TILES, SC], i32)
            fill = sb("fill", [P, TILES, SC], bf16)
        stats, mv = sb("stats", [P, CT, 6]), sb("mv", [P, CT, 2])
        var, rstd = sb("var", [P, CT]), sb("rstd", [P, CT])
        xn = sb("xn", [P, CT, D])
        xnT = sb("xnT", [P, HALVES, CW])
        qT = sb("qT", [P, HALVES, TOKENS])
        qst = sb("qst", [P, HALVES, CW])
        prob = sb("prob", [P, CT, H, SC])
        mx, den, rden = (sb(n, [P, CT, H]) for n in ("mx", "den", "rden"))
        pT = sb("pT", [P, H // 2, CW])
        oT = sb("oT", [P, HALVES, CW])
        front = ps("front", [P, HALVES, CW])
        score = [ps(f"score{i}", [P, H, SC]) for i in range(2)]
        ptps = [ps(f"ptps{i}", [P, CW]) for i in range(2)]

        mask_loaded, filled, identb_made, pair_made = sem("mask_loaded"), sem("filled"), sem("identb_made"), sem("pair_made")
        k_psum, k_made, kblk_made = sem("k_psum"), sem("k_made"), sem("kblk_made")
        v_psum, v_added, v_made = sem("v_psum"), sem("v_added"), sem("v_made")
        v_banks = [score[b // 2][:].rearrange("p h k -> p (h k)")[:, 512 * (b % 2):512 * (b % 2) + D] for b in range(B)]
        stats_done, ln_stats, var_done, rstd_ready = sem("stats_done"), sem("ln_stats"), sem("var_done"), sem("rstd_ready")
        xn_ready, xnT_psum, xnT_ready = sem("xn_ready"), sem("xnT_psum"), sem("xnT_ready")
        q_psum, qT_ready, bo_added = sem("q_psum"), sem("qT_ready"), sem("bo_added")
        scores_ready, max_done, centered, exp_ready = sem("scores_ready"), sem("max_done"), sem("centered"), sem("exp_ready")
        den_ready, rden_ready, probs_ready = sem("den_ready"), sem("rden_ready"), sem("probs_ready")
        qst_ready, pT_psum, pT_ready, vst_ready = sem("qst_ready"), sem("pT_psum"), sem("pT_ready"), sem("vst_ready")
        o_psum, oT_ready, y_psum, y_added = sem("o_psum"), sem("oT_ready"), sem("y_psum"), sem("y_added")
        q_banks = [score[half][:].rearrange("p h k -> p (h k)")[:, 0:CW] for half in range(HALVES)]

        def chunks(eng, body):
            body(0, True)
            with eng.Fori(1, CHUNKS - 1) as c:
                body(c, True)
            body(CHUNKS - 1, False)

        def after(c, t):
            return c + t // CT, t % CT

        def steps(c, more, body):
            for t in range(CT):
                ahead = after(c, t + 3) if more or t == 0 else None
                body(t, ahead)

        with nc.Block() as block:
            @block.sync
            def _(sp):
                if not context.issued:
                    context.issue(sp)
                if masked:
                    sp.dma_start(mask_i[:], mask.rearrange("(t p) k -> p t k", p=P)).then_inc(mask_loaded, 16)

            @block.vector
            def _(dve):
                def spread_values():
                    for rows in range(2):
                        for a in range(2):
                            nc.vector.memset(pairmask[SC * rows:SC * rows + SC, :, a, :],
                                             1.0 if a == rows else 0.0).then_inc(pair_made, 1)
                    dve.wait_ge(context.loaded, context.count)
                    dve.wait_ge(pair_made, 4)
                    split = lambda ap: ap.rearrange("p (j a d) -> p j a d", a=2, d=DK)
                    for b in range(B):
                        dve.wait_ge(v_psum, b + 1)
                        nc.vector.tensor_tensor(vblk[:, b], split(v_banks[b]), split(bv[:]), ALU.add).then_inc(v_added, 1)
                    for b in range(B):
                        dve.wait_ge(v_added, b + 1)
                        nc.vector.tensor_tensor(vblk[:, b], vblk[:, b], pairmask[:], ALU.mult).then_inc(v_made, 1)

                def spread_keys():
                    for half in range(HALVES):
                        dve.wait_ge(k_made, half + 1)
                        for b in range(B):
                            nc.vector.tensor_tensor(kblk[:, b, half], bc(kT[:, half, b, :], 1, [P, HH, SC]),
                                                    bc(headmask[:], 2, [P, HH, SC]), ALU.mult).then_inc(kblk_made, 1)
                    nc.vector.tensor_copy(identb[:], ident[:]).then_inc(identb_made, 1)
                    if masked:
                        dve.wait_ge(mask_loaded, 16)
                        nc.vector.tensor_scalar(fill[:], mask_i[:], 0.0, FILL, ALU.is_equal, ALU.mult).then_inc(filled, 1)

                def moments(c):
                    if isinstance(c, int) and c == 1 and rest_loaded is not None:
                        dve.wait_ge(rest_loaded, 16)
                    for t in range(CT):
                        nc.vector.bn_stats(stats[:, t], x_sb[:, ds(CT * c + t, 1), :]).then_inc(stats_done, 1)
                    if later(c, 1):
                        dve.wait_ge(xn_ready, CT * c)
                        dve.wait_ge(var_done, c)
                    passed(dve, stats_done, CT * (c + 1), turnstile)
                    for t in range(CT):
                        nc.vector.bn_aggr(mv[:, t], stats[:, t]).then_inc(ln_stats, 1)

                def normalize_x(c, more):
                    dve.wait_ge(rstd_ready, c + 1)
                    dve.wait_ge(ln_stats, CT * (c + 1))
                    if later(c, 1):
                        dve.wait_ge(xnT_psum, c)
                    for t in range(CT):
                        nc.vector.tensor_scalar(xn[:, t], x_sb[:, ds(CT * c + t, 1), :], mv[:, t, 0:1], rstd[:, t:t + 1],
                                                ALU.subtract, ALU.mult).then_inc(xn_ready, 1)
                    if isinstance(c, int) and c == 0:
                        spread_keys()
                    if more:
                        moments(c + 1)

                def center(c, t):
                    n = CT * c + t
                    dve.wait_ge(scores_ready, n + 1)
                    if later(c, 1):
                        dve.wait_ge(pT_psum, 2 * (n - CT + 1))
                        if t == 0:
                            dve.wait_ge(centered, n)
                    nc.vector.tensor_reduce(mx[:, t], score[t % 2][:], axis=X, op=ALU.max).then_inc(max_done, 1)
                    dve.wait_ge(max_done, n + 1)
                    nc.vector.tensor_tensor(prob[:, t], score[t % 2][:], bc(mx[:, t], 2, [P, H, SC]),
                                            ALU.subtract).then_inc(centered, 1)

                def normalizer(c, t):
                    n = CT * c + t
                    dve.wait_ge(exp_ready, n + 1)
                    nc.vector.tensor_reduce(den[:, t], prob[:, t], axis=X, op=ALU.add).then_inc(den_ready, 1)
                    dve.wait_ge(den_ready, n + 1)
                    if later(c, 1):
                        dve.wait_ge(probs_ready, n - CT + 1)
                    nc.vector.reciprocal(rden[:, t], den[:, t]).then_inc(rden_ready, 1)

                def add_residual(c):
                    dve.wait_ge(bo_added, c + 1)
                    for bank in range(2):
                        dve.wait_ge(y_psum, 2 * c + bank + 1)
                        xs = x_sb[:, ds(CT * c + 2 * bank, 2), :]
                        nc.vector.tensor_tensor(xs, front[:, bank].rearrange("p (t d) -> p t d", t=2), xs,
                                                ALU.add).then_inc(y_added, 1)

                def attend(c, more):
                    def step(t, ahead):
                        if ahead:
                            center(*ahead)
                        if more or t < 2:
                            normalizer(*after(c, t + 2))
                        if t == 2 and later(c, 1):
                            add_residual(c - 1)

                    steps(c, more, step)

                moments(0)
                spread_values()
                chunks(dve, normalize_x)
                for t in range(3):
                    center(0, t)
                for t in range(2):
                    normalizer(0, t)
                chunks(dve, attend)
                add_residual(CHUNKS - 1)

            @block.gpsimd
            def _(pool):
                def make_rstd(c):
                    pool.wait_ge(ln_stats, CT * (c + 1))
                    nc.gpsimd.tensor_tensor(var[:], mv[:, :, 1], eps_pow[:, 0], ALU.add).then_inc(var_done, 1)
                    pool.wait_ge(var_done, c + 1)
                    if later(c, 1):
                        pool.wait_ge(xn_ready, CT * c)
                    nc.gpsimd.tensor_tensor(rstd[:], var[:], eps_pow[:, 1], ALU.pow).then_inc(rstd_ready, 1)

                def norm_chunk(c, more):
                    if more:
                        make_rstd(c + 1)
                    pool.wait_ge(xn_ready, CT * (c + 1))
                    if isinstance(c, int) and c == 0:
                        pool.wait_ge(context.loaded, context.count)
                    xs = x_sb[:, ds(CT * c, CT), :]
                    nc.gpsimd.tensor_tensor(xs, xs, bc(bo[:], 1, [P, CT, D]), ALU.add).then_inc(bo_added, 1)

                def divide(c, t):
                    pool.wait_ge(rden_ready, CT * c + t + 1)
                    nc.gpsimd.tensor_tensor(prob[:, t], prob[:, t], bc(rden[:, t], 2, [P, H, SC]),
                                            ALU.mult).then_inc(probs_ready, 1)

                def attend(c, more):
                    for t in range(CT):
                        if t == 1:
                            if later(c, 1):
                                pool.wait_ge(o_psum, 2 * c)
                            else:
                                pool.wait_ge(v_made, B)
                            nc.gpsimd.tensor_copy(vst[:], vblk[:, ds(c // 2, 1)]).then_inc(vst_ready, 1)
                        if more or t < 2:
                            divide(*after(c, t + 2))

                make_rstd(0)
                chunks(pool, norm_chunk)
                divide(0, 0)
                divide(0, 1)
                chunks(pool, attend)

            @block.scalar
            def _(act):
                def evacuate_xnT(c):
                    act.wait_ge(xnT_psum, c + 1)
                    if later(c, 1):
                        act.wait_ge(q_psum, 2 * c)
                    nc.scalar.activation(xnT[:], front[:], ACT.Copy).then_inc(xnT_ready, 1)

                def evacuate_qT(c, half):
                    act.wait_ge(q_psum, 2 * c + half + 1)
                    nc.scalar.activation(qT[:, half, ds(CW * c, CW)], q_banks[half], ACT.Identity,
                                         bias=bqk[:, 0, half:half + 1]).then_inc(qT_ready, 1)

                def q_chunk(c, more):
                    evacuate_qT(c, 0)
                    if more:
                        evacuate_xnT(c + 1)
                    evacuate_qT(c, 1)

                def fix_qT(c):
                    if later(c, 1):
                        act.wait_ge(scores_ready, CT * c)
                    nc.scalar.activation(qst[:], qT[:, :, ds(CW * c, CW)], ACT.Copy).then_inc(qst_ready, 1)

                def exponential(c, t):
                    act.wait_ge(centered, CT * c + t + 1)
                    nc.scalar.activation(prob[:, t], prob[:, t], ACT.Exp, scale=SCALE).then_inc(exp_ready, 1)

                def evacuate_pT(c, t):
                    for part in range(2):
                        act.wait_ge(pT_psum, 2 * (CT * c + t) + part + 1)
                        nc.scalar.activation(pT[:, 4 * part:4 * part + 4, t * P:(t + 1) * P],
                                             ptps[part][:].rearrange("p (j t) -> p j t", j=4), ACT.Copy).then_inc(pT_ready, 1)

                def evacuate_oT(c):
                    if later(c, 1):
                        act.wait_ge(y_psum, 2 * c)
                    for half in range(HALVES):
                        act.wait_ge(o_psum, 2 * c + half + 1)
                        nc.scalar.activation(oT[:, half], front[:, half], ACT.Copy).then_inc(oT_ready, 1)

                def attend(c, more):
                    def step(t, ahead):
                        if t == 0:
                            if more:
                                fix_qT(c + 1)
                            if later(c, 1):
                                evacuate_oT(c - 1)
                        evacuate_pT(c, t)
                        if ahead:
                            exponential(*ahead)

                    steps(c, more, step)

                act.wait_ge(context.loaded, context.count)
                for half in range(HALVES):
                    act.wait_ge(k_psum, half + 1)
                    nc.scalar.activation(kT[:, half], front[:, half, 0:B * SC], ACT.Identity,
                                         bias=bqk[:, 1, half:half + 1]).then_inc(k_made, 1)
                evacuate_xnT(0)
                chunks(act, q_chunk)
                act.wait_ge(qT_ready, 2 * CHUNKS)
                fix_qT(0)
                for t in range(3):
                    exponential(0, t)
                chunks(act, attend)
                evacuate_oT(CHUNKS - 1)

            @block.tensor
            def _(pe):
                def transpose_xn(c):
                    pe.wait_ge(xn_ready, CT * (c + 1))
                    if later(c, 1):
                        pe.wait_ge(xnT_ready, c)
                    for t in range(CT):
                        for half in range(HALVES):
                            last = nc.tensor.transpose(front[:, half, t * P:(t + 1) * P],
                                                       xn[:, t, half * P:(half + 1) * P], ident[:])
                    last.then_inc(xnT_psum, 1)

                def project_q(c, more):
                    if more:
                        transpose_xn(c + 1)
                    pe.wait_ge(xnT_ready, c + 1)
                    for half in range(HALVES):
                        if later(c, 1):
                            pe.wait_ge(qT_ready, 2 * c + half - 1)
                        for k in range(HALVES):
                            last = nc.tensor.matmul(q_banks[half], wts[:, 0, k, half * P:(half + 1) * P], xnT[:, k],
                                                    start=(k == 0), stop=(k == HALVES - 1))
                        last.then_inc(q_psum, 1)

                def scores(c, t):
                    if t == 0:
                        pe.wait_ge(qst_ready, c + 1)
                    if later(c, 1) or t >= 2:
                        pe.wait_ge(centered, CT * c + t - 1)
                    for half in range(HALVES):
                        bank = score[t % 2][:, half * HH:(half + 1) * HH, :]
                        last = nc.tensor.matmul(bank, qst[:, half, t * P:(t + 1) * P],
                                                kblk[:, ds(c // 2, 1), half].rearrange("p o h k -> p (o h k)"),
                                                start=True, stop=not masked)
                        if masked:
                            last = nc.tensor.matmul(bank, identb[:], fill[:, ds(CT * c + t, 1), :].broadcast_to([P, HH, SC]),
                                                    start=False, stop=True)
                    last.then_inc(scores_ready, 1)

                def transpose_probs(c, t):
                    pe.wait_ge(probs_ready, CT * c + t + 1)
                    for part in range(2):
                        if later(c, 1) or t:
                            pe.wait_ge(pT_ready, 2 * (CT * c + t) + part - 1)
                        for j in range(4):
                            pair = 4 * part + j
                            last = nc.tensor.transpose(ptps[part][:, j * P:(j + 1) * P], prob[:, t, 2 * pair:2 * pair + 2, :],
                                                       ident[:])
                        last.then_inc(pT_psum, 1)

                def weigh_values(c):
                    pe.wait_ge(vst_ready, c + 1)
                    pe.wait_ge(pT_ready, 2 * CT * (c + 1))
                    if later(c, 1):
                        pe.wait_ge(y_added, 2 * c)
                    for half in range(HALVES):
                        for j in range(4):
                            last = nc.tensor.matmul(front[32 * j:32 * j + 32, half],
                                                    vst[:, half * P + 32 * j:half * P + 32 * j + 32],
                                                    pT[:, half * 4 + j], start=True, stop=True)
                        last.then_inc(o_psum, 1)

                def project_out(c):
                    pe.wait_ge(oT_ready, 2 * (c + 1))
                    for bank in range(2):
                        for t in (2 * bank, 2 * bank + 1):
                            for k in range(HALVES):
                                last = nc.tensor.matmul(front[:, bank, (t % 2) * D:(t % 2 + 1) * D],
                                                        oT[:, k, t * P:(t + 1) * P], wts[:, 3, k],
                                                        start=(k == 0), stop=(k == HALVES - 1))
                        last.then_inc(y_psum, 1)

                def attend(c, more):
                    def step(t, ahead):
                        if ahead:
                            scores(*ahead)
                        if t == 0 and later(c, 1):
                            weigh_values(c - 1)
                        if t == 1 and later(c, 1):
                            project_out(c - 1)
                        transpose_probs(c, t)

                    steps(c, more, step)

                pe.wait_ge(context.loaded, context.count)
                for half in range(HALVES):
                    for k in range(HALVES):
                        last = nc.tensor.matmul(front[:, half, 0:B * SC], wts[:, 1, k, half * P:(half + 1) * P],
                                                ctxT[:, k, :, 0, :], start=(k == 0), stop=(k == HALVES - 1))
                    last.then_inc(k_psum, 1)
                for b in range(B):
                    for k in range(HALVES):
                        last = nc.tensor.matmul(v_banks[b], ctxT[:, k, b, :, :], wts[:, 2, k, :], start=(k == 0),
                                                stop=(k == HALVES - 1))
                    last.then_inc(v_psum, 1)
                pe.wait_ge(k_made, HALVES)
                transpose_xn(0)
                pe.wait_ge(v_added, B)
                chunks(pe, project_q)
                pe.wait_ge(qT_ready, 2 * CHUNKS)
                pe.wait_ge(kblk_made, HALVES * B)
                pe.wait_ge(identb_made, 1)
                if masked:
                    pe.wait_ge(filled, 1)
                for t in range(3):
                    scores(0, t)
                chunks(pe, attend)
                weigh_values(CHUNKS - 1)
                project_out(CHUNKS - 1)

PAIRS = ((0, 0), (1, 0), (2, 0), (0, 1), (1, 1), (0, 2))
KROWS = len(PAIRS) * DK
MROWS = 2
GH = 4
GROUPS = B * H // GH
KT = S // P
VW = DK + 1
UNITS = GROUPS * 2


def self_projections(nc, x_sb, src_sb, ident, eps_pow, w, q_parts, k_parts, v_dram):
    with ExitStack() as ctx:
        kit = Kit(nc, ctx, "sp_")
        sb, ps, sem = kit.sb, kit.ps, kit.sem
        turnstile = sem("turnstile")
        wts = sb("wts", [P, 3, HALVES, D])
        swcol = sb("swcol", [P, HALVES])
        swblk = sb("swblk", [P, HALVES, P])
        stats, mv = sb("stats", [P, CT, 6]), sb("mv", [P, CT, 2])
        var, rstd = sb("var", [P, CT]), sb("rstd", [P, CT])
        xn = sb("xn", [P, CT, D])
        srcT = sb("srcT", [P, HALVES, CW])
        qT, th = sb("qT", [P, HALVES, CW]), sb("th", [P, HALVES, CW])
        qrest, krest = sb("qrest", [P, HALVES, CW]), sb("krest", [P, HALVES, CW])
        qpart = [sb(f"qpart{i}", [P, 3, HALVES, CW], bf16) for i in range(2)]
        kpart = [sb(f"kpart{i}", [P, 3, HALVES, CW], bf16) for i in range(2)]
        vt = [sb(f"vt{i}", [P, H // GH, CT, GH, VW]) for i in range(2)]
        vps, qps, kps, zps = (ps(n, [P, HALVES, CW]) for n in ("vps", "qps", "kps", "zps"))

        loaded, blk_made = sem("loaded"), sem("blk_made")
        stats_done, ln_stats, var_done, rstd_ready = sem("stats_done"), sem("ln_stats"), sem("var_done"), sem("rstd_ready")
        xn_ready, xnT_psum, srcT_ready = sem("xn_ready"), sem("xnT_psum"), sem("srcT_ready")
        v_psum, v_ready, q_psum, k_psum, z_psum = (sem("v_psum"), sem("v_ready"), sem("q_psum"), sem("k_psum"),
                                                   sem("z_psum"))
        qT_ready, th_ready, q_scaled = sem("qT_ready"), sem("th_ready"), sem("q_scaled")
        k1, krest_made, k2, k3 = sem("k1"), sem("krest_made"), sem("k2"), sem("k3")
        q1, qrest_made, q2, q3 = sem("q1"), sem("qrest_made"), sem("q2"), sem("q3")
        src_kept = sem("src_kept")
        q_stored, k_stored, v_stored = ([sem(f"{n}_stored{i}") for i in range(2)] for n in "qkv")

        RUNS = 3 * HALVES

        def batches(eng, chunk, flags=False):
            def pair(i, last):
                for par in range(2):
                    if flags:
                        chunk(i, par, last and par == 1)
                    else:
                        chunk(i, par)

            pair(0, False)
            with eng.Fori(1, B - 1) as i:
                pair(i, False)
            pair(B - 1, True)

        with nc.Block() as block:
            @block.sync
            def _(sp):
                sp.dma_start(wts[:], w["ffn_qkv"].rearrange("f (k p) n -> p f k n", p=P)).then_inc(loaded, 16)
                sp.dma_start(swcol[:], w["scale_w"]).then_inc(loaded, 16)

                q_runs = ((0, 3, 0, False), (3, 2, 0, False), (5, 1, 0, False))
                k_runs = ((0, 3, 0, True), (3, 2, 1, True), (5, 1, 2, True))

                def store(i, par):
                    c = 2 * i + par
                    sp.wait_ge(v_ready, 2 * (c + 1))
                    sp.dma_start(v_dram[ds(4 * i, 4), :, CT * par:CT * (par + 1), :].rearrange("g p k x -> p g (k x)"),
                                 vt[par][:].rearrange("p g t h v -> p g (t h v)")).then_inc(v_stored[par], 16)
                    for parts, dram, ready, stored, runs in ((kpart, k_parts, k3, k_stored, k_runs),
                                                             (qpart, q_parts, q3, q_stored, q_runs)):
                        sp.wait_ge(ready, c + 1)
                        for half in range(HALVES):
                            rows = dram[ds(4 * i + 2 * half, 2)].rearrange("g h (d r) t -> (g h d) r t", r=len(PAIRS))
                            for pair, pairs, part, same in runs:
                                src = (parts[par][:, part:part + 1, half].broadcast_to([P, pairs, CW]) if same else
                                       parts[par][:, part:part + pairs, half])
                                sp.dma_start(rows[:, pair:pair + pairs, par * CW:(par + 1) * CW], src).then_inc(stored[par], 16)

                batches(sp, store)
                for par in range(2):
                    sp.wait_ge(v_stored[par], 16 * B)
                    for stored in (q_stored, k_stored):
                        sp.wait_ge(stored[par], 16 * B * RUNS)

            @block.vector
            def _(dve):
                dve.wait_ge(loaded, 32)
                for half in range(HALVES):
                    nc.vector.tensor_tensor(swblk[:, half].rearrange("p (h d) -> p h d", d=DK),
                                            bc(w["headmask"][:], 2, [P, HH, DK]),
                                            bc(swcol[:, half:half + 1].broadcast_to([P, HH]), 2, [P, HH, DK]),
                                            ALU.mult).then_inc(blk_made, 1)
                for i in range(2):
                    nc.vector.memset(vt[i][:, :, :, :, DK:], 1.0).then_inc(blk_made, 1)

                def layernorm(c):
                    for t in range(CT):
                        nc.vector.bn_stats(stats[:, t], x_sb[:, ds(CT * c + t, 1), :]).then_inc(stats_done, 1)
                    if later(c, 1):
                        dve.wait_ge(var_done, c)
                        dve.wait_ge(xn_ready, CT * c)
                    passed(dve, stats_done, CT * (c + 1), turnstile)
                    for t in range(CT):
                        nc.vector.bn_aggr(mv[:, t], stats[:, t]).then_inc(ln_stats, 1)

                def ln_apply(c):
                    dve.wait_ge(rstd_ready, c + 1)
                    dve.wait_ge(ln_stats, CT * (c + 1))
                    if later(c, 1):
                        dve.wait_ge(xnT_psum, c)
                    if later(c, 1):
                        dve.wait_ge(src_kept, c)
                    for t in range(CT):
                        nc.vector.tensor_scalar(xn[:, t], x_sb[:, ds(CT * c + t, 1), :], mv[:, t, 0:1], rstd[:, t:t + 1],
                                                ALU.subtract, ALU.mult).then_inc(xn_ready, 1)

                def chunk(i, par, last):
                    c = 2 * i + par
                    if not last:
                        ln_apply(c + 1)
                    if not isinstance(i, int) or c + 2 < CHUNKS:
                        layernorm(c + 2)
                    dve.wait_ge(k1, c + 1)
                    if later(c, 1):
                        dve.wait_ge(k3, c)
                    nc.vector.tensor_tensor(krest[:], kps[:], kpart[par][:, 0], ALU.subtract).then_inc(krest_made, 1)
                    dve.wait_ge(th_ready, c + 1)
                    dve.wait_ge(qT_ready, c + 1)
                    nc.vector.scalar_tensor_tensor(out=qT[:], in0=th[:], scalar=1.0, in1=qT[:], op0=ALU.add,
                                                   op1=ALU.mult).then_inc(q_scaled, 1)
                    dve.wait_ge(q1, c + 1)
                    if later(c, 1):
                        dve.wait_ge(q3, c)
                    nc.vector.tensor_tensor(qrest[:], qT[:], qpart[par][:, 0], ALU.subtract).then_inc(qrest_made, 1)

                layernorm(0)
                ln_apply(0)
                layernorm(1)
                batches(dve, chunk, True)

            @block.gpsimd
            def _(pool):
                def make_rstd(c):
                    pool.wait_ge(ln_stats, CT * (c + 1))
                    nc.gpsimd.tensor_tensor(var[:], mv[:, :, 1], eps_pow[:, 0], ALU.add).then_inc(var_done, 1)
                    pool.wait_ge(var_done, c + 1)
                    if later(c, 1):
                        pool.wait_ge(xn_ready, CT * c)
                    nc.gpsimd.tensor_tensor(rstd[:], var[:], eps_pow[:, 1], ALU.pow).then_inc(rstd_ready, 1)

                def chunk(i, par, last):
                    c = 2 * i + par
                    pool.wait_ge(k2, c + 1)
                    nc.gpsimd.tensor_tensor(kpart[par][:, 2], krest[:], kpart[par][:, 1], ALU.subtract).then_inc(k3, 1)
                    if not isinstance(i, int) or c + 2 < CHUNKS:
                        make_rstd(c + 2)
                    pool.wait_ge(q2, c + 1)
                    nc.gpsimd.tensor_tensor(qpart[par][:, 2], qrest[:], qpart[par][:, 1], ALU.subtract).then_inc(q3, 1)

                make_rstd(0)
                make_rstd(1)
                batches(pool, chunk, True)

            @block.scalar
            def _(act):
                def keep_src(c):
                    act.wait_ge(xn_ready, CT * (c + 1))
                    nc.scalar.activation(src_sb[:, ds(CT * c, CT), :], xn[:], ACT.Copy).then_inc(src_kept, 1)

                def evacuate_srcT(c):
                    act.wait_ge(xnT_psum, c + 1)
                    if later(c, 1):
                        act.wait_ge(k_psum, c)
                    nc.scalar.activation(srcT[:], vps[:], ACT.Copy).then_inc(srcT_ready, 1)

                def chunk(i, par, last):
                    c = 2 * i + par
                    act.wait_ge(blk_made, 4)
                    if later(i, 1):
                        act.wait_ge(v_stored[par], 16 * i)
                    for bank in range(2):
                        act.wait_ge(v_psum, 2 * c + bank + 1)
                        for t in range(2):
                            copied = nc.scalar.activation(vt[par][:, :, 2 * bank + t, :, 0:DK],
                                                        vps[:, bank, t * D:(t + 1) * D].rearrange("p (g h d) -> p g h d", h=GH,
                                                                                                  d=DK), ACT.Copy)
                        copied.then_inc(v_ready, 1)
                    act.wait_ge(q_psum, c + 1)
                    if later(c, 1):
                        act.wait_ge(qrest_made, c)
                    nc.scalar.activation(qT[:], qps[:], ACT.Copy).then_inc(qT_ready, 1)
                    act.wait_ge(k_psum, c + 1)
                    if later(i, 1):
                        act.wait_ge(k_stored[par], 16 * RUNS * i)
                    nc.scalar.activation(kpart[par][:, 0], kps[:], ACT.Copy).then_inc(k1, 1)
                    if not last:
                        evacuate_srcT(c + 1)
                    act.wait_ge(krest_made, c + 1)
                    nc.scalar.activation(kpart[par][:, 1], krest[:], ACT.Copy).then_inc(k2, 1)
                    if not last:
                        keep_src(c + 1)
                    act.wait_ge(z_psum, c + 1)
                    if later(c, 1):
                        act.wait_ge(q_scaled, c)
                    nc.scalar.activation(th[:], zps[:], ACT.Tanh, scale=0.5).then_inc(th_ready, 1)
                    act.wait_ge(q_scaled, c + 1)
                    if later(i, 1):
                        act.wait_ge(q_stored[par], 16 * RUNS * i)
                    nc.scalar.activation(qpart[par][:, 0], qT[:], ACT.Copy).then_inc(q1, 1)
                    act.wait_ge(qrest_made, c + 1)
                    nc.scalar.activation(qpart[par][:, 1], qrest[:], ACT.Copy).then_inc(q2, 1)

                evacuate_srcT(0)
                keep_src(0)
                batches(act, chunk, True)

            @block.tensor
            def _(pe):
                def transpose_xn(c):
                    pe.wait_ge(xn_ready, CT * (c + 1))
                    if later(c, 1):
                        pe.wait_ge(v_ready, 2 * c)
                    for t in range(CT):
                        for half in range(HALVES):
                            last = nc.tensor.transpose(vps[:, half, t * P:(t + 1) * P],
                                                       xn[:, t, half * P:(half + 1) * P], ident[:])
                    last.then_inc(xnT_psum, 1)

                def chunk(i, par, last_chunk):
                    c = 2 * i + par
                    pe.wait_ge(srcT_ready, c + 1)
                    for bank in range(2):
                        for t in (2 * bank, 2 * bank + 1):
                            for k in range(HALVES):
                                last = nc.tensor.matmul(vps[:, bank, (t % 2) * D:(t % 2 + 1) * D],
                                                        srcT[:, k, t * P:(t + 1) * P], wts[:, 2, k],
                                                        start=(k == 0), stop=(k == HALVES - 1))
                        last.then_inc(v_psum, 1)
                    if later(c, 1):
                        pe.wait_ge(qT_ready, c)
                    for half in range(HALVES):
                        for k in range(HALVES):
                            last = nc.tensor.matmul(qps[:, half], wts[:, 0, k, half * P:(half + 1) * P], srcT[:, k],
                                                    start=(k == 0), stop=(k == HALVES - 1))
                    last.then_inc(q_psum, 1)
                    if later(c, 1):
                        pe.wait_ge(krest_made, c)
                    for half in range(HALVES):
                        for k in range(HALVES):
                            last = nc.tensor.matmul(kps[:, half], wts[:, 1, k, half * P:(half + 1) * P], srcT[:, k],
                                                    start=(k == 0), stop=(k == HALVES - 1))
                    last.then_inc(k_psum, 1)
                    if not last_chunk:
                        transpose_xn(c + 1)
                    pe.wait_ge(qT_ready, c + 1)
                    if later(c, 1):
                        pe.wait_ge(th_ready, c)
                    for half in range(HALVES):
                        last = nc.tensor.matmul(zps[:, half], swblk[:, half], qT[:, half], start=True, stop=True)
                    last.then_inc(z_psum, 1)

                pe.wait_ge(loaded, 32)
                pe.wait_ge(blk_made, 4)
                transpose_xn(0)
                batches(pe, chunk, True)


def self_attention(nc, attn, ident, q_parts, k_parts, v_dram, m_dram, x_sb, n2_b):
    SETS = 3
    with ExitStack() as ctx:
        kit = Kit(nc, ctx, "sa_")
        sb, ps, sem = kit.sb, kit.ps, kit.sem
        turnstile = sem("turnstile")
        qs = [sb(f"q{i}", [KROWS + MROWS, GH, S], bf16) for i in range(SETS)]
        ks = [sb(f"k{i}", [KROWS + MROWS, GH, S], bf16) for i in range(SETS)]
        vs = [sb(f"v{i}", [P, KT, GH, VW]) for i in range(SETS)]
        ex = [[sb(f"e{i}{p}", [P, 2, CW]) for p in range(2)] for i in range(2)]
        mpart = [sb(f"mpart{i}", [P, GH, CT, 2]) for i in range(2)]
        mfull = sb("mfull", [P, GH, CT])
        negm = sb("negm", [GH * CT, MROWS, P], bf16)
        o_sb = sb("o", [P, CW])
        rden = sb("rden", [P, CT, GH])
        n2b = sb("n2b", [P, D])
        n2b_loaded, x_biased = sem("n2b_loaded"), sem("x_biased")
        bps = [ps(f"b{p}", [P, 2, CW]) for p in range(2)]
        aps = [ps(f"a{i}", [P, CW]) for i in range(2)]
        ops = ps("ops", [P, CW])
        misc = ps("misc", [P, CT, P])

        q_loaded, k_loaded, v_loaded = ([sem(f"{n}_loaded{i}") for i in range(SETS)] for n in "qkv")
        ones_made, b_scores, exp_done, pv_done = sem("ones_made"), sem("b_scores"), sem("exp_done"), sem("pv_done")
        a_scores, max_done, m_full, m_psum = sem("a_scores"), sem("max_done"), sem("m_full"), sem("m_psum")
        negm_hi, negm_ready, m_stored, m_loaded = sem("negm_hi"), sem("negm_ready"), sem("m_stored"), sem("m_loaded")
        o_evacuated, o_psum, rden_made, o_done = sem("o_evacuated"), sem("o_psum"), sem("rden_made"), sem("o_done")
        AM = GH * CT * 2

        def groups(eng, body):
            with eng.Fori(0, GROUPS // SETS - 1) as i:
                for j in range(SETS):
                    body(i * SETS + j, i, j)
            for g in range(GROUPS - SETS - 1, GROUPS):
                body(g, g // SETS, g % SETS)

        with nc.Block() as block:
            @block.sync
            def _(sp):
                def load(g, turn, s):
                    sp.dma_start(qs[s][0:KROWS], q_parts[ds(g, 1)].rearrange("g h r t -> r (g h) t")).then_inc(q_loaded[s], 16)
                    sp.dma_start(ks[s][0:KROWS], k_parts[ds(g, 1)].rearrange("g h r t -> r (g h) t")).then_inc(k_loaded[s], 16)
                    sp.dma_start(vs[s][:].rearrange("p k h v -> p k (h v)"),
                                 v_dram[ds(g, 1)].rearrange("g p k x -> p (g k) x")).then_inc(v_loaded[s], 16)

                def pass_max(a, s, qc):
                    sp.wait_ge(negm_ready, a + 1)
                    sp.dma_start(m_dram[ds(a, 1)].rearrange("a r c q -> (a c) r q"), negm[:]).then_inc(m_stored, 16)
                    sp.wait_ge(m_stored, 16 * (a + 1))
                    sp.dma_start(qs[s][KROWS:, :, qc * CW:(qc + 1) * CW],
                                 m_dram[ds(a, 1)].rearrange("a r (h t) q -> r (a h) (t q)", h=GH)).then_inc(m_loaded, 16)

                def body(g, turn, j):
                    for qc in range(2):
                        n = 2 * g + qc
                        if qc == 0 and not (isinstance(g, int) and g + 2 >= GROUPS):
                            sp.wait_ge(pv_done, 16 * n + 4)
                            load(g + 2, turn, (j + 2) % SETS)
                        a = n + 1
                        if not (isinstance(a, int) and a >= UNITS):
                            pass_max(a, (j + (a_is_next(qc))) % SETS, (qc + 1) % 2)

                def a_is_next(qc):
                    return 1 if qc == 1 else 0

                load(0, 0, 0)
                load(1, 0, 1)
                sp.dma_start(n2b[:], n2_b.partition_broadcast(P)).then_inc(n2b_loaded, 16)
                pass_max(0, 0, 0)
                groups(sp, body)

            @block.gpsimd
            def _(pool):
                for s in range(SETS):
                    nc.gpsimd.memset(ks[s][KROWS:], 1.0).then_inc(ones_made, 1)
                pool.wait_ge(ones_made, SETS + 2)
                pool.wait_ge(n2b_loaded, 16)
                with pool.Fori(0, CHUNKS) as c:
                    xs = x_sb[:, ds(CT * c, CT), :]
                    nc.gpsimd.tensor_tensor(xs, xs, bc(n2b[:], 1, [P, CT, D]), ALU.add).then_inc(x_biased, 1)
                    pool.wait_ge(x_biased, c + 1)

            @block.vector
            def _(dve):
                def maxima(a, k, par):
                    head, rest = k // (CT * 2), k % (CT * 2)
                    dve.wait_ge(a_scores, AM * a + k + 1)
                    nc.vector.tensor_reduce(mpart[par][:, head, rest // 2, rest % 2:rest % 2 + 1], aps[k % 2][:], axis=X,
                                            op=ALU.max).then_inc(max_done, 1)

                def combine(a, par):
                    dve.wait_ge(max_done, AM * (a + 1))
                    dve.wait_ge(m_psum, a)
                    nc.vector.tensor_tensor(mfull[:], mpart[par][:, :, :, 0], mpart[par][:, :, :, 1],
                                            ALU.max).then_inc(m_full, 1)

                def split_max(a):
                    src = misc[:].rearrange("p a b -> p (a b)")[0:GH * CT, 0:P]
                    dve.wait_ge(m_psum, a + 1)
                    dve.wait_ge(m_stored, 16 * a)
                    nc.vector.tensor_scalar(negm[:, 0], src, -1.0, None, ALU.mult).then_inc(negm_hi, 1)
                    dve.wait_ge(negm_hi, a + 1)
                    nc.vector.scalar_tensor_tensor(out=negm[:, 1], in0=src, scalar=-1.0, in1=negm[:, 0], op0=ALU.mult,
                                                   op1=ALU.subtract).then_inc(negm_ready, 1)

                def normalize(n):
                    view = misc[:].rearrange("p t (h x) -> p t h x", h=GH)
                    dve.wait_ge(o_psum, n + 1)
                    nc.vector.reciprocal(rden[:], view[:, :, :, DK]).then_inc(rden_made, 1)
                    dve.wait_ge(rden_made, n + 1)
                    nc.vector.tensor_tensor(attn[:, ds(n, 1)].rearrange("p o (t h d) -> p (o t) h d", t=CT, h=GH),
                                            view[:, :, :, 0:DK], bc(rden[:], 3, [P, CT, GH, DK]),
                                            ALU.mult).then_inc(o_done, 1)

                def body(g, turn, j):
                    for qc in range(2):
                        n = 2 * g + qc
                        known = isinstance(g, int)
                        for kt in range(KT):
                            if not (known and g + 1 >= GROUPS):
                                for k in range(4 * kt, 4 * kt + 4):
                                    maxima(n + 2, k, qc)
                            if kt == 1 and not (known and n + 1 >= UNITS):
                                split_max(n + 1)
                            if kt == 4:
                                normalize(n)
                        if not (known and n + 2 >= UNITS):
                            combine(n + 2, qc)

                nc.vector.memset(o_sb[:], 1.0).then_inc(ones_made, 1)
                nc.vector.memset(ops[:], 0.0).then_inc(ones_made, 1)
                nc.vector.memset(rden[:], 0.0).then_inc(exp_done, 2)
                nc.vector.memset(mfull[:], 0.0).then_inc(pv_done, 4)
                dve.wait_ge(exp_done, 2)
                dve.wait_ge(pv_done, 4)
                for a in range(2):
                    for k in range(AM):
                        maxima(a, k, a)
                    combine(a, a)
                    if a == 0:
                        split_max(0)
                groups(dve, body)
                normalize(UNITS)

            @block.scalar
            def _(act):
                def body(g, turn, j):
                    for qc in range(2):
                        n = 2 * g + qc
                        for kt in range(KT):
                            for p in range(2):
                                act.wait_ge(b_scores, 16 * n + 2 * kt + p + 1)
                                act.wait_ge(pv_done, 16 * n + 2 * kt + p + 1)
                                nc.scalar.activation(ex[kt % 2][p][:], bps[p][:], ACT.Exp, scale=SCALE).then_inc(exp_done, 1)
                        act.wait_ge(pv_done, 16 * (n + 1) + 4)
                        act.wait_ge(o_psum, n + 1)
                        nc.scalar.activation(o_sb[:], ops[:], ACT.Copy).then_inc(o_evacuated, 1)

                act.wait_ge(ones_made, SETS + 2)
                groups(act, body)

            @block.tensor
            def _(pe):
                def first_scores(a, k, s, turn, qc):
                    head, rest = k // (CT * 2), k % (CT * 2)
                    if k == 0:
                        pe.wait_ge(q_loaded[s], 16 * (turn + 1))
                        pe.wait_ge(k_loaded[s], 16 * (turn + 1))
                    if not (isinstance(a, int) and a == 0 and k < 2):
                        pe.wait_ge(max_done, AM * a + k - 1)
                    q0 = (qc * CT + rest // 2) * P
                    nc.tensor.matmul(aps[k % 2][:], qs[s][0:KROWS, head, q0:q0 + P],
                                     ks[s][0:KROWS, head, (rest % 2) * CW:(rest % 2 + 1) * CW],
                                     start=True, stop=True).then_inc(a_scores, 1)

                def transpose_max(a):
                    pe.wait_ge(m_full, a + 1)
                    if not (isinstance(a, int) and a == 0):
                        pe.wait_ge(o_done, a - 1)
                    nc.tensor.transpose(misc[:].rearrange("p a b -> p (a b)")[0:GH * CT, 0:P],
                                        mfull[:].rearrange("p h t -> p (h t)"), ident[:]).then_inc(m_psum, 1)

                def transpose_out(n):
                    pe.wait_ge(o_evacuated, n)
                    if not (isinstance(n, int) and n >= UNITS - 1):
                        pe.wait_ge(negm_ready, n + 2)
                    else:
                        pe.wait_ge(o_done, n)
                    for t in range(CT):
                        last = nc.tensor.transpose(misc[:, t], o_sb[:, t * P:(t + 1) * P], ident[:])
                    last.then_inc(o_psum, 1)

                def scores(n, kt, p, s, qc):
                    if kt == 0 and p == 0:
                        pe.wait_ge(m_loaded, 16 * (n + 1))
                    pe.wait_ge(exp_done, 16 * n + 2 * kt + p + 1)
                    for head in (2 * p, 2 * p + 1):
                        last = nc.tensor.matmul(bps[p][:, head % 2], ks[s][:, head, kt * P:(kt + 1) * P],
                                                qs[s][:, head, qc * CW:(qc + 1) * CW], start=True, stop=True)
                    last.then_inc(b_scores, 1)

                def weigh_values(n, kt, p, s, turn):
                    if kt == 0 and p == 0:
                        pe.wait_ge(o_evacuated, n)
                        pe.wait_ge(v_loaded[s], 16 * (turn + 1))
                    pe.wait_ge(exp_done, 16 * n + 2 * kt + p + 3)
                    for head in (2 * p, 2 * p + 1):
                        last = nc.tensor.matmul(ops[32 * head:32 * head + VW], vs[s][:, kt, head], ex[kt % 2][p][:, head % 2],
                                                start=(kt == 0), stop=(kt == KT - 1))
                    last.then_inc(pv_done, 1)

                def body(g, turn, j):
                    known = isinstance(g, int)
                    s1 = (j + 1) % SETS
                    turn1 = turn + (j + 1) // SETS
                    for qc in range(2):
                        n = 2 * g + qc

                        def ahead(k):
                            if not (known and g + 1 >= GROUPS):
                                first_scores(n + 2, k, s1, turn1, qc)

                        for kt in range(KT):
                            scores(n, kt, 0, j, qc)
                            ahead(4 * kt)
                            scores(n, kt, 1, j, qc)
                            ahead(4 * kt + 1)
                            if kt:
                                for p in range(2):
                                    weigh_values(n, kt - 1, p, j, turn)
                            ahead(4 * kt + 2)
                            ahead(4 * kt + 3)
                            if kt == 1 and not (known and n + 1 >= UNITS):
                                transpose_max(n + 1)
                            if kt == 3:
                                transpose_out(n)
                        for p in range(2):
                            weigh_values(n, KT - 1, p, j, turn)

                for a in range(2):
                    for k in range(AM):
                        first_scores(a, k, 0, 0, a)
                    if a == 0:
                        transpose_max(0)
                pe.wait_ge(ones_made, SETS + 2)
                groups(pe, body)
                transpose_out(UNITS)

E8 = 8
MT = TILES + E8
F1 = 512
FK = F1 // P


def attention_out(nc, src_sb, attn, ident, eps_pow, w, logits, top, topi, gathered_in, load_vectors):
    with ExitStack() as ctx:
        kit = Kit(nc, ctx, "ao_")
        sb, ps, sem = kit.sb, kit.ps, kit.sem
        turnstile = sem("turnstile")
        wg, wo = sb("wg", [P, HALVES, D]), sb("wo", [P, HALVES, D])
        wr, br = sb("wr", [P, HALVES, E8]), sb("br", [P, E8])
        gb, n1g, n1b = sb("gb", [P, HALVES]), sb("n1g", [P, D]), sb("n1b", [P, D])
        gbh = sb("gbh", [P, HALVES])
        zero = sb("zero", [P, D])
        ao = sb("ao", [P, CT, D])
        outT, th, ogT = sb("outT", [P, HALVES, CW]), sb("th", [P, HALVES, CW]), sb("ogT", [P, HALVES, CW])
        y = sb("y", [P, CT, D])
        stats, mv = sb("stats", [P, CT, 6]), sb("mv", [P, CT, 2])
        var, rstd = sb("var", [P, CT]), sb("rstd", [P, CT])
        xr = sb("xr", [P, CT, D])
        xrT = sb("xrT", [P, HALVES, CW])
        tps, gps, yps, xps = (ps(n, [P, HALVES, CW]) for n in ("tps", "gps", "yps", "xps"))

        loaded, cleared, zero_made, gbh_made = sem("loaded"), sem("cleared"), sem("zero_made"), sem("gbh_made")
        ao_ready, outT_psum, outT_ready = sem("ao_ready"), sem("outT_psum"), sem("outT_ready")
        gate_psum, th_ready, og_ready, y_psum, y_ready = (sem("gate_psum"), sem("th_ready"), sem("og_ready"),
                                                          sem("y_psum"), sem("y_ready"))
        stats_done, ln_stats, var_done, rstd_ready = sem("stats_done"), sem("ln_stats"), sem("var_done"), sem("rstd_ready")
        yn_ready, yg_ready, xr_ready, src_ready = sem("yn_ready"), sem("yg_ready"), sem("xr_ready"), sem("src_ready")
        xrT_psum, xrT_ready, lg_psum, lg_ready, top_done = (
            sem("xrT_psum"), sem("xrT_ready"), sem("lg_psum"), sem("lg_ready"), sem("top_done"))

        def chunks(eng, body):
            body(0, True)
            with eng.Fori(1, CHUNKS - 1) as c:
                body(c, True)
            body(CHUNKS - 1, False)

        with nc.Block() as block:
            @block.sync
            def _(sp):
                for dst, name in ((wg, "gate_w"), (wo, "out_w"), (wr, "moe_gate_w")):
                    sp.dma_start(dst[:], w[name].rearrange("(k p) n -> p k n", p=P)).then_inc(loaded, 16)
                for dst, name in ((br, "moe_gate_b"), (n1g, "n1_g"), (n1b, "n1_b")):
                    sp.dma_start(dst[:], w[name].partition_broadcast(P)).then_inc(loaded, 16)
                sp.dma_start(gb[:], w["gate_b"]).then_inc(loaded, 16)
                load_vectors(sp)
                sp.wait_ge(zero_made, 1)
                sp.dma_start(gathered_in.rearrange("(k p) d -> p k d", p=P),
                             bc(zero[:], 1, [P, MT, D])).then_inc(cleared, 16)
                sp.wait_ge(cleared, 16)

            @block.gpsimd
            def _(pool):
                def body(c, more):
                    pool.wait_ge(ln_stats, CT * (c + 1))
                    nc.gpsimd.tensor_tensor(var[:], mv[:, :, 1], eps_pow[:, 0], ALU.add).then_inc(var_done, 1)
                    pool.wait_ge(var_done, c + 1)
                    if later(c, 1):
                        pool.wait_ge(yn_ready, CT * c)
                    nc.gpsimd.tensor_tensor(rstd[:], var[:], eps_pow[:, 1], ALU.pow).then_inc(rstd_ready, 1)
                    pool.wait_ge(yn_ready, CT * (c + 1))
                    nc.gpsimd.tensor_tensor(xr[:], xr[:], bc(n1g[:], 1, [P, CT, D]), ALU.mult).then_inc(yg_ready, 1)
                    pool.wait_ge(yg_ready, c + 1)
                    nc.gpsimd.tensor_tensor(xr[:], xr[:], bc(n1b[:], 1, [P, CT, D]), ALU.add).then_inc(xr_ready, 1)

                pool.wait_ge(loaded, 16 * 7)
                chunks(pool, body)

            @block.scalar
            def _(act):
                def copy_attention(c):
                    if later(c, 1):
                        act.wait_ge(outT_psum, c)
                    units = attn[:, ds(c + 6 * (c // 2) + 1, 7), :][:, 0:7:2, :]
                    nc.scalar.activation(ao[:].rearrange("p t (g x) -> p g t x", g=4),
                                         units.rearrange("p g (t x) -> p g t x", t=CT), ACT.Copy).then_inc(ao_ready, 1)

                def evacuate_outT(c):
                    act.wait_ge(outT_psum, c + 1)
                    if later(c, 1):
                        act.wait_ge(og_ready, c)
                    nc.scalar.activation(outT[:], tps[:], ACT.Copy).then_inc(outT_ready, 1)

                def gate(c):
                    act.wait_ge(gate_psum, c + 1)
                    for half in range(HALVES):
                        nc.scalar.activation(th[:, half], gps[:, half], ACT.Tanh, bias=gbh[:, half:half + 1],
                                             scale=0.5).then_inc(th_ready, 1)

                def keep_and_evacuate(c):
                    act.wait_ge(xr_ready, c + 1)
                    nc.scalar.activation(src_sb[:, ds(CT * c, CT), :], xr[:], ACT.Copy).then_inc(src_ready, 1)
                    act.wait_ge(xrT_psum, c + 1)
                    if later(c, 1):
                        act.wait_ge(lg_psum, c)
                    nc.scalar.activation(xrT[:], xps[:], ACT.Copy).then_inc(xrT_ready, 1)

                def body(c, more):
                    if more:
                        evacuate_outT(c + 1)
                    if later(c, 1):
                        keep_and_evacuate(c - 1)
                    if more:
                        gate(c + 1)
                    if more and (not isinstance(c, int) or c + 2 < CHUNKS):
                        copy_attention(c + 2)

                act.wait_ge(gbh_made, 1)
                copy_attention(0)
                evacuate_outT(0)
                copy_attention(1)
                gate(0)
                body(0, True)
                with act.Fori(1, CHUNKS - 2) as c:
                    body(c, True)
                body(CHUNKS - 2, True)
                body(CHUNKS - 1, False)
                keep_and_evacuate(CHUNKS - 1)

            @block.vector
            def _(dve):
                nc.vector.memset(zero[:], 0.0).then_inc(zero_made, 1)
                dve.wait_ge(loaded, 16 * 7)
                nc.vector.tensor_scalar(gbh[:], gb[:], 0.5, None, ALU.mult).then_inc(gbh_made, 1)

                def apply_gate(c):
                    dve.wait_ge(th_ready, 2 * (c + 1))
                    dve.wait_ge(outT_ready, c + 1)
                    if later(c, 1):
                        dve.wait_ge(y_psum, 2 * c)
                    nc.vector.scalar_tensor_tensor(out=ogT[:], in0=th[:], scalar=1.0, in1=outT[:], op0=ALU.add,
                                                   op1=ALU.mult).then_inc(og_ready, 1)

                def add_router_bias(c):
                    dve.wait_ge(lg_psum, c + 1)
                    nc.vector.tensor_tensor(logits[:, ds(CT * c, CT), :],
                                            xps[:, 0, 0:CT * E8].rearrange("p (t e) -> p t e", t=CT),
                                            bc(br[:], 1, [P, CT, E8]), ALU.add).then_inc(lg_ready, 1)

                def body(c, more):
                    for bank in range(2):
                        dve.wait_ge(y_psum, 2 * c + bank + 1)
                        nc.vector.scalar_tensor_tensor(
                            out=y[:, 2 * bank:2 * bank + 2], in0=yps[:, bank].rearrange("p (t d) -> p t d", t=2), scalar=0.5,
                            in1=src_sb[:, ds(CT * c + 2 * bank, 2), :], op0=ALU.mult, op1=ALU.add).then_inc(y_ready, 1)
                    for t in range(CT):
                        if t % 2 == 0:
                            dve.wait_ge(y_ready, 2 * c + t // 2 + 1)
                        nc.vector.bn_stats(stats[:, t], y[:, t]).then_inc(stats_done, 1)
                    passed(dve, stats_done, CT * (c + 1), turnstile)
                    for t in range(CT):
                        nc.vector.bn_aggr(mv[:, t], stats[:, t]).then_inc(ln_stats, 1)
                    if later(c, 1):
                        dve.wait_ge(src_ready, c)
                        dve.wait_ge(xrT_psum, c)
                    dve.wait_ge(rstd_ready, c + 1)
                    dve.wait_ge(ln_stats, CT * (c + 1))
                    for t in range(CT):
                        nc.vector.tensor_scalar(xr[:, t], y[:, t], mv[:, t, 0:1], rstd[:, t:t + 1], ALU.subtract,
                                                ALU.mult).then_inc(yn_ready, 1)
                    if later(c, 1):
                        add_router_bias(c - 1)
                    if more:
                        apply_gate(c + 1)

                apply_gate(0)
                chunks(dve, body)
                add_router_bias(CHUNKS - 1)
                dve.wait_ge(lg_ready, CHUNKS)
                for t in range(TILES):
                    nc.vector.max(out=top[:, t], in_=logits[:, t]).then_inc(top_done, 1)
                for t in range(TILES):
                    dve.wait_ge(top_done, t + 1)
                    nc.vector.max_index(out=topi[:, t], in_max=top[:, t], in_values=logits[:, t])

            @block.tensor
            def _(pe):
                def transpose_attention(c):
                    pe.wait_ge(ao_ready, c + 1)
                    if later(c, 1):
                        pe.wait_ge(outT_ready, c)
                    for t in range(CT):
                        for half in range(HALVES):
                            last = nc.tensor.transpose(tps[:, half, t * P:(t + 1) * P], ao[:, t, half * P:(half + 1) * P],
                                                       ident[:])
                    last.then_inc(outT_psum, 1)

                def gate(c):
                    pe.wait_ge(outT_ready, c + 1)
                    if later(c, 1):
                        pe.wait_ge(th_ready, 2 * c)
                    for half in range(HALVES):
                        for k in range(HALVES):
                            last = nc.tensor.matmul(gps[:, half], wg[:, k, half * P:(half + 1) * P], outT[:, k],
                                                    start=(k == 0), stop=(k == HALVES - 1))
                    last.then_inc(gate_psum, 1)

                def project(c):
                    pe.wait_ge(og_ready, c + 1)
                    if later(c, 1):
                        pe.wait_ge(y_ready, 2 * c)
                    for bank in range(2):
                        for t in (2 * bank, 2 * bank + 1):
                            for k in range(HALVES):
                                last = nc.tensor.matmul(yps[:, bank, (t % 2) * D:(t % 2 + 1) * D],
                                                        ogT[:, k, t * P:(t + 1) * P], wo[:, k],
                                                        start=(k == 0), stop=(k == HALVES - 1))
                        last.then_inc(y_psum, 1)

                def transpose_xr(c):
                    pe.wait_ge(xr_ready, c + 1)
                    if later(c, 1):
                        pe.wait_ge(lg_ready, c)
                    for t in range(CT):
                        for half in range(HALVES):
                            last = nc.tensor.transpose(xps[:, half, t * P:(t + 1) * P], xr[:, t, half * P:(half + 1) * P],
                                                       ident[:])
                    last.then_inc(xrT_psum, 1)

                def route(c):
                    pe.wait_ge(xrT_ready, c + 1)
                    for t in range(CT):
                        for k in range(HALVES):
                            last = nc.tensor.matmul(xps[:, 0, t * E8:(t + 1) * E8], xrT[:, k, t * P:(t + 1) * P], wr[:, k],
                                                    start=(k == 0), stop=(k == HALVES - 1))
                    last.then_inc(lg_psum, 1)

                def body(c, more):
                    if more:
                        transpose_attention(c + 1)
                    project(c)
                    if later(c, 1):
                        transpose_xr(c - 1)
                    if more:
                        gate(c + 1)
                    if later(c, 1):
                        route(c - 1)

                pe.wait_ge(loaded, 16 * 7)
                transpose_attention(0)
                gate(0)
                chunks(pe, body)
                transpose_xr(CHUNKS - 1)
                route(CHUNKS - 1)


def make_prefix(nc, kit, tri, ones):
    return dict(pre=kit.ps("prefix", [P, TILES * E8]), tot=kit.ps("totals", [P, TILES * E8]),
                tot_sb=kit.sb("tot_sb", [P, TILES, E8]), incl=kit.sb("incl", [P, TILES, E8]),
                one=kit.sb("one", [P, TILES]), tri=tri, ones=ones)


def prefix_products(nc, pe, pf, marks, done):
    nc.tensor.matmul(pf["pre"][:], pf["tri"][:], marks[:].rearrange("p t e -> p (t e)"), start=True, stop=True)
    nc.tensor.matmul(pf["tot"][:], pf["ones"][:], marks[:].rearrange("p t e -> p (t e)"), start=True,
                     stop=True).then_inc(done, 1)


def route_tokens(nc, w, src_sb, logits, top, topi, tri, ones, wsum, slot_i, tile_expert, gathered_in,
                 load_weights):
    with ExitStack() as ctx:
        kit = Kit(nc, ctx, "rt_")
        sb, sem = kit.sb, kit.sem
        turnstile = sem("turnstile")
        pf = make_prefix(nc, kit, tri, ones)
        chosen = sb("chosen", [P, TILES])
        iota8 = sb("iota8", [P, E8])
        mark, markb = sb("mark", [P, TILES, E8]), sb("markb", [P, TILES, E8], bf16)
        rank = sb("rank", [P, TILES, E8])
        count_i, tiles, end, start = sb("count_i", [P, E8], i32), sb("tiles", [P, E8]), sb("end", [P, E8]), sb("start", [P, E8])
        delta, total = sb("delta", [P, TILES]), sb("total", [P, TILES])
        slot = sb("slot", [P, TILES])
        iotam = sb("iotam", [1, MT])
        past = sb("past", [1, MT, E8])
        texp = sb("texp", [1, MT])
        iota_made, step, marks_ready, products = sem("iota_made"), sem("step"), sem("marks_ready"), sem("products")
        delta_ready, exp_ready, slots_ready, scattered = sem("delta_ready"), sem("exp_ready"), sem("slots_ready"), sem("scattered")

        with nc.Block() as block:
            @block.sync
            def _(sp):
                load_weights(sp)

            @block.gpsimd
            def _(pool):
                nc.gpsimd.iota(iota8[:], [[1, E8]], base=0, channel_multiplier=0,
                               allow_small_or_imprecise_dtypes=True).then_inc(iota_made, 1)
                pool.wait_ge(iota_made, 1)
                nc.gpsimd.iota(iotam[:], [[1, MT]], base=0, channel_multiplier=0,
                               allow_small_or_imprecise_dtypes=True).then_inc(iota_made, 1)
                pool.wait_ge(slots_ready, 1)
                for t in range(TILES):
                    pool.indirect_dma_start(out=gathered_in, out_offset=bass.IndirectOffsetOnAxis(ap=slot_i[:, t:t + 1], axis=0),
                                            in_=src_sb[:, t, :], in_offset=None).then_inc(scattered, 16)
                pool.wait_ge(scattered, 16 * TILES)

            @block.scalar
            def _(act):
                act.wait_ge(delta_ready, 1)
                nc.scalar.activation(delta[:], delta[:], ACT.Exp).then_inc(exp_ready, 1)

            @block.tensor
            def _(pe):
                pe.wait_ge(marks_ready, 1)
                prefix_products(nc, pe, pf, markb, products)

            @block.vector
            def _(dve):
                at = [0]

                def link(instruction):
                    at[0] += 1
                    instruction.then_inc(step, 1)
                    dve.wait_ge(step, at[0])

                nc.vector.tensor_tensor(delta[:], top[:, :, 1], top[:, :, 0], ALU.subtract).then_inc(delta_ready, 1)
                link(nc.vector.tensor_tensor(chosen[:], topi[:, :, 0], topi[:, :, 1], ALU.max))
                dve.wait_ge(iota_made, 2)
                link(nc.vector.tensor_tensor(mark[:], bc(chosen[:], 2, [P, TILES, E8]), bc(iota8[:], 1, [P, TILES, E8]),
                                             ALU.is_equal))
                nc.vector.tensor_copy(markb[:], mark[:]).then_inc(marks_ready, 1)
                link(nc.vector.memset(pf["one"][:], 1.0))
                dve.wait_ge(products, 1)
                link(nc.vector.tensor_copy(pf["tot_sb"][:], pf["tot"][:].rearrange("p (t e) -> p t e", e=E8)))
                for e in range(E8):
                    at[0] += 1
                    nc.vector.tensor_tensor_scan(pf["incl"][:, :, e], pf["one"][:], pf["tot_sb"][:, :, e], 0.0,
                                                 ALU.mult, ALU.add).then_inc(step, 1)
                dve.wait_ge(step, at[0])
                link(nc.vector.tensor_tensor(rank[:], pf["pre"][:].rearrange("p (t e) -> p t e", e=E8), pf["incl"][:], ALU.add))
                link(nc.vector.tensor_tensor(rank[:], rank[:], pf["tot_sb"][:], ALU.subtract))
                link(nc.vector.tensor_scalar(count_i[:], pf["incl"][:, TILES - 1], float(P - 1), None, ALU.add))
                link(nc.vector.tensor_scalar(count_i[:], count_i[:], 7, None, ALU.arith_shift_right))
                link(nc.vector.tensor_copy(tiles[:], count_i[:]))
                link(nc.vector.tensor_tensor_scan(end[:], pf["one"][:, 0:E8], tiles[:], 0.0, ALU.mult, ALU.add))
                link(nc.vector.tensor_tensor(start[:], end[:], tiles[:], ALU.subtract))
                link(nc.vector.tensor_scalar(start[:], start[:], float(P), None, ALU.mult))
                link(nc.vector.tensor_tensor(rank[:], rank[:], bc(start[:], 1, [P, TILES, E8]), ALU.add))
                link(nc.vector.tensor_tensor(rank[:], rank[:], mark[:], ALU.mult))
                link(nc.vector.tensor_reduce(slot[:], rank[:], axis=X, op=ALU.add))
                nc.vector.tensor_copy(slot_i[:], slot[:]).then_inc(slots_ready, 1)
                link(nc.vector.tensor_tensor(past[:], bc(iotam[:], 2, [1, MT, E8]), bc(end[0:1, :], 1, [1, MT, E8]), ALU.is_ge))
                link(nc.vector.tensor_reduce(texp[:], past[:], axis=X, op=ALU.add))
                link(nc.vector.tensor_scalar(tile_expert[:], texp[:], float(E8 - 1), None, ALU.min))
                dve.wait_ge(exp_ready, 1)
                link(nc.vector.tensor_scalar(total[:], delta[:], 1.0, None, ALU.add))
                link(nc.vector.reciprocal(total[:], total[:]))
                link(nc.vector.tensor_tensor(delta[:], delta[:], total[:], ALU.mult))
                link(nc.vector.tensor_tensor(wsum[:], delta[:], total[:], ALU.add))


def expert_tiles(nc, ident, eps_pow, w, ew, spent, tile_expert, gathered_in, gathered_out):
    U, AHEAD = 4, 3
    with ExitStack() as ctx:
        kit = Kit(nc, ctx, "ex_")
        sb, ps, sem = kit.sb, kit.ps, kit.sem
        turnstile = sem("turnstile")
        xg = [b[:].rearrange("p t e -> p (t e)") for b in spent] + [sb(f"xg{i}", [P, D]) for i in range(len(spent), U)]
        xb = [sb(f"xb{i}", [P, D]) for i in range(U)]
        xT = [sb(f"xT{i}", [P, HALVES, P]) for i in range(2)]
        hb = [sb(f"hb{i}", [P, F1]) for i in range(U)]
        stats, mv = sb("stats", [P, 2, 6]), sb("mv", [P, 2, 2])
        var, rstd = sb("var", [P, 2]), sb("rstd", [P, 2])
        hT = [sb(f"hT{i}", [P, FK, P]) for i in range(2)]
        xps = [ps(f"xps{i}", [P, F1]) for i in range(2)]
        hps = [ps(f"hps{i}", [P, F1]) for i in range(2)]
        tps = [ps(f"tps{i}", [P, F1]) for i in range(2)]
        yps = [ps(f"yps{i}", [P, F1]) for i in range(2)]
        x_loaded = [sem(f"x_loaded{i}") for i in range(U)]
        y_stored = [sem(f"y_stored{i}") for i in range(U)]
        xT_psum, xT_ready, h_psum, hb_ready, stats_done, ln_stats = (sem("xT_psum"), sem("xT_ready"), sem("h_psum"),
                                                                     sem("hb_ready"), sem("stats_done"), sem("ln_stats"))
        var_done, rstd_ready, hn_ready = sem("var_done"), sem("rstd_ready"), sem("hn_ready")
        hT_psum, hT_ready, y_psum, xb_ready, y_ready = (sem("hT_psum"), sem("hT_ready"), sem("y_psum"), sem("xb_ready"),
                                                        sem("y_ready"))

        def turns(eng, body):
            for j in range(U):
                body(j, 0, j, True)
            with eng.Fori(1, MT // U - 1) as i:
                for j in range(U):
                    body(i * U + j, i, j, True)
            for j in range(U):
                body(MT - U + j, MT // U - 1, j, j + AHEAD < U)

        def expert(eng, k):
            return eng.value_load(tile_expert[0:1, ds(k, 1)], min_val=0, max_val=E8 - 1)

        with nc.Block() as block:
            @block.sync
            def _(sp):
                def load(k, j):
                    sp.dma_start(xg[j][:], gathered_in[ds(P * k, P), :]).then_inc(x_loaded[j], 16)

                def body(k, turn, j, ahead):
                    if ahead:
                        if later(k, 1):
                            passed(sp, xb_ready, k + 2, turnstile)
                            passed(sp, xT_psum, k, turnstile)
                        load(k + AHEAD, (j + AHEAD) % U)

                for k in range(AHEAD):
                    load(k, k)
                turns(sp, body)
                for i in range(U):
                    sp.wait_ge(y_stored[i], 16 * (MT // U))

            @block.tensor
            def _(pe):
                def transpose_x(k, turn, j):
                    pe.wait_ge(x_loaded[j], 16 * (turn + 1))
                    if later(k, 2):
                        pe.wait_ge(xT_ready, k - 1)
                    for half in range(HALVES):
                        last = nc.tensor.transpose(xps[j % 2][:, half * P:(half + 1) * P], xg[j][:, half * P:(half + 1) * P],
                                                   ident[:])
                    last.then_inc(xT_psum, 1)

                def hidden(k, j):
                    e = expert(pe, k)
                    pe.wait_ge(xT_ready, k + 1)
                    if later(k, 2):
                        pe.wait_ge(hb_ready, k - 1)
                    for half in range(HALVES):
                        last = nc.tensor.matmul(hps[j % 2][:], xT[j % 2][:, half], ew["w1"][:, half, ds(e, 1), :],
                                                start=(half == 0), stop=(half == HALVES - 1))
                    last.then_inc(h_psum, 1)

                def body(k, turn, j, ahead):
                    if ahead:
                        transpose_x(k + AHEAD, turn + (j + AHEAD) // U, (j + AHEAD) % U)
                    pe.wait_ge(hn_ready, k + 1)
                    if later(k, 2):
                        pe.wait_ge(hT_ready, k - 1)
                    for f in range(FK):
                        last = nc.tensor.transpose(tps[j % 2][:, f * P:(f + 1) * P], hb[j][:, f * P:(f + 1) * P], ident[:])
                    last.then_inc(hT_psum, 1)
                    if ahead:
                        hidden(k + AHEAD, (j + AHEAD) % U)
                    e = expert(pe, k)
                    pe.wait_ge(hT_ready, k + 1)
                    pe.wait_ge(y_ready, k + 1)
                    for f in range(FK):
                        last = nc.tensor.matmul(yps[j % 2][:, 0:D], hT[j % 2][:, f], ew["w2"][:, f, ds(e, 1), :],
                                                start=(f == 0), stop=(f == FK - 1))
                    last.then_inc(y_psum, 1)

                pe.wait_ge(ew["w_loaded"], ew["w_count"])
                for k in range(AHEAD):
                    transpose_x(k, 0, k)
                    hidden(k, k)
                turns(pe, body)

            @block.scalar
            def _(act):
                def evacuate_xT(k, j):
                    act.wait_ge(xT_psum, k + 1)
                    if later(k, 2):
                        act.wait_ge(h_psum, k - 1)
                    nc.scalar.activation(xT[j % 2][:].rearrange("p k t -> p (k t)"), xps[j % 2][:, 0:D],
                                         ACT.Copy).then_inc(xT_ready, 1)

                def gelu(k, j):
                    e = expert(act, k)
                    act.wait_ge(hT_psum, k + 1)
                    if later(k, 2):
                        act.wait_ge(y_psum, k - 1)
                    for f in range(FK):
                        last = nc.scalar.activation(hT[j % 2][:, f], tps[j % 2][:, f * P:(f + 1) * P], ACT.Gelu,
                                                    bias=ew["bt"][:, f, ds(e, 1)], scale=ew["g"][:, f, ds(e, 1)])
                    last.then_inc(hT_ready, 1)

                def store(k, j):
                    act.wait_ge(y_ready, k + 3)
                    act.dma_start(gathered_out[ds(P * k, P), :], xb[j][:]).then_inc(y_stored[j], 16)

                def body(k, turn, j, ahead):
                    if ahead:
                        evacuate_xT(k + AHEAD, (j + AHEAD) % U)
                    gelu(k, j)
                    if later(k, 2):
                        store(k - 2, (j - 2) % U)

                for k in range(AHEAD):
                    evacuate_xT(k, k)
                act.wait_ge(ew["b_loaded"], ew["b_count"])
                turns(act, body)
                for k in (MT - 2, MT - 1):
                    store(k, k % U)

            @block.vector
            def _(dve):
                def add_b1(k, j, e):
                    dve.wait_ge(h_psum, k + 1)
                    nc.vector.tensor_tensor(hb[j][:], hps[j % 2][:], ew["b1"][:, ds(e, 1), :].rearrange("p o f -> p (o f)"),
                                            ALU.add).then_inc(hb_ready, 1)
                    dve.wait_ge(hb_ready, k + 1)
                    nc.vector.bn_stats(stats[:, j % 2], hb[j][:]).then_inc(stats_done, 1)
                    passed(dve, stats_done, k + 1, turnstile)
                    nc.vector.bn_aggr(mv[:, j % 2], stats[:, j % 2]).then_inc(ln_stats, 1)

                def apply_norm(k, j):
                    dve.wait_ge(rstd_ready, k + 1)
                    nc.vector.tensor_scalar(hb[j][:], hb[j][:], mv[:, j % 2, 0:1], rstd[:, j % 2:j % 2 + 1], ALU.subtract,
                                            ALU.mult).then_inc(hn_ready, 1)

                def finish(k, j):
                    e = expert(dve, k)
                    dve.wait_ge(y_psum, k + 1)
                    dve.wait_ge(xb_ready, k + 3)
                    nc.vector.scalar_tensor_tensor(out=xb[j][:], in0=yps[j % 2][:, 0:D], scalar=ew["rs"][:, ds(e, 1)],
                                                   in1=xb[j][:], op0=ALU.mult, op1=ALU.add).then_inc(y_ready, 1)

                def body(k, turn, j, ahead):
                    if ahead:
                        add_b1(k + AHEAD, (j + AHEAD) % U, expert(dve, k + AHEAD))
                    if later(k, 1):
                        finish(k - 1, (j - 1) % U)
                    if ahead:
                        apply_norm(k + AHEAD, (j + AHEAD) % U)

                dve.wait_ge(ew["b_loaded"], ew["b_count"])
                nc.vector.tensor_tensor(ew["b2"][:], ew["b2"][:], bc(ew["rs"][:], 2, [P, E8, D]), ALU.mult).then_inc(ew["b2_scaled"], 1)
                dve.wait_ge(ew["b2_scaled"], 1)
                nc.vector.memset(var[:], 0.0).then_inc(xb_ready, 2)
                nc.vector.memset(rstd[:], 0.0).then_inc(y_ready, 2)
                for k in range(AHEAD):
                    add_b1(k, k, expert(dve, k))
                    apply_norm(k, k)
                turns(dve, body)
                finish(MT - 1, (MT - 1) % U)

            @block.gpsimd
            def _(pool):
                def make_rstd(k, j):
                    par = slice(j % 2, j % 2 + 1)
                    pool.wait_ge(ln_stats, k + 1)
                    nc.gpsimd.tensor_tensor(var[:, par], mv[:, j % 2, 1:2], eps_pow[:, 0, 0:1], ALU.add).then_inc(var_done, 1)
                    pool.wait_ge(var_done, k + 1)
                    nc.gpsimd.tensor_tensor(rstd[:, par], var[:, par], eps_pow[:, 1, 0:1], ALU.pow).then_inc(rstd_ready, 1)

                def add_b2(k, turn, j):
                    e = expert(pool, k)
                    pool.wait_ge(x_loaded[j], 16 * (turn + 1))
                    if later(k, U):
                        pool.wait_ge(y_stored[j], 16 * turn)
                    nc.gpsimd.tensor_tensor(xb[j][:], xg[j][:], ew["b2"][:, ds(e, 1), :].rearrange("p o f -> p (o f)"),
                                            ALU.add).then_inc(xb_ready, 1)

                def body(k, turn, j, ahead):
                    if not isinstance(k, int) or k + 1 < MT:
                        add_b2(k + 1, turn + (j + 1) // U, (j + 1) % U)
                    if ahead:
                        make_rstd(k + AHEAD, (j + AHEAD) % U)

                pool.wait_ge(ew["b2_scaled"], 1)
                pool.wait_ge(y_ready, 2)
                pool.wait_ge(xb_ready, 2)
                add_b2(0, 0, 0)
                for k in range(AHEAD):
                    make_rstd(k, k)
                turns(pool, body)


def combine_experts(nc, x_sb, src_sb, eps_pow, w, wsum, slot_i, gathered_out):
    with ExitStack() as ctx:
        kit = Kit(nc, ctx, "co_")
        sb, sem = kit.sb, kit.sem
        n2g = sb("n2g", [P, D])
        yg = sb("yg", [P, TILES, D])
        z = [sb(f"z{i}", [P, CT, D]) for i in range(2)]
        stats, mv = sb("stats", [P, CT, 6]), sb("mv", [P, CT, 2])
        var, rstd, shift = sb("var", [P, CT]), sb("rstd", [P, CT]), sb("shift", [P, CT])
        loaded, z_ready, stats_done, ln_stats = sem("loaded"), sem("z_ready"), sem("stats_done"), sem("ln_stats")
        gathered = [sem(f"gathered{c}") for c in range(CHUNKS)]
        var_done, rstd_ready, zn_ready, zg_ready, x_done = (sem("var_done"), sem("rstd_ready"), sem("zn_ready"),
                                                                      sem("zg_ready"), sem("x_done"))
        shift_ready = sem("shift_ready")
        with nc.Block() as block:
            @block.sync
            def _(sp):
                sp.dma_start(n2g[:], w["n2_g"].partition_broadcast(P)).then_inc(loaded, 16)

            @block.gpsimd
            def _(pool):
                def gather(c):
                    for t in range(CT * c, CT * (c + 1)):
                        pool.indirect_dma_start(out=yg[:, t, :], out_offset=None, in_=gathered_out,
                                                in_offset=bass.IndirectOffsetOnAxis(ap=slot_i[:, t:t + 1], axis=0)
                                                ).then_inc(gathered[c], 16)

                gather(0)
                gather(1)
                for c in range(CHUNKS):
                    pool.wait_ge(ln_stats, CT * (c + 1))
                    nc.gpsimd.tensor_tensor(var[:], mv[:, :, 1], eps_pow[:, 0], ALU.add).then_inc(var_done, 1)
                    pool.wait_ge(var_done, c + 1)
                    if c >= 1:
                        pool.wait_ge(zn_ready, CT * c)
                    nc.gpsimd.tensor_tensor(rstd[:], var[:], eps_pow[:, 1], ALU.pow).then_inc(rstd_ready, 1)
                    if c + 2 < CHUNKS:
                        gather(c + 2)

            @block.scalar
            def _(act):
                for c in range(CHUNKS):
                    act.wait_ge(shift_ready, c + 1)
                    act.wait_ge(rstd_ready, c + 1)
                    act.wait_ge(z_ready, CT * (c + 1))
                    for t in range(CT):
                        nc.scalar.activation(z[c % 2][:, t], z[c % 2][:, t], ACT.Identity, bias=shift[:, t:t + 1],
                                             scale=rstd[:, t:t + 1]).then_inc(zn_ready, 1)

            @block.vector
            def _(dve):
                def moments(c):
                    dve.wait_ge(gathered[c], 16 * CT)
                    if c >= 2:
                        dve.wait_ge(x_done, c - 1)
                    for t in range(CT):
                        nc.vector.scalar_tensor_tensor(out=z[c % 2][:, t], in0=yg[:, CT * c + t],
                                                       scalar=wsum[:, CT * c + t:CT * c + t + 1], in1=src_sb[:, CT * c + t],
                                                       op0=ALU.mult, op1=ALU.add).then_inc(z_ready, 1)
                    for t in range(CT):
                        dve.wait_ge(z_ready, CT * c + t + 1)
                        nc.vector.bn_stats(stats[:, t], z[c % 2][:, t]).then_inc(stats_done, 1)
                    for t in range(CT):
                        dve.wait_ge(stats_done, CT * c + t + 1)
                        nc.vector.bn_aggr(mv[:, t], stats[:, t]).then_inc(ln_stats, 1)

                def finish(c):
                    xs = x_sb[:, CT * c:CT * (c + 1), :]
                    dve.wait_ge(zn_ready, CT * (c + 1))
                    nc.vector.tensor_tensor(z[c % 2][:], z[c % 2][:], bc(n2g[:], 1, [P, CT, D]), ALU.mult).then_inc(zg_ready, 1)
                    dve.wait_ge(zg_ready, c + 1)
                    nc.vector.tensor_tensor(xs, xs, z[c % 2][:], ALU.add).then_inc(x_done, 1)

                dve.wait_ge(loaded, 16)
                moments(0)
                for c in range(CHUNKS):
                    dve.wait_ge(rstd_ready, c + 1)
                    dve.wait_ge(ln_stats, CT * (c + 1))
                    if c >= 1:
                        dve.wait_ge(zn_ready, CT * c)
                    nc.vector.scalar_tensor_tensor(out=shift[:], in0=mv[:, :, 0], scalar=-1.0, in1=rstd[:], op0=ALU.mult,
                                                   op1=ALU.mult).then_inc(shift_ready, 1)
                    if c + 1 < CHUNKS:
                        dve.wait_ge(shift_ready, c + 1)
                        moments(c + 1)
                    finish(c)


def allocate_constants(kit):
    sb = kit.sb
    return dict(ident=sb("ident", [P, P]), eps_pow=sb("eps_pow", [P, 2, CT]), headmask=sb("headmask", [P, HH]),
                trif=sb("trif", [P, P]), tri=sb("tri", [P, P], bf16), ones=sb("ones", [P, P], bf16))


def make_constants(nc, kit, k, load):
    made = kit.sem("constants_made")
    with nc.Block() as block:
        @block.sync
        def _(sp):
            load(sp)

        @block.gpsimd
        def _(pool):
            steps = [0]

            def link(instruction):
                steps[0] += 1
                instruction.then_inc(made, 1)
                pool.wait_ge(made, steps[0])

            link(nc.gpsimd.memset(k["eps_pow"][:, 0], EPS))
            link(nc.gpsimd.memset(k["eps_pow"][:, 1], -0.5))
            link(nc.gpsimd.memset(k["ident"][:], 0.0))
            link(nc.gpsimd.affine_select(out=k["ident"][:], in_=k["ident"][:], compare_op=ALU.not_equal, fill=1.0, base=0,
                                         pattern=[[-1, P]], channel_multiplier=1))
            link(nc.gpsimd.memset(k["headmask"][:], 1.0))
            link(nc.gpsimd.affine_select(out=k["headmask"][:], in_=k["headmask"][:], compare_op=ALU.is_ge, fill=0.0, base=0,
                                         pattern=[[-DK, HH]], channel_multiplier=1))
            link(nc.gpsimd.affine_select(out=k["headmask"][:], in_=k["headmask"][:], compare_op=ALU.is_ge, fill=0.0,
                                         base=DK - 1, pattern=[[DK, HH]], channel_multiplier=-1))
            link(nc.gpsimd.memset(k["trif"][:], 1.0))
            link(nc.gpsimd.affine_select(out=k["trif"][:], in_=k["trif"][:], compare_op=ALU.is_gt, fill=0.0, base=0,
                                         pattern=[[1, P]], channel_multiplier=-1))
            link(nc.gpsimd.tensor_copy(k["tri"][:], k["trif"][:]))
            link(nc.gpsimd.memset(k["ones"][:], 1.0))


def load_inputs(sp, kit, x_sb, x, context):
    first_loaded, rest_loaded = kit.sem("x_first_loaded"), kit.sem("x_rest_loaded")
    tiles = x.rearrange("(t p) d -> p t d", p=P)
    sp.dma_start(x_sb[:, 0:CT], tiles[:, 0:CT]).then_inc(first_loaded, 16)
    if context is not None:
        context.issue(sp)
        context.x_rest_loaded = rest_loaded
    sp.dma_start(x_sb[:, CT:], tiles[:, CT:]).then_inc(rest_loaded, 16)
    sp.wait_ge(first_loaded, 16)
    if context is None:
        sp.wait_ge(rest_loaded, 16)


def self_attention_moe(nc, kit, x_sb, k, w):
    q_parts = nc.dram_tensor("q_parts", (GROUPS, GH, KROWS, S), bf16, kind="Internal").ap()
    k_parts = nc.dram_tensor("k_parts", (GROUPS, GH, KROWS, S), bf16, kind="Internal").ap()
    v_dram = nc.dram_tensor("v_groups", (GROUPS, P, KT, GH * VW), fp32, kind="Internal").ap()
    m_dram = nc.dram_tensor("neg_maxima", (UNITS, MROWS, GH * CT, P), bf16, kind="Internal").ap()
    gathered_in = nc.dram_tensor("expert_in", (MT * P, D), fp32, kind="Internal").ap()
    gathered_out = nc.dram_tensor("expert_out", (MT * P, D), fp32, kind="Internal").ap()
    ident, eps_pow = k["ident"], k["eps_pow"]
    w = dict(w, headmask=k["headmask"])
    with ExitStack() as ctx:
        own = Kit(nc, ctx, "sm_")
        src_sb = own.sb("src", [P, TILES, D])
        self_projections(nc, x_sb, src_sb, ident, eps_pow, w, q_parts, k_parts, v_dram)
        wsum, slot_i = own.sb("wsum", [P, TILES]), own.sb("slot_i", [P, TILES], i32)
        tile_expert = own.sb("tile_expert", [1, MT], i32)
        logits, top = own.sb("logits", [P, TILES, E8]), own.sb("top", [P, TILES, E8])
        topi = own.sb("topi", [P, TILES, E8], u32)
        ew = dict(b1=own.sb("b1", [P, E8, F1]), b2=own.sb("b2", [P, E8, D]), rs=own.sb("rs", [P, E8]),
                  g=own.sb("g", [P, FK, E8]), bt=own.sb("bt", [P, FK, E8]), b_loaded=own.sem("b_loaded"), b2_scaled=own.sem("b2_scaled"))

        def issue(sp, loads, semaphore):
            for dst, source in loads:
                sp.dma_start(dst, source).then_inc(semaphore, 16)
            return 16 * len(loads)

        def load_vectors(sp):
            ew["b_count"] = issue(sp, [(ew["b1"][:].rearrange("p e f -> p (e f)"), w["b1"].partition_broadcast(P)),
                                      (ew["b2"][:].rearrange("p e f -> p (e f)"), w["b2"].partition_broadcast(P)),
                                      (ew["g"][:], w["ln_g"]), (ew["bt"][:], w["ln_b"]), (ew["rs"][:], w["res_scale"].partition_broadcast(P))], ew["b_loaded"])

        with ExitStack() as ctx2:
            attn = Kit(nc, ctx2, "at_").sb("attn", [P, UNITS + 1, CT * GH * DK])
            self_attention(nc, attn, ident, q_parts, k_parts, v_dram, m_dram, x_sb, w["n2_b"])
            attention_out(nc, src_sb, attn, ident, eps_pow, w, logits, top, topi, gathered_in,
                          load_vectors)
        with ExitStack() as ctx2:
            ek = Kit(nc, ctx2, "ew_")
            ew.update(w1=ek.sb("w1", [P, HALVES, E8, F1]), w2=ek.sb("w2", [P, FK, E8, D]), w_loaded=ek.sem("w_loaded"))

            def load_weights(sp):
                loads = [(ew["w1"][:, half], w["w1"][:, half * P:(half + 1) * P, :].rearrange("e p f -> p e f"))
                         for half in range(HALVES)]
                loads += [(ew["w2"][:, f], w["w2"][:, f * P:(f + 1) * P, :].rearrange("e p d -> p e d")) for f in range(FK)]
                ew["w_count"] = issue(sp, loads, ew["w_loaded"])

            route_tokens(nc, w, src_sb, logits, top, topi, k["tri"], k["ones"], wsum, slot_i, tile_expert, gathered_in,
                         load_weights)
            expert_tiles(nc, ident, eps_pow, w, ew, (logits, top), tile_expert, gathered_in, gathered_out)
        combine_experts(nc, x_sb, src_sb, eps_pow, w, wsum, slot_i, gathered_out)

CAP = TOKENS // E8
CAPT = CAP // P
NV = 5


def token_scores(nc, x_sb, ident, eps_pow, w, sc, xn_dram, out):
    with ExitStack() as ctx:
        kit = Kit(nc, ctx, "ts_")
        sb, ps, sem = kit.sb, kit.ps, kit.sem
        turnstile = sem("turnstile")
        wg = sb("wg", [P, HALVES, E8])
        stats, mv = [sb(f"stats{i}", [P, CT, 6]) for i in range(2)], [sb(f"mv{i}", [P, CT, 2]) for i in range(2)]
        var, rstd = sb("var", [P, 2, CT]), sb("rstd", [P, 2, CT])
        xn = [sb(f"xn{i}", [P, CT, D]) for i in range(2)]
        xnT = [sb(f"xnT{i}", [P, HALVES, CW]) for i in range(2)]
        tps = [ps(f"tps{i}", [P, HALVES, CW]) for i in range(2)]
        sT = [sb(f"sT{i}", [E8, CW]) for i in range(2)]
        sTps = [ps(f"sTps{i}", [P, CW]) for i in range(2)]
        sps = [ps(f"sps{i}", [P, CW]) for i in range(2)]
        loaded, x_stored = sem("loaded"), sem("x_stored")
        xn_stored = [sem(f"xn_stored{i}") for i in range(2)]
        stats_done, ln_stats, var_done, rstd_ready = sem("stats_done"), sem("ln_stats"), sem("var_done"), sem("rstd_ready")
        xn_ready, xnT_psum, xnT_ready, s_psum, s_ready = (sem("xn_ready"), sem("xnT_psum"), sem("xnT_ready"), sem("s_psum"),
                                                          sem("s_ready"))
        sT_psum, sT_ready = sem("sT_psum"), sem("sT_ready")

        def turns(eng, body):
            for c in range(2):
                body(0, c, c, True)
            with eng.Fori(1, CHUNKS // 2 - 1) as i:
                for par in range(2):
                    body(i, par, 2 * i + par, True)
            for par in range(2):
                body(CHUNKS // 2 - 1, par, CHUNKS - 2 + par, par == 0)

        with nc.Block() as block:
            @block.sync
            def _(sp):
                sp.dma_start(wg[:], w["Wg"].rearrange("(k p) e -> p k e", p=P)).then_inc(loaded, 16)
                sp.dma_start(out.rearrange("(t p) d -> p t d", p=P), x_sb[:]).then_inc(x_stored, 16)
                xv = xn_dram.rearrange("(t p) d -> p t d", p=P)

                def body(i, par, c, more):
                    sp.wait_ge(xn_ready, CT * (c + 1))
                    sp.dma_start(xv[:, ds(CT * c, CT), :], xn[par][:]).then_inc(xn_stored[par], 16)

                turns(sp, body)
                sp.wait_ge(x_stored, 16)
                for par in range(2):
                    sp.wait_ge(xn_stored[par], 16 * (CHUNKS // 2))

            @block.vector
            def _(dve):
                def moments(c, par):
                    if later(c, 2):
                        dve.wait_ge(xn_ready, CT * (c - 1))
                    for t in range(CT):
                        nc.vector.bn_stats(stats[par][:, t], x_sb[:, ds(CT * c + t, 1), :]).then_inc(stats_done, 1)
                    passed(dve, stats_done, CT * (c + 1), turnstile)
                    for t in range(CT):
                        nc.vector.bn_aggr(mv[par][:, t], stats[par][:, t]).then_inc(ln_stats, 1)

                def body(i, par, c, more):
                    if more:
                        moments(c + 1, 1 - par)
                    dve.wait_ge(rstd_ready, c + 1)
                    dve.wait_ge(ln_stats, CT * (c + 1))
                    if later(c, 2):
                        dve.wait_ge(xn_stored[par], 16 * i)
                        dve.wait_ge(xnT_psum, c - 1)
                    for t in range(CT):
                        nc.vector.tensor_scalar(xn[par][:, t], x_sb[:, ds(CT * c + t, 1), :], mv[par][:, t, 0:1],
                                                rstd[:, par, t:t + 1], ALU.subtract, ALU.mult).then_inc(xn_ready, 1)

                moments(0, 0)
                turns(dve, body)

            @block.gpsimd
            def _(pool):
                def body(i, par, c, more):
                    pool.wait_ge(ln_stats, CT * (c + 1))
                    nc.gpsimd.tensor_tensor(var[:, par], mv[par][:, :, 1], eps_pow[:, 0], ALU.add).then_inc(var_done, 1)
                    pool.wait_ge(var_done, c + 1)
                    nc.gpsimd.tensor_tensor(rstd[:, par], var[:, par], eps_pow[:, 1], ALU.pow).then_inc(rstd_ready, 1)

                turns(pool, body)

            @block.scalar
            def _(act):
                def evacuate_scores(c, par):
                    act.wait_ge(sT_psum, c + 1)
                    nc.scalar.activation(sT[par][:], sTps[par][0:E8], ACT.Copy).then_inc(sT_ready, 1)
                    act.wait_ge(s_psum, c + 1)
                    nc.scalar.activation(sc[:, ds(CT * c, CT), :], sps[par][:, 0:CT * E8].rearrange("p (t e) -> p t e", t=CT),
                                         ACT.Copy).then_inc(s_ready, 1)

                def body(i, par, c, more):
                    act.wait_ge(xnT_psum, c + 1)
                    nc.scalar.activation(xnT[par][:], tps[par][:], ACT.Copy).then_inc(xnT_ready, 1)
                    if later(c, 1):
                        evacuate_scores(c - 1, 1 - par)

                turns(act, body)
                evacuate_scores(CHUNKS - 1, (CHUNKS - 1) % 2)

            @block.tensor
            def _(pe):
                def scores(c, par):
                    pe.wait_ge(xnT_ready, c + 1)
                    for k in range(HALVES):
                        last = nc.tensor.matmul(sTps[par][0:E8], wg[:, k], xnT[par][:, k], start=(k == 0), stop=(k == HALVES - 1))
                    last.then_inc(sT_psum, 1)
                    if later(c, 1):
                        pe.wait_ge(s_ready, c)
                    passed(pe, sT_ready, c + 1, turnstile)
                    for t in range(CT):
                        last = nc.tensor.transpose(sps[par][:, t * E8:(t + 1) * E8], sT[par][:, t * P:(t + 1) * P],
                                                   ident[0:E8, 0:E8])
                    last.then_inc(s_psum, 1)

                def body(i, par, c, more):
                    pe.wait_ge(xn_ready, CT * (c + 1))
                    for t in range(CT):
                        for half in range(HALVES):
                            last = nc.tensor.transpose(tps[par][:, half, t * P:(t + 1) * P],
                                                       xn[par][:, t, half * P:(half + 1) * P], ident[:])
                    last.then_inc(xnT_psum, 1)
                    if later(c, 1):
                        scores(c - 1, 1 - par)

                pe.wait_ge(loaded, 16)
                turns(pe, body)
                scores(CHUNKS - 1, (CHUNKS - 1) % 2)


def choose_tokens(nc, k, sc, idx, wt, load_experts):
    STEPS, TRIED = 15, 3
    with ExitStack() as ctx:
        kit = Kit(nc, ctx, "ct_")
        sb, sem = kit.sb, kit.sem
        turnstile = sem("turnstile")
        pf = make_prefix(nc, kit, k["tri"], k["ones"])
        cps, ips, zps = kit.ps("cps", [P, TRIED, E8]), kit.ps("ips", [P, E8, CAPT, NV]), kit.ps("zps", [P, E8])
        ge = sb("ge", [P, TRIED, TILES, E8], bf16)
        met_rows = sb("met_rows", [P, TRIED, E8], bf16)
        enough = sb("enough", [P, TRIED, E8])
        digit = sb("digit", [P, E8], i32)
        try_key = sb("try_key", [P, TRIED, E8], i32)
        met, key, flip, thr = (sb(n, [P, E8], i32) for n in ("met", "key", "flip", "thr"))
        digits, shift, tries = (sb(n, [P, STEPS, TRIED], i32) for n in ("digits", "shift", "tries"))
        gt, eq = sb("gt", [P, TILES, E8]), sb("eq", [P, TILES, E8])
        sel, selb = sb("sel", [P, TILES, E8]), sb("selb", [P, TILES, E8], bf16)
        need, rank = sb("need", [P, E8]), sb("rank", [P, TILES, E8])
        rowmax, best = sb("rowmax", [P, E8]), sb("best", [P, E8])
        ex, rowsum, rz = sb("ex", [P, TILES, E8]), sb("rowsum", [P, E8]), sb("rz", [P, E8])
        onesf = sb("onesf", [P, P])
        slot_i, low_i, high_i = (sb(n, [P, TILES, E8], i32) for n in ("slot_i", "low_i", "high_i"))
        low, high = sb("low", [P, TILES, E8]), sb("high", [P, TILES, E8])
        iota4 = sb("iota4", [P, CAPT])
        iota128f, iota128 = sb("iota128f", [P, P]), sb("iota128", [P, P], bf16)
        val = sb("val", [P, TILES, E8, NV])
        part = sb("part", [P, TILES, E8], bf16)
        rest = sb("rest", [P, TILES, E8])
        hot4 = sb("high_hot", [P, TILES, E8, CAPT])
        rhs = sb("rhs", [P, TILES, E8, CAPT, NV], bf16)
        GT = 8
        hot = [sb(f"hot{i}", [P, GT, P], bf16) for i in range(6)]
        got = sb("got", [P, E8, CAPT, NV])
        idf = sb("idf", [P, E8, CAPT])
        step, made, ge_ready, c_psum = sem("step"), sem("made"), sem("ge_ready"), sem("c_psum")
        rows_counted = sem("rows_counted")
        rowmax_ready, best_ready, centered, exp_ready, rowsum_ready, z_psum = (
            sem("rowmax_ready"), sem("best_ready"), sem("centered"), sem("exp_ready"), sem("rowsum_ready"), sem("z_psum"))
        eqb_ready, selb_ready, products = sem("eqb_ready"), sem("selb_ready"), sem("products")
        rhs_ready, hot_used, low_ready = sem("rhs_ready"), sem("hot_used"), sem("low_ready")
        hot_dve, hot_pool = sem("hot_dve"), sem("hot_pool")
        view = lambda b: b[:].rearrange("p t e -> p (t e)")
        per_expert = lambda b: bc(b[:], 1, [P, TILES, E8])
        SIGN, SIGN2, MADE, UNROLL = -2 ** 31, 2 ** 30, 7, 3

        def hot_of(group):
            return hot[3 + group // 4 % 3] if group % 4 == 3 else hot[group % 4]

        def build_hot(eng, unit, groups, back, ready):
            for group in groups:
                if group >= back:
                    eng.wait_ge(hot_used, group - back + 1)
                for i in range(GT):
                    e, t = group * GT // TILES, group * GT % TILES + i
                    unit.tensor_scalar(hot_of(group)[:, i], iota128[:], low[:, t, e:e + 1], None,
                                       ALU.is_equal).then_inc(ready, 1)

        with nc.Block() as block:
            @block.sync
            def _(sp):
                load_experts(sp)

            @block.gpsimd
            def _(pool):
                n = [0]

                def link(instruction):
                    n[0] += 1
                    instruction.then_inc(made, 1)
                    pool.wait_ge(made, n[0])

                link(nc.gpsimd.iota(digits[:], [[0, STEPS], [1, TRIED]], base=1, channel_multiplier=0))
                link(nc.gpsimd.iota(shift[:], [[-2, STEPS], [0, TRIED]], base=2 * (STEPS - 1), channel_multiplier=0))
                link(nc.gpsimd.iota(iota128f[:], [[1, P]], base=0, channel_multiplier=0, allow_small_or_imprecise_dtypes=True))
                link(nc.gpsimd.iota(iota4[:], [[1, CAPT]], base=0, channel_multiplier=0, allow_small_or_imprecise_dtypes=True))
                link(nc.gpsimd.iota(val[:, :, :, 0], [[1, TILES], [0, E8]], base=0, channel_multiplier=0,
                                    allow_small_or_imprecise_dtypes=True))
                link(nc.gpsimd.iota(val[:, :, :, 1], [[0, TILES], [0, E8]], base=0, channel_multiplier=1,
                                    allow_small_or_imprecise_dtypes=True))
                link(nc.gpsimd.memset(onesf[:], 1.0))
                pool.wait_ge(rowmax_ready, 1)
                nc.gpsimd.partition_all_reduce(best[:], rowmax[:], P, bass.bass_isa.ReduceOp.max).then_inc(best_ready, 1)
                pool.wait_ge(low_ready, 1)
                build_hot(pool, nc.gpsimd, range(3, E8 * TILES // GT, 4), 12, hot_pool)

            @block.scalar
            def _(act):
                act.wait_ge(centered, 1)
                nc.scalar.activation(ex[:], ex[:], ACT.Exp).then_inc(exp_ready, 1)

            @block.tensor
            def _(pe):
                def count(value, tried):
                    pe.wait_ge(rows_counted, value)
                    nc.tensor.matmul(cps[:, 0:tried], k["ones"][:], met_rows[:, 0:tried], start=True, stop=True
                                     ).then_inc(c_psum, 1)

                count(1, 1)
                count(2, 1)
                with pe.Fori(0, STEPS // UNROLL) as turn:
                    for j in range(UNROLL):
                        count(turn * UNROLL + j + 3, TRIED)
                count(STEPS + 3, 1)
                pe.wait_ge(eqb_ready, 1)
                prefix_products(nc, pe, pf, selb, products)
                pe.wait_ge(selb_ready, 1)
                prefix_products(nc, pe, pf, selb, products)
                pe.wait_ge(rowsum_ready, 1)
                nc.tensor.matmul(zps[:], onesf[:], rowsum[:], start=True, stop=True).then_inc(z_psum, 1)
                pe.wait_ge(rhs_ready, 2)
                for e in range(E8):
                    for t in range(TILES):
                        n = e * TILES + t
                        if t % GT == 0:
                            group = n // GT
                            if group % 4 == 3:
                                pe.wait_ge(hot_pool, GT * (group // 4 + 1))
                            else:
                                pe.wait_ge(hot_dve, GT * (3 * (group // 4) + group % 4 + 1))
                        last = nc.tensor.matmul(ips[:, e].rearrange("p a v -> p (a v)"), hot_of(group)[:, t % GT],
                                                rhs[:, t, e].rearrange("p a v -> p (a v)"), start=(t == 0),
                                                stop=(t == TILES - 1))
                        if t % GT == GT - 1:
                            last.then_inc(hot_used, 1)

            @block.vector
            def _(dve):
                n = [0]

                def link(instruction):
                    n[0] += 1
                    instruction.then_inc(step, 1)
                    dve.wait_ge(step, n[0])

                def note(instruction):
                    n[0] += 1
                    instruction.then_inc(step, 1)

                def count(nth, tried):
                    dve.wait_ge(ge_ready, nth)
                    with nc.allow_low_precision(reason="whole numbers up to the number of tiles"):
                        nc.vector.tensor_reduce(met_rows[:, 0:tried], ge[:, 0:tried].rearrange("p j t e -> p j e t"), axis=X,
                                                op=ALU.add).then_inc(rows_counted, 1)
                    dve.wait_ge(c_psum, nth)

                nc.vector.tensor_reduce(rowmax[:], sc[:].rearrange("p t e -> p e t"), axis=X, op=ALU.max).then_inc(rowmax_ready, 1)
                nc.vector.tensor_scalar(ge[:, 0], sc[:], 0.0, None, ALU.is_ge).then_inc(ge_ready, 1)
                dve.wait_ge(made, MADE)
                note(nc.vector.tensor_tensor(tries[:], digits[:], shift[:], ALU.logical_shift_left))
                note(nc.vector.tensor_copy(iota128[:], iota128f[:]))
                link(nc.vector.memset(pf["one"][:], 1.0))
                count(1, 1)
                link(nc.vector.tensor_scalar(met[:], cps[:, 0], float(CAP), -1.0, ALU.is_ge, ALU.mult))
                link(nc.vector.tensor_scalar(key[:], met[:], SIGN, None, ALU.bitwise_and))
                link(nc.vector.tensor_scalar(flip[:], met[:], -1, SIGN, ALU.bitwise_xor, ALU.bitwise_or))
                link(nc.vector.tensor_scalar(try_key[:, 0], key[:], SIGN2, None, ALU.bitwise_or))
                link(nc.vector.tensor_tensor(thr[:], try_key[:, 0], flip[:], ALU.bitwise_xor))
                nc.vector.tensor_tensor(ge[:, 0], sc[:], per_expert(thr[:].bitcast(fp32)), ALU.is_ge).then_inc(ge_ready, 1)
                count(2, 1)
                link(nc.vector.tensor_scalar(met[:], cps[:, 0], float(CAP), -1.0, ALU.is_ge, ALU.mult))
                link(nc.vector.tensor_scalar(met[:], met[:], SIGN2, None, ALU.bitwise_and))
                link(nc.vector.tensor_tensor(key[:], key[:], met[:], ALU.bitwise_or))
                link(nc.vector.tensor_tensor(key[:], key[:], flip[:], ALU.bitwise_xor))
                base = n[0]
                LINKS = 4
                def next_digit(i):
                    at = base + LINKS * i
                    nc.vector.tensor_tensor(try_key[:], bc(key[:], 1, [P, TRIED, E8]),
                                            tries[:, ds(i, 1)].rearrange("p o j -> p (o j)").unsqueeze(2).broadcast_to(
                                                [P, TRIED, E8]), ALU.bitwise_xor).then_inc(step, 1)
                    dve.wait_ge(step, at + 1)
                    nc.vector.tensor_tensor(ge[:], bc(sc[:], 1, [P, TRIED, TILES, E8]),
                                            bc(try_key[:].bitcast(fp32), 2, [P, TRIED, TILES, E8]), ALU.is_ge).then_inc(ge_ready, 1)
                    count(i + 3, TRIED)
                    nc.vector.tensor_scalar(enough[:], cps[:], float(CAP), None, ALU.is_ge).then_inc(step, 1)
                    dve.wait_ge(step, at + 2)
                    with nc.allow_low_precision(reason="at most 3, as an integer"):
                        nc.vector.tensor_reduce(digit[:], enough[:].rearrange("p j e -> p e j"), axis=X,
                                                op=ALU.add).then_inc(step, 1)
                    dve.wait_ge(step, at + 3)
                    nc.vector.scalar_tensor_tensor(out=key[:], in0=digit[:], scalar=shift[:, ds(i, 1), 0], in1=key[:],
                                                   op0=ALU.logical_shift_left, op1=ALU.bitwise_xor).then_inc(step, 1)
                    dve.wait_ge(step, at + 4)

                with dve.Fori(0, STEPS // UNROLL) as turn:
                    for j in range(UNROLL):
                        next_digit(turn * UNROLL + j)
                n[0] = base + LINKS * STEPS
                thrf = per_expert(key[:].bitcast(fp32))
                nc.vector.tensor_tensor(ge[:, 0], sc[:], thrf, ALU.is_gt).then_inc(ge_ready, 1)
                note(nc.vector.tensor_tensor(gt[:], sc[:], thrf, ALU.is_gt))
                link(nc.vector.tensor_tensor(eq[:], sc[:], thrf, ALU.is_equal))
                nc.vector.tensor_copy(selb[:], eq[:]).then_inc(eqb_ready, 1)
                count(STEPS + 3, 1)
                link(nc.vector.tensor_scalar(need[:], cps[:, 0], -1.0, float(CAP), ALU.mult, ALU.add))

                def ranks(done):
                    dve.wait_ge(products, done)
                    link(nc.vector.tensor_copy(view(pf["tot_sb"]), pf["tot"][:]))
                    for e in range(E8):
                        (link if e == E8 - 1 else note)(nc.vector.tensor_tensor_scan(pf["incl"][:, :, e], pf["one"][:], pf["tot_sb"][:, :, e], 0.0,
                                                          ALU.mult, ALU.add))
                    link(nc.vector.tensor_tensor(rank[:], pf["pre"][:].rearrange("p (t e) -> p t e", e=E8), pf["incl"][:],
                                                 ALU.add))
                    link(nc.vector.tensor_tensor(rank[:], rank[:], pf["tot_sb"][:], ALU.subtract))

                ranks(1)
                link(nc.vector.tensor_tensor(rank[:], rank[:], per_expert(need), ALU.is_lt))
                link(nc.vector.tensor_tensor(rank[:], rank[:], eq[:], ALU.mult))
                link(nc.vector.tensor_tensor(sel[:], rank[:], gt[:], ALU.add))
                nc.vector.tensor_copy(selb[:], sel[:]).then_inc(selb_ready, 1)
                dve.wait_ge(best_ready, 1)
                nc.vector.tensor_tensor(ex[:], sc[:], per_expert(best), ALU.subtract).then_inc(centered, 1)
                ranks(2)
                dve.wait_ge(exp_ready, 1)
                link(nc.vector.tensor_tensor(ex[:], ex[:], sel[:], ALU.mult))
                nc.vector.tensor_reduce(rowsum[:], ex[:].rearrange("p t e -> p e t"), axis=X, op=ALU.add).then_inc(rowsum_ready, 1)
                link(nc.vector.tensor_copy(slot_i[:], rank[:]))
                note(nc.vector.tensor_scalar(low_i[:], slot_i[:], P - 1, None, ALU.bitwise_and))
                link(nc.vector.tensor_scalar(high_i[:], slot_i[:], 7, None, ALU.arith_shift_right))
                note(nc.vector.tensor_copy(high[:], high_i[:]))
                link(nc.vector.tensor_scalar(low[:], low_i[:], 1.0, None, ALU.add))
                link(nc.vector.tensor_tensor(low[:], low[:], sel[:], ALU.mult))
                nc.vector.tensor_scalar(low[:], low[:], 1.0, None, ALU.subtract).then_inc(low_ready, 1)
                dve.wait_ge(low_ready, 1)
                dve.wait_ge(z_psum, 1)
                link(nc.vector.reciprocal(rz[:], zps[:]))
                link(nc.vector.tensor_tensor(rest[:], ex[:], per_expert(rz), ALU.mult))
                for i in range(3):
                    link(nc.vector.tensor_copy(part[:], rest[:]))
                    note(nc.vector.tensor_copy(val[:, :, :, 2 + i], part[:]))
                    link(nc.vector.tensor_tensor(rest[:], rest[:], part[:], ALU.subtract))
                link(nc.vector.tensor_tensor(hot4[:], bc(high[:], 3, [P, TILES, E8, CAPT]),
                                             iota4[:].unsqueeze(1).unsqueeze(1).broadcast_to([P, TILES, E8, CAPT]), ALU.is_equal))
                h4 = hot4[:].rearrange("p t e a -> p (t e) a")
                v5 = val[:].rearrange("p t e v -> p (t e) v")
                r5 = rhs[:].rearrange("p t e a v -> p (t e) a v")
                TE = TILES * E8
                for part_of in range(2):
                    rows = slice(part_of * TE // 2, (part_of + 1) * TE // 2)
                    nc.vector.tensor_tensor(r5[:, rows], bc(h4[:, rows], 3, [P, TE // 2, CAPT, NV]),
                                            bc(v5[:, rows], 2, [P, TE // 2, CAPT, NV]), ALU.mult).then_inc(rhs_ready, 1)
                build_hot(dve, nc.vector, [g for g in range(E8 * TILES // GT) if g % 4 != 3], 4, hot_dve)
                dve.wait_ge(hot_used, E8 * TILES // GT)
                link(nc.vector.tensor_copy(got[:], ips[:]))
                link(nc.vector.scalar_tensor_tensor(out=idf[:], in0=got[:, :, :, 0], scalar=float(P), in1=got[:, :, :, 1],
                                                    op0=ALU.mult, op1=ALU.add))
                link(nc.vector.tensor_copy(idx[:], idf[:]))
                link(nc.vector.tensor_tensor(wt[:], got[:, :, :, 2], got[:, :, :, 3], ALU.add))
                link(nc.vector.tensor_tensor(wt[:], wt[:], got[:, :, :, 4], ALU.add))


def swiglu_experts(nc, ident, weights, load, w_loaded, idx, wt, xn_dram, out):
    with ExitStack() as ctx:
        kit = Kit(nc, ctx, "sw_")
        sb, ps, sem = kit.sb, kit.ps, kit.sem
        turnstile = sem("turnstile")
        w1, w3, w2 = weights
        ids = [sb(f"ids{i}", [P, CAPT], i32) for i in range(2)]
        xg = [sb(f"xg{i}", [P, CAPT, D]) for i in range(2)]
        xT = sb("xT", [P, HALVES, CAP])
        act1 = [sb(f"act1{i}", [P, CAP]) for i in range(2)]
        hT = sb("hT", [P, FK, CAP])
        yo = [sb(f"yo{i}", [P, CAPT, D]) for i in range(2)]
        tps, yps = ps("tps", [P, HALVES, CAP]), ps("yps", [P, 2, CAP])
        p1 = [ps(f"p1{i}", [P, CAP]) for i in range(2)]
        p3 = [ps(f"p3{i}", [P, CAP]) for i in range(2)]
        gathered = [sem(f"gathered{i}") for i in range(2)]
        ids_ready, scattered = sem("ids_ready"), sem("scattered")
        xT_psum, xT_ready, h_psum, silu_ready, h_ready = (sem("xT_psum"), sem("xT_ready"), sem("h_psum"), sem("silu_ready"),
                                                          sem("h_ready"))
        y_psum, y_ready = sem("y_psum"), sem("y_ready")

        def experts(eng, body):
            with eng.Fori(0, E8 // 2 - 1) as i:
                for par in range(2):
                    body(2 * i + par, i, par, False)
            for par in range(2):
                body(E8 - 2 + par, E8 // 2 - 1, par, par == 1)

        with nc.Block() as block:
            @block.sync
            def _(sp):
                def body(e, turn, par, last):
                    if not isinstance(e, int):
                        sp.wait_ge(y_psum, 2 * e + 2)
                        load(sp, e + 2, par)

                experts(sp, body)

            @block.gpsimd
            def _(pool):
                def gather(e, turn, par):
                    if later(e, 1):
                        pool.wait_ge(xT_psum, e - 1)
                        pool.wait_ge(scattered, 16 * CAPT * (e - 1))
                    nc.gpsimd.tensor_copy(ids[par][:], idx[:, ds(e, 1), :].rearrange("p o a -> p (o a)")).then_inc(ids_ready, 1)
                    passed(pool, ids_ready, e + 1, turnstile)
                    for a in range(CAPT):
                        pool.indirect_dma_start(out=xg[par][:, a, :], out_offset=None, in_=xn_dram,
                                                in_offset=bass.IndirectOffsetOnAxis(ap=ids[par][:, a:a + 1], axis=0)
                                                ).then_inc(gathered[par], 16)

                def body(e, turn, par, last):
                    if not last:
                        gather(e + 1, turn + (par + 1) // 2, (par + 1) % 2)
                    pool.wait_ge(y_ready, CAPT * (e + 1))
                    pool.wait_ge(scattered, 16 * CAPT * e)
                    passed(pool, y_ready, 1, turnstile)
                    for a in range(CAPT):
                        pool.indirect_dma_start(out=out, out_offset=bass.IndirectOffsetOnAxis(ap=ids[par][:, a:a + 1], axis=0),
                                                in_=yo[par][:, a, :], in_offset=None, compute_op=ALU.add).then_inc(scattered, 16)

                gather(0, 0, 0)
                experts(pool, body)
                pool.wait_ge(scattered, 16 * CAPT * E8)

            @block.tensor
            def _(pe):
                def transpose_x(e, turn, par):
                    pe.wait_ge(gathered[par], 16 * CAPT * (turn + 1))
                    for a in range(CAPT):
                        for half in range(HALVES):
                            last = nc.tensor.transpose(tps[:, half, a * P:(a + 1) * P], xg[par][:, a, half * P:(half + 1) * P],
                                                       ident[:])
                    last.then_inc(xT_psum, 1)

                def body(e, turn, par, final):
                    pe.wait_ge(w_loaded[par], 48 * (turn + 1))
                    pe.wait_ge(xT_ready, e + 1)
                    for f in range(FK):
                        pe.wait_ge(h_ready, FK * e + f + 1)
                        for wt_, bank in ((w1, p1), (w3, p3)):
                            for half in range(HALVES):
                                last = nc.tensor.matmul(bank[f % 2][:], wt_[par][:, half, f * P:(f + 1) * P], xT[:, half],
                                                        start=(half == 0), stop=(half == HALVES - 1))
                            last.then_inc(h_psum, 1)
                    if not final:
                        transpose_x(e + 1, turn + (par + 1) // 2, (par + 1) % 2)
                    pe.wait_ge(h_ready, FK * (e + 1) + 2)
                    pe.wait_ge(y_ready, CAPT * e)
                    for bank in range(2):
                        for a in (2 * bank, 2 * bank + 1):
                            for f in range(FK):
                                last = nc.tensor.matmul(yps[:, bank, (a % 2) * D:(a % 2 + 1) * D], hT[:, f, a * P:(a + 1) * P],
                                                        w2[par][:, f], start=(f == 0), stop=(f == FK - 1))
                        last.then_inc(y_psum, 1)

                transpose_x(0, 0, 0)
                experts(pe, body)

            @block.scalar
            def _(act):
                def evacuate_xT(e):
                    act.wait_ge(xT_psum, e + 1)
                    act.wait_ge(h_psum, 2 * FK * e)
                    nc.scalar.activation(xT[:], tps[:], ACT.Copy).then_inc(xT_ready, 1)

                def body(e, turn, par, last):
                    for f in range(FK):
                        act.wait_ge(h_psum, 2 * (FK * e + f) + 1)
                        act.wait_ge(h_ready, FK * e + f + 1)
                        nc.scalar.activation(act1[f % 2][:], p1[f % 2][:], ACT.Silu).then_inc(silu_ready, 1)
                    if not last:
                        evacuate_xT(e + 1)

                evacuate_xT(0)
                experts(act, body)

            @block.vector
            def _(dve):
                def body(e, turn, par, last):
                    dve.wait_ge(y_psum, 2 * e)
                    for f in range(FK):
                        dve.wait_ge(silu_ready, FK * e + f + 1)
                        dve.wait_ge(h_psum, 2 * (FK * e + f) + 2)
                        nc.vector.tensor_tensor(hT[:, f], p3[f % 2][:], act1[f % 2][:], ALU.mult).then_inc(h_ready, 1)
                    for a in range(CAPT):
                        dve.wait_ge(y_psum, 2 * e + a // 2 + 1)
                        nc.vector.tensor_scalar(yo[par][:, a], yps[:, a // 2, (a % 2) * D:(a % 2 + 1) * D],
                                                wt[:, ds(e, 1), a], None, ALU.mult).then_inc(y_ready, 1)

                nc.vector.memset(yo[0][:], 0.0).then_inc(h_ready, 2)
                experts(dve, body)


def token_choice_moe(nc, x_sb, k, w, out):
    xn_dram = nc.dram_tensor("normalized", (TOKENS, D), fp32, kind="Internal").ap()
    with ExitStack() as ctx:
        own = Kit(nc, ctx, "tc_")
        sc = own.sb("sc", [P, TILES, E8])
        idx, wt = own.sb("idx", [P, E8, CAPT], i32), own.sb("wt", [P, E8, CAPT])
        w1 = [own.sb(f"w1{i}", [P, HALVES, F1]) for i in range(2)]
        w3 = [own.sb(f"w3{i}", [P, HALVES, F1]) for i in range(2)]
        w2 = [own.sb(f"w2{i}", [P, FK, D]) for i in range(2)]
        w_loaded = [own.sem(f"w_loaded{i}") for i in range(2)]

        def load(sp, e, par):
            for dst, name in ((w1, "W1"), (w3, "W3"), (w2, "W2")):
                sp.dma_start(dst[par][:], w[name][ds(e, 1)].rearrange("e (k p) n -> p (e k) n", p=P)).then_inc(w_loaded[par], 16)

        def load_experts(sp):
            load(sp, 0, 0)
            load(sp, 1, 1)

        token_scores(nc, x_sb, k["ident"], k["eps_pow"], w, sc, xn_dram, out)
        choose_tokens(nc, k, sc, idx, wt, load_experts)
        swiglu_experts(nc, k["ident"], (w1, w3, w2), load, w_loaded, idx, wt, xn_dram, out)


def decoder(nc, a, out):
    with ExitStack() as ctx:
        kit = Kit(nc, ctx, "x_")
        x_sb = kit.sb("x", [P, TILES, D])
        of = lambda layer: {name[len(layer):]: ap for name, ap in a.items() if name.startswith(layer)}
        k = allocate_constants(kit)
        context = lambda layer, ctx: Context(Kit(nc, ctx, f"c{layer}_"), dict(of(f"L{layer}_xattn_"), ctxT=a["ctxT"]))
        with ExitStack() as ctx2:
            first = context(0, ctx2)
            make_constants(nc, kit, k, lambda sp: load_inputs(sp, kit, x_sb, a["x"], first))
            cross_attention(nc, x_sb, k["ident"], k["eps_pow"], k["headmask"], first, a["mask"], "xa0")
        self_attention_moe(nc, kit, x_sb, k, of("L0_ffn_"))
        with ExitStack() as ctx2:
            cross_attention(nc, x_sb, k["ident"], k["eps_pow"], k["headmask"], context(1, ctx2), None, "xa1")
        token_choice_moe(nc, x_sb, k, of("L1_ffn_"), out)



def kernel(**inputs):
    import numpy as np
    import concourse.bacc as bacc
    from concourse.bass_utils import run_bass_kernel_spmd

    def take(name):
        return np.asarray(inputs[name])

    def columns(v):
        return v.reshape(2, 128).T

    arrays = {"x": take("x").reshape(4096, 256), "ctxT": take("ctx_1024").transpose(2, 0, 1),
              "mask": take("mask_Bx1xSxS2_ik0").reshape(4096, 64)}
    for layer, transposed in (("L0_xattn_", True), ("L1_xattn_", False)):
        weights = [take(layer + "W" + n) for n in "qkvo"]
        arrays[layer + "wts"] = np.stack([m.T if transposed else m for m in weights])
        arrays[layer + "bqk"] = np.stack([columns(take(layer + "b" + n)) for n in "qk"], 1)
        arrays[layer + "bv"], arrays[layer + "bo"] = take(layer + "bv"), take(layer + "bo")
    f = "L0_ffn_"
    arrays[f + "ffn_qkv"] = np.stack([take(f + n + "_w") for n in "qkv"])
    for n in ("scale_w", "gate_b"):
        arrays[f + n] = columns(take(f + n))
    for n in ("gate_w", "out_w", "n1_g", "n1_b", "n2_g", "n2_b", "moe_gate_w", "moe_gate_b", "w1", "w2", "res_scale"):
        arrays[f + n] = take(f + n)
    for n in ("b1", "b2"):
        arrays[f + n] = take(f + n).reshape(-1)
    for n in ("ln_g", "ln_b"):
        arrays[f + n] = take(f + n).reshape(8, 4, 128).transpose(2, 1, 0)
    f = "L1_ffn_"
    arrays[f + "Wg"] = take(f + "Wg").T
    for n in ("W1", "W2", "W3"):
        arrays[f + n] = take(f + n).transpose(0, 2, 1)

    nc = bacc.Bacc("TRN2", target_bir_lowering=False, num_devices=1)
    feeds, aps = {}, {}
    for name, array in arrays.items():
        array = np.ascontiguousarray(array)
        feeds["in_" + name] = array
        aps[name] = nc.dram_tensor("in_" + name, array.shape, mybir.dt.from_np(array.dtype), kind="ExternalInput").ap()
    out = nc.dram_tensor("out_x", (4096, 256), fp32, kind="ExternalOutput").ap()
    decoder(nc, aps, out)
    result = run_bass_kernel_spmd(nc, [feeds], core_ids=[0])
    return result.results[0]["out_x"].reshape(4, 1024, 256)
```
